# Optimizing a Trainium2 kernel written in Bass

```python
import numpy as np
import jax
import jax.numpy as jnp

def _softmax(x, axis=-1):
    return jax.nn.softmax(x, axis=axis)

def _gelu(x):
    return jax.nn.gelu(x, approximate=True)

def _silu(x):
    return jax.nn.silu(x)

def _sigmoid(x):
    return jax.nn.sigmoid(x)

def _layernorm(x, axis=-1, eps=1e-05):
    m = jnp.mean(x, axis=axis, keepdims=True)
    v = jnp.var(x, axis=axis, keepdims=True)
    return (x - m) / jnp.sqrt(v + eps)

def _scatter_add(tgt, idx, src, axis=0):
    return tgt.at[idx].add(src)

def _segment_sum(src, seg, n):
    return jax.ops.segment_sum(src, seg, n)
kernel_name = 'mk_vit_tower_cls_d2_tok_img512_r4_365918'

def setup_inputs(seed: int=0):
    np.random.seed(seed)
    _w = jnp.asarray

    def _rec_inputs():
        import jax
        import jax.numpy as jnp
        _rk = jax.random.key(seed)
        x = -0.000147625 + 0.999875 * jax.random.normal(jax.random.fold_in(_rk, 1), (64, 3, 224, 224), jnp.float32)
        cls_tok = 0.02 * jax.random.normal(jax.random.fold_in(_rk, 5), (1, 1, 128), jnp.float32)
        return (x, cls_tok)
    x, cls_tok = _rec_inputs()

    def _L0_tok_setup():
        import jax, jax.numpy as jnp
        import numpy as np
        N_PATCHES = 8
        PATCH = 28
        C = 3
        IN_D = C * PATCH * PATCH
        HID = 128
        SEQ = N_PATCHES * N_PATCHES + 1

        def _positional_embedding(seq_len, dim):
            i = np.arange(seq_len)[:, None].astype(np.float32)
            j = np.arange(dim)[None, :].astype(np.float32)
            ang = i / np.power(100000.0, j / dim)
            pe = np.where(j % 2 == 0, np.sin(ang), np.cos(ang))
            return jnp.asarray(pe, dtype=jnp.float32)
        key = jax.random.key(seed)
        k1, k2, k3, k4 = jax.random.split(key, 4)
        B = 64
        X = jax.random.normal(k1, (B, C, 224, 224), dtype=jnp.float32)
        bound = 1.0 / np.sqrt(IN_D)
        W = jax.random.uniform(k2, (HID, IN_D), minval=-bound, maxval=bound, dtype=jnp.float32)
        b = jax.random.uniform(k3, (HID,), minval=-bound, maxval=bound, dtype=jnp.float32)
        class_token = jax.random.uniform(k4, (1, HID), dtype=jnp.float32)
        pos_embed = _positional_embedding(SEQ, HID)
        return {'X': X, 'W': W, 'b': b, 'class_token': class_token, 'pos_embed': pos_embed}
    _L0_tok_all = _L0_tok_setup()
    _L0_tok_in = {k: v for k, v in _L0_tok_all.items() if k in ('W', 'b', 'class_token', 'pos_embed')}
    del _L0_tok_all

    def _L0_attn_setup():
        import jax, jax.numpy as jnp
        import numpy as np
        import math
        B, N_COLS, CHANNELS, N_HEADS = (64, 64, 128, 8)
        D_HEAD = CHANNELS // N_HEADS

        def _split_heads(t):
            b, n, c = t.shape
            return t.reshape(b, n, N_HEADS, D_HEAD).transpose(0, 2, 1, 3)
        key = jax.random.key(seed)
        ks = jax.random.split(key, 9)
        C = CHANNELS
        s = 0.02
        x = jax.random.normal(ks[0], (B, N_COLS, C), dtype=jnp.float32)
        Wq = jax.random.normal(ks[1], (C, C), dtype=jnp.float32) * s
        Wk = jax.random.normal(ks[2], (C, C), dtype=jnp.float32) * s
        Wv = jax.random.normal(ks[3], (C, C), dtype=jnp.float32) * s
        Wo = jax.random.normal(ks[4], (C, C), dtype=jnp.float32) * s
        bq = jnp.zeros((C,), dtype=jnp.float32)
        bk = jnp.zeros((C,), dtype=jnp.float32)
        bv = jnp.zeros((C,), dtype=jnp.float32)
        bo = jnp.zeros((C,), dtype=jnp.float32)
        return {'x': x, 'Wq': Wq, 'bq': bq, 'Wk': Wk, 'bk': bk, 'Wv': Wv, 'bv': bv, 'Wo': Wo, 'bo': bo}
    _L0_attn_all = _L0_attn_setup()
    _L0_attn_in = {k: v for k, v in _L0_attn_all.items() if k in ('Wq', 'bq', 'Wk', 'bk', 'Wv', 'bv', 'Wo', 'bo')}
    del _L0_attn_all

    def _L0_ffn_setup():
        import jax, jax.numpy as jnp
        import numpy as np
        TOP_K = 2
        key = jax.random.key(seed)
        ks = jax.random.split(key, 4)
        b, t, d, e, h = (2, 512, 128, 8, 256)
        scale = 0.02
        return {'x': jax.random.normal(ks[0], (b, t, d), dtype=jnp.float32), 'router_w': jax.random.normal(ks[1], (e, d), dtype=jnp.float32) * scale, 'router_b': jnp.zeros((e,), dtype=jnp.float32), 'fc1_w': jax.random.normal(ks[2], (e, 2 * h, d), dtype=jnp.float32) * scale, 'fc1_b': jnp.zeros((e, 2 * h), dtype=jnp.float32), 'fc2_w': jax.random.normal(ks[3], (e, d, h), dtype=jnp.float32) * scale, 'fc2_b': jnp.zeros((e, d), dtype=jnp.float32)}
    _L0_ffn_all = _L0_ffn_setup()
    _L0_ffn_in = {k: v for k, v in _L0_ffn_all.items() if k in ('router_w', 'router_b', 'fc1_w', 'fc1_b', 'fc2_w', 'fc2_b')}
    del _L0_ffn_all

    def _L1_attn_setup():
        import jax, jax.numpy as jnp
        import numpy as np
        OUT_DIM = 128
        key = jax.random.key(seed)
        k1, k2 = jax.random.split(key)
        x = jax.random.normal(k1, (8, 512, 128), dtype=jnp.float32)
        w_qkv = jax.random.normal(k2, (128, 3 * OUT_DIM), dtype=jnp.float32) * 128 ** (-0.5)
        return {'x': x, 'w_qkv': w_qkv}
    _L1_attn_all = _L1_attn_setup()
    _L1_attn_in = {k: v for k, v in _L1_attn_all.items() if k in ('w_qkv',)}
    del _L1_attn_all

    def _L1_ffn_setup():
        import jax, jax.numpy as jnp
        import numpy as np
        NUM_TILES = 64
        TPC = 8
        GRID = 16
        EPS = 1e-05
        key = jax.random.key(seed)
        ks = jax.random.split(key, 6)
        B, S, D, T, DH, G = (2, 256, 128, NUM_TILES, 128, GRID)
        x = jax.random.normal(ks[0], (B, S, D), dtype=jnp.float32)
        gamma = jnp.ones((D,), jnp.float32)
        beta = jnp.zeros((D,), jnp.float32)
        Wd = jax.random.normal(ks[1], (T, DH, D), dtype=jnp.float32) * 0.02
        spline_bases = jax.random.normal(ks[2], (T, DH, G), dtype=jnp.float32) * 0.1
        spline_slopes = jax.random.normal(ks[3], (T, DH, G), dtype=jnp.float32) * 0.1
        Wu = jax.random.normal(ks[4], (T, D, DH), dtype=jnp.float32) * 0.02
        scale = jnp.full((T,), 0.1, jnp.float32)
        return {'x': x, 'gamma': gamma, 'beta': beta, 'Wd': Wd, 'spline_bases': spline_bases, 'spline_slopes': spline_slopes, 'Wu': Wu, 'scale': scale}
    _L1_ffn_all = _L1_ffn_setup()
    _L1_ffn_in = {k: v for k, v in _L1_ffn_all.items() if k in ('gamma', 'beta', 'Wd', 'spline_bases', 'spline_slopes', 'Wu', 'scale')}
    del _L1_ffn_all
    return {'x': x, 'cls_tok': cls_tok, 'L0_tok_W': _L0_tok_in['W'], 'L0_tok_b': _L0_tok_in['b'], 'L0_tok_class_token': _L0_tok_in['class_token'], 'L0_tok_pos_embed': _L0_tok_in['pos_embed'], 'L0_attn_Wq': _L0_attn_in['Wq'], 'L0_attn_bq': _L0_attn_in['bq'], 'L0_attn_Wk': _L0_attn_in['Wk'], 'L0_attn_bk': _L0_attn_in['bk'], 'L0_attn_Wv': _L0_attn_in['Wv'], 'L0_attn_bv': _L0_attn_in['bv'], 'L0_attn_Wo': _L0_attn_in['Wo'], 'L0_attn_bo': _L0_attn_in['bo'], 'L0_ffn_router_w': _L0_ffn_in['router_w'], 'L0_ffn_router_b': _L0_ffn_in['router_b'], 'L0_ffn_fc1_w': _L0_ffn_in['fc1_w'], 'L0_ffn_fc1_b': _L0_ffn_in['fc1_b'], 'L0_ffn_fc2_w': _L0_ffn_in['fc2_w'], 'L0_ffn_fc2_b': _L0_ffn_in['fc2_b'], 'L1_attn_w_qkv': _L1_attn_in['w_qkv'], 'L1_ffn_gamma': _L1_ffn_in['gamma'], 'L1_ffn_beta': _L1_ffn_in['beta'], 'L1_ffn_Wd': _L1_ffn_in['Wd'], 'L1_ffn_spline_bases': _L1_ffn_in['spline_bases'], 'L1_ffn_spline_slopes': _L1_ffn_in['spline_slopes'], 'L1_ffn_Wu': _L1_ffn_in['Wu'], 'L1_ffn_scale': _L1_ffn_in['scale']}

def reference(x, cls_tok, L0_tok_W, L0_tok_b, L0_tok_class_token, L0_tok_pos_embed, L0_attn_Wq, L0_attn_bq, L0_attn_Wk, L0_attn_bk, L0_attn_Wv, L0_attn_bv, L0_attn_Wo, L0_attn_bo, L0_ffn_router_w, L0_ffn_router_b, L0_ffn_fc1_w, L0_ffn_fc1_b, L0_ffn_fc2_w, L0_ffn_fc2_b, L1_attn_w_qkv, L1_ffn_gamma, L1_ffn_beta, L1_ffn_Wd, L1_ffn_spline_bases, L1_ffn_spline_slopes, L1_ffn_Wu, L1_ffn_scale):
    import jax
    import jax.numpy as jnp

    def _L0_tok_ref(X, W, b, class_token, pos_embed):
        import jax, jax.numpy as jnp
        import numpy as np
        N_PATCHES = 8
        PATCH = 28
        C = 3
        IN_D = C * PATCH * PATCH
        HID = 128
        SEQ = N_PATCHES * N_PATCHES + 1

        def _positional_embedding(seq_len, dim):
            i = np.arange(seq_len)[:, None].astype(np.float32)
            j = np.arange(dim)[None, :].astype(np.float32)
            ang = i / np.power(100000.0, j / dim)
            pe = np.where(j % 2 == 0, np.sin(ang), np.cos(ang))
            return jnp.asarray(pe, dtype=jnp.float32)
        B = X.shape[0]
        patches = X.reshape(B, C, N_PATCHES, PATCH, N_PATCHES, PATCH)
        patches = patches.transpose(0, 2, 4, 1, 3, 5).reshape(B, N_PATCHES * N_PATCHES, IN_D)
        tokens = jnp.einsum('bpi,hi->bph', patches, W) + b
        cls = jnp.broadcast_to(class_token[None, :, :], (B, 1, HID))
        tokens = jnp.concatenate([cls, tokens], axis=1)
        return tokens * pos_embed[None, :, :]

    def _L0_attn_ref(x, Wq, bq, Wk, bk, Wv, bv, Wo, bo):
        import jax, jax.numpy as jnp
        import numpy as np
        import math
        B, N_COLS, CHANNELS, N_HEADS = (64, 64, 128, 8)
        D_HEAD = CHANNELS // N_HEADS

        def _split_heads(t):
            b, n, c = t.shape
            return t.reshape(b, n, N_HEADS, D_HEAD).transpose(0, 2, 1, 3)
        b, n, c = x.shape
        Q = _split_heads(x @ Wq + bq)
        K = _split_heads(x @ Wk + bk)
        V = _split_heads(x @ Wv + bv)
        scores = jnp.einsum('bhqd,bhkd->bhqk', Q, K)
        ids = jnp.arange(n)
        mask = jnp.where(ids[None, :] <= ids[:, None], 0.0, -100000.0).astype(scores.dtype)
        scaled = (scores + mask[None, None]) / math.sqrt(D_HEAD)
        probs = jax.nn.softmax(scaled, axis=-1)
        attn = jnp.einsum('bhqk,bhkd->bhqd', probs, V)
        out = attn.transpose(0, 2, 1, 3).reshape(b, n, c)
        return out @ Wo + bo

    def _L0_ffn_ref(x, router_w, router_b, fc1_w, fc1_b, fc2_w, fc2_b):
        import jax, jax.numpy as jnp
        import numpy as np
        TOP_K = 2
        n_experts = router_w.shape[0]
        temp = 1.0
        logits = (jnp.einsum('btd,ed->bte', x, router_w) + router_b) / temp
        topk_val, topk_idx = jax.lax.top_k(logits, TOP_K)
        weights = jax.nn.softmax(topk_val, axis=-1)
        onehot = jax.nn.one_hot(topk_idx, n_experts, dtype=x.dtype)
        cw = jnp.einsum('btk,btke->bte', weights, onehot)
        h = jnp.einsum('btd,efd->btef', x, fc1_w) + fc1_b
        h1, h2 = jnp.split(h, 2, axis=-1)
        a = jax.nn.silu(h1) * h2
        y = jnp.einsum('bteh,edh->bted', a, fc2_w) + fc2_b
        out = jnp.einsum('bted,bte->btd', y, cw)
        return out

    def _L1_attn_ref(x, w_qkv):
        import jax, jax.numpy as jnp
        import numpy as np
        OUT_DIM = 128
        qkv = jnp.einsum('bnd,de->bne', x, w_qkv)
        q, k, v = jnp.split(qkv, 3, axis=-1)
        scale = OUT_DIM ** (-0.5)
        att_logit = jnp.einsum('bqd,bkd->bqk', q, k) * scale
        att_weight = jax.nn.softmax(att_logit, axis=-1)
        return jnp.einsum('bqk,bkd->bqd', att_weight, v)

    def _L1_ffn_ref(x, gamma, beta, Wd, spline_bases, spline_slopes, Wu, scale):
        import jax, jax.numpy as jnp
        import numpy as np
        NUM_TILES = 64
        TPC = 8
        GRID = 16
        EPS = 1e-05
        B, S, D = x.shape
        T, DH, _ = Wd.shape
        C = T // TPC
        N = B * S
        mu = x.mean(-1, keepdims=True)
        var = ((x - mu) ** 2).mean(-1, keepdims=True)
        xn = (x - mu) * jax.lax.rsqrt(var + EPS) * gamma + beta
        xf = xn.reshape(N, D)
        tile_sigs = jnp.sign(Wd.mean(axis=1))
        cluster_sigs = jnp.sign(tile_sigs.reshape(C, TPC, D).mean(1))
        in_sigs = jnp.sign(xf)
        best_c = jnp.argmax(in_sigs @ cluster_sigs.T, axis=-1)
        tile_scores = (in_sigs @ tile_sigs.T).reshape(N, C, TPC)
        sc = jnp.take_along_axis(tile_scores, best_c[:, None, None], axis=1)[:, 0, :]
        local_best = jnp.argmax(sc, axis=-1)
        tidx = best_c * TPC + local_best
        h = jnp.einsum('nd,nhd->nh', xf, Wd[tidx])
        hn = jax.nn.sigmoid(h)
        idx = jnp.clip((hn * GRID).astype(jnp.int32), 0, GRID - 1)
        base = jnp.take_along_axis(spline_bases[tidx], idx[..., None], axis=-1)[..., 0]
        slope = jnp.take_along_axis(spline_slopes[tidx], idx[..., None], axis=-1)[..., 0]
        local_pos = hn * GRID - idx.astype(h.dtype)
        hs = base + slope * local_pos
        y = jnp.einsum('nh,ndh->nd', hs, Wu[tidx]) * scale[tidx][:, None]
        return x + y.reshape(B, S, D)
    h = _L0_tok_ref(x, L0_tok_W, L0_tok_b, L0_tok_class_token, L0_tok_pos_embed)
    h = jnp.concatenate([jnp.broadcast_to(cls_tok, (h.shape[0], 1, h.shape[2])), h], axis=1)
    h = h + _L0_attn_ref(_layernorm(h, axis=-1), L0_attn_Wq, L0_attn_bq, L0_attn_Wk, L0_attn_bk, L0_attn_Wv, L0_attn_bv, L0_attn_Wo, L0_attn_bo)
    h = h + _L0_ffn_ref(_layernorm(h, axis=-1), L0_ffn_router_w, L0_ffn_router_b, L0_ffn_fc1_w, L0_ffn_fc1_b, L0_ffn_fc2_w, L0_ffn_fc2_b)
    h = h + _L1_attn_ref(_layernorm(h, axis=-1), L1_attn_w_qkv)
    h = h + _L1_ffn_ref(_layernorm(h, axis=-1), L1_ffn_gamma, L1_ffn_beta, L1_ffn_Wd, L1_ffn_spline_bases, L1_ffn_spline_slopes, L1_ffn_Wu, L1_ffn_scale)
    return h

_drawn_inputs = setup_inputs


def setup_inputs(seed=0):
    import zlib

    import numpy as np

    out = dict(_drawn_inputs(seed))
    spreads = {'L0_attn_bq': (0.0, 0.8),
     'L0_attn_bk': (0.0, 0.8),
     'L0_attn_bv': (0.0, 0.1),
     'L0_attn_bo': (0.0, 0.1),
     'L0_ffn_router_b': (0.0, 0.1),
     'L0_ffn_fc1_b': (0.0, 0.8),
     'L0_ffn_fc2_b': (0.0, 0.1),
     'L1_ffn_gamma': (1.0, 0.6),
     'L1_ffn_beta': (0.0, 0.8),
     'L1_ffn_scale': (0.10000000149011612, 0.6)}
    factors = {'L0_attn_Wq': 8.0,
     'L0_attn_Wk': 8.0,
     'L0_ffn_fc1_w': 3.387,
     'L0_ffn_fc2_w': 3.308,
     'L1_ffn_Wd': 8.0,
     'L1_ffn_spline_bases': 8.0,
     'L1_ffn_spline_slopes': 8.0,
     'L1_ffn_Wu': 8.0}
    for name, (base, spread) in spreads.items():
        noise = np.random.default_rng([zlib.crc32(name.encode()), seed]).standard_normal(out[name].shape)
        drawn = base * np.exp(spread * noise) if base else spread * noise
        out[name] = jnp.asarray(drawn.astype(out[name].dtype))
    for name, factor in factors.items():
        out[name] = (out[name] * factor).astype(out[name].dtype)
    return out
```

```python
from contextlib import ExitStack

import concourse.bass as bass
from concourse import mybir

P = 128
IMAGES = 64
PATCHES = 64
CLS = 2
SEQ = CLS + PATCHES
D = 128
TILES = IMAGES * SEQ // P
PTILES = TILES - 1
GROUP = 4
GROUPS = IMAGES // GROUP
GT = GROUP * PATCHES // P
PK, PC = 112, 21
HEADS, DH = 8, 16
EPS = 1e-5

ALU = mybir.AluOpType
ACT = mybir.ActivationFunctionType
F32 = mybir.dt.float32
BF16 = mybir.dt.bfloat16
I32 = mybir.dt.int32
U32 = mybir.dt.uint32
AX_X = mybir.AxisListType.X
ds = bass.ds


class Chain:

    def __init__(self, eng, sem, turns=None):
        self.turns = turns
        self.eng, self.sem, self.count, self.made = eng, sem, 0, 0

    def mark(self, ins):
        ins.then_inc(self.sem, 1)
        self.count = self.count + 1
        self.made += 1
        return ins

    def sync(self):
        self.eng.wait_ge(self.sem, self.count)

    def apart(self):
        self.sync()
        self.eng.sem_inc(self.turns, 1)

    def step(self, ins):
        self.mark(ins)
        self.sync()

    def enter(self, i, marks):
        self.base, self.marks, self.made = self.count, marks, 0
        self.count = self.base + i * marks

    def leave(self, trips):
        assert self.made == self.marks, (self.made, self.marks)
        self.count = self.base + trips * self.marks


def row_bc(dram_row):
    return dram_row.rearrange("(o d) -> o d", o=1).to_broadcast([P, dram_row.shape[0]])


def rsqrt_steps(pool, chain, var, minus_half, veps, t, r):
    g = pool
    chain.eng.sem_inc(chain.turns, 1)
    chain.step(g.tensor_scalar(veps, var, EPS, None, ALU.add))
    chain.step(g.tensor_tensor(r, veps, minus_half, ALU.pow))
    chain.step(g.tensor_tensor(t, r, r, ALU.mult))
    chain.step(g.tensor_tensor(t, t, veps, ALU.mult))
    chain.eng.sem_inc(chain.turns, 1)
    chain.step(g.tensor_scalar(t, t, -0.5, 1.5, ALU.mult, ALU.add))
    return g.tensor_tensor(r, r, t, ALU.mult)


RSQRT_MARKS = 5


def patch_attention(nc, resid, ident, a):
    with ExitStack() as ctx:
        def sb(name, shape, dt=F32):
            return ctx.enter_context(nc.sbuf_tensor(name, shape, dt))

        def psum(name, shape):
            return ctx.enter_context(nc.psum_tensor(name, shape, F32))

        def sem(name):
            return ctx.enter_context(nc.semaphore(name))

        ps_s = psum("pa_scores", [P, 2, 512])
        ps_pt = psum("pa_probsT", [P, 2, 512])
        ps_tok = psum("pa_tokens", [P, 512])
        ps_m0 = psum("pa_m0", [P, 512])
        ps_m1 = psum("pa_m1", [P, 512])
        ps_m2 = psum("pa_m2", [P, 512])

        w_patch = sb("pa_w_patch", [P, PC, D])
        x_patch = [sb(f"pa_x{t}", [P, PC, P]) for t in range(GT)]
        wq, wk, wv, wo = (sb(f"pa_w{n}", [P, D]) for n in "qkvo")
        bias_cols = sb("pa_bias_cols", [P, 3])
        b_patch = sb("pa_b_patch", [P, D])
        b_out = sb("pa_b_out", [P, D])
        pos = sb("pa_pos", [P, D])
        cls_mul = sb("pa_cls_mul", [P, D])
        head_mask = sb("pa_head_mask", [P, HEADS])
        diag125 = sb("pa_diag125", [P, SEQ], BF16)
        causal = sb("pa_causal", [P, 4, SEQ], BF16)
        minus_half = sb("pa_minus_half", [P, GT])
        stats = sb("pa_stats", [P, GT, 6])
        mv = sb("pa_mv", [P, GT, 2])
        veps, newton, rstd = (sb(f"pa_{n}", [P, GT]) for n in ("veps", "newton", "rstd"))
        xn = sb("pa_xn", [P, GT, D])
        xnT = sb("pa_xnT", [P, GROUP, SEQ])
        qT = sb("pa_qT", [P, GROUP, SEQ])
        kT = sb("pa_kT", [P, GROUP, SEQ])
        kbd = sb("pa_kbd", [P, GROUP, HEADS, SEQ])
        v1 = sb("pa_v1", [P, GROUP, HEADS, DH + 1])
        top = sb("pa_top", [P, GROUP, HEADS])
        probs = [sb(f"pa_probs{b}", [P, HEADS, SEQ]) for b in range(2)]
        probsT = [sb(f"pa_probsT{b}", [P, HEADS, SEQ]) for b in range(2)]
        rsum = sb("pa_rsum", [P, GROUP, HEADS])
        o_rows = sb("pa_o_rows", [P, GROUP, D])
        oT = sb("pa_oT", [P, GROUP * PATCHES])
        oT_cls = sb("pa_oT_cls", [P, IMAGES, CLS])

        s_w = sem("pa_weights")
        s_w2 = sem("pa_weights_act")
        s_wp = sem("pa_patch_weights")
        s_x = [sem(f"pa_x_loaded{t}") for t in range(GT)]
        s_xfree = [sem(f"pa_x_used{t}") for t in range(GT)]
        s_const = sem("pa_constants")
        s_pool = sem("pa_pool_chain")
        s_dve = sem("pa_dve_chain")
        s_turns = [sem(f"pa_turns{e}") for e in range(2)]
        s_stats = sem("pa_stats_ready")
        s_rstd = sem("pa_rstd_ready")
        s_xn = sem("pa_xn_ready")
        s_xnT_ps = sem("pa_xnT_in_psum")
        s_xnT = sem("pa_xnT_ready")
        s_q_ps = sem("pa_q_in_psum")
        s_k_ps = sem("pa_k_in_psum")
        s_v_ps = sem("pa_v_in_psum")
        s_q = sem("pa_q_ready")
        s_k = sem("pa_k_ready")
        s_v = sem("pa_v_ready")
        s_kbd = sem("pa_kbd_ready")
        s_s = sem("pa_scores_ready")
        s_sub = sem("pa_scores_taken")
        s_p = sem("pa_probs_ready")
        s_pT_ps = sem("pa_probsT_in_psum")
        s_pT = sem("pa_probsT_ready")
        s_o_ps = sem("pa_o_in_psum")
        s_o = sem("pa_o_ready")
        s_oT_ps = sem("pa_oT_in_psum")
        s_oT = sem("pa_oT_ready")
        s_cls = sem("pa_oT_cls_kept")
        s_proj = sem("pa_projection_ready")
        s_bo = sem("pa_bias_added")
        s_h = sem("pa_projection_taken")

        scores = ps_s[0:SEQ, :, 0:4 * SEQ].rearrange("p b (h k) -> p b h k", h=4)
        probsT_ps = ps_pt[0:SEQ, :, 0:4 * SEQ].rearrange("p b (h k) -> p b h k", h=4)

        def rows(n):
            return n[:, 0:GROUP * SEQ].rearrange("p (i s) -> p i s", i=GROUP)

        def o_ps(i):
            return (ps_m1, ps_m2)[i % 2][0:SEQ, 0:HEADS * (DH + 1)].rearrange("p (h d) -> p h d", h=HEADS)

        LAST = GROUPS - 1

        block = ctx.enter_context(nc.Block())

        @block.sync
        def _(sp):
            sp.dma_start(w_patch[0:PK, :, :], a["w_patch"]).then_inc(s_wp, 16)
            for t in range(GT):
                sp.dma_start(x_patch[t][0:PK, :, :], a["x"][0, t]).then_inc(s_x[t], 16)
            with sp.Fori(1, GROUPS) as g:
                for t in range(GT):
                    sp.wait_ge(s_xfree[t], g)
                    sp.dma_start(x_patch[t][0:PK, :, :], a["x"][g, t]).then_inc(s_x[t], 16)

        @block.gpsimd
        def _(pool):
            ch = Chain(pool, s_pool, s_turns[0])
            ch.mark(pool.memset(head_mask[:], 1.0))
            ch.mark(pool.memset(diag125[:], 0.0))
            ch.mark(pool.memset(causal[:], 0.0))
            ch.sync()
            ch.step(pool.affine_select(out=head_mask[:], in_=head_mask[:], compare_op=ALU.is_ge, fill=0.0,
                                       base=0, pattern=[[-DH, HEADS]], channel_multiplier=1))
            pool.affine_select(out=head_mask[:], in_=head_mask[:], compare_op=ALU.is_ge, fill=0.0,
                               base=DH - 1, pattern=[[DH, HEADS]], channel_multiplier=-1).then_inc(s_const, 1)
            pool.affine_select(out=diag125[:], in_=diag125[:], compare_op=ALU.not_equal, fill=125.0,
                               base=0, pattern=[[-1, SEQ]], channel_multiplier=1).then_inc(s_const, 1)
            pool.affine_select(out=causal[:], in_=causal[:], compare_op=ALU.is_ge, fill=-800.0,
                               base=0, pattern=[[0, 4], [-1, SEQ]], channel_multiplier=1).then_inc(s_const, 1)
            pool.memset(v1[:], 1.0).then_inc(s_const, 1)
            pool.memset(minus_half[:], -0.5).then_inc(s_const, 1)
            pool.wait_ge(s_const, 5)

            def norm_scale(n):
                pool.wait_ge(s_stats, n)
                rsqrt_steps(pool, ch, mv[:, :, 1], minus_half[:], veps[:], newton[:], rstd[:]).then_inc(s_rstd, 1)

            def add_output_bias(g):
                pool.wait_ge(s_xn, g + 2)
                tiles = resid[:, ds(g * GT, GT), :]
                pool.tensor_tensor(tiles, tiles, b_out[:, None, :].to_broadcast([P, GT, D]),
                                   ALU.add).then_inc(s_bo, 1)

            def attention(g, more):
                pool.wait_ge(s_k, g + 1)
                for i in range(GROUP):
                    pool.wait_ge(s_s, g * GROUP + i + 1)
                    pool.tensor_tensor(kbd[:, i], kT[:, i, None, :].to_broadcast([P, HEADS, SEQ]),
                                       head_mask[:, :, None].to_broadcast([P, HEADS, SEQ]),
                                       ALU.mult).then_inc(s_kbd, 1)
                if more:
                    norm_scale(g + 3)
                    add_output_bias(g + 1)

            norm_scale(1)
            norm_scale(2)
            pool.wait_ge(s_w2, 16)
            pool.wait_ge(s_xn, 1)
            pool.tensor_tensor(resid[:, PTILES, :], resid[:, PTILES, :], b_out[:], ALU.add).then_inc(s_bo, 1)
            add_output_bias(0)
            with pool.Fori(0, LAST) as g:
                ch.enter(g, RSQRT_MARKS)
                attention(g, True)
                ch.leave(LAST)
            attention(LAST, False)

        @block.vector
        def _(dve):
            ch = Chain(dve, s_dve, s_turns[1])

            def norm_apply(t, tile):
                return dve.tensor_scalar(xn[:, t, :], resid[:, tile, :], mv[:, t, 0:1], rstd[:, t:t + 1],
                                         ALU.subtract, ALU.mult)

            dve.wait_ge(s_w, 16 * 10)
            ch.step(dve.tensor_tensor(resid[:, PTILES, :], resid[:, PTILES, :], cls_mul[:], ALU.mult))
            for t in range(GT):
                ch.mark(dve.bn_stats(stats[:, t, :], resid[:, PTILES, :]))
            ch.sync()
            for t in range(GT):
                ins = dve.bn_aggr(mv[:, t, :], stats[:, t, :])
                if t < GT - 1:
                    ch.mark(ins)
            ch.sync()
            ins.then_inc(s_stats, 1)
            dve.wait_ge(s_rstd, 1)
            norm_apply(0, PTILES).then_inc(s_xn, 1)

            def tokens(g, n):
                tiles = resid[:, ds(g * GT, GT), :]
                dve.wait_ge(s_xfree[GT - 1], g + 1)
                ch.step(dve.tensor_tensor(tiles, ps_tok[:, 0:GT * D].rearrange("p (t d) -> p t d", t=GT),
                                          b_patch[:, None, :].to_broadcast([P, GT, D]), ALU.add))
                ch.step(dve.tensor_tensor(tiles, tiles, pos[:, None, :].to_broadcast([P, GT, D]), ALU.mult))
                ch.apart()
                for t in range(GT):
                    ch.mark(dve.bn_stats(stats[:, t, :], resid[:, g * GT + t, :]))
                ch.apart()
                for t in range(GT - 1):
                    ch.mark(dve.bn_aggr(mv[:, t, :], stats[:, t, :]))
                dve.bn_aggr(mv[:, GT - 1, :], stats[:, GT - 1, :]).then_inc(s_stats, 1)

            TOKEN_MARKS = 2 + GT + GT - 1

            def normalise(g):
                dve.wait_ge(s_rstd, g + 2)
                dve.wait_ge(s_xnT_ps, g + 1)
                for t in range(GT - 1):
                    ch.mark(norm_apply(t, g * GT + t))
                ch.sync()
                norm_apply(GT - 1, g * GT + GT - 1).then_inc(s_xn, 1)

            def softmax(g, i):
                dve.wait_ge(s_s, (g + 1) * GROUP + i + 1)
                ch.step(dve.tensor_reduce(top[0:SEQ, i, :].rearrange("p (b h) -> p b h", b=2), scores, AX_X, ALU.max))
                dve.tensor_tensor(probs[i % 2][0:SEQ].rearrange("p (b h) k -> p b h k", b=2), scores,
                                  top[0:SEQ, i, :].rearrange("p (b h) -> p b h", b=2)[:, :, :, None]
                                  .to_broadcast([SEQ, 2, 4, SEQ]), ALU.subtract).then_inc(s_sub, 1)

            def divide(g, i):
                dve.wait_ge(s_o_ps, g * GROUP + i + 1)
                ch.step(dve.reciprocal(rsum[0:SEQ, i, :], o_ps(i)[:, :, DH]))
                dve.tensor_tensor(o_rows[0:SEQ, i, :].rearrange("p (h d) -> p h d", h=HEADS), o_ps(i)[:, :, 0:DH],
                                  rsum[0:SEQ, i, :, None].to_broadcast([SEQ, HEADS, DH]), ALU.mult).then_inc(s_o, 1)

            def attention(g, more):
                dve.wait_ge(s_v_ps, g + 1)
                dve.tensor_copy(v1[0:SEQ, :, :, 0:DH],
                                ps_m0[0:SEQ, :].rearrange("p (i h d) -> p i h d", i=GROUP, h=HEADS)).then_inc(s_v, 1)
                softmax(g, 0)
                softmax(g, 1)
                divide(g, 0)
                softmax(g, 2)
                divide(g, 1)
                softmax(g, 3)
                divide(g, 2)
                if more:
                    tokens(g + 1, 0)
                divide(g, 3)
                if more:
                    normalise(g + 1)
                dve.wait_ge(s_proj, g + 1)
                dve.wait_ge(s_bo, g + 2)
                tiles = resid[:, ds(g * GT, GT), :]
                dve.tensor_tensor(tiles, tiles, ps_m1[:, 0:GT * D].rearrange("p (t d) -> p t d", t=GT),
                                  ALU.add).then_inc(s_h, 1)

            tokens(0, 0)
            normalise(0)
            dve.wait_ge(s_const, 5)
            with dve.Fori(0, LAST) as g:
                ch.enter(g, 2 * GROUP + TOKEN_MARKS + GT - 1)
                attention(g, True)
                ch.leave(LAST)
            attention(LAST, False)
            dve.wait_ge(s_proj, GROUPS + 1)
            dve.wait_ge(s_bo, GROUPS + 1)
            dve.tensor_tensor(resid[:, PTILES, :], resid[:, PTILES, :], ps_m2[:, 0:D], ALU.add).then_inc(s_h, 1)

        @block.scalar
        def _(act):
            for dst, src in [(wq[:], a["wq"]), (wk[:], a["wk"]), (wv[:], a["wv"]), (wo[:], a["wo"]),
                             (bias_cols[:], a["bias_cols"]), (b_patch[:], row_bc(a["b_patch"])),
                             (resid[:, PTILES, :], a["cls_rows"]), (cls_mul[:], a["cls_mul"]),
                             (pos[0:PATCHES, :], a["pos"]), (pos[PATCHES:P, :], a["pos"])]:
                act.dma_start(dst, src).then_inc(s_w, 16)
            act.dma_start(b_out[:], row_bc(a["bo"])).then_inc(s_w2, 16)

            def norm_transposed(g):
                act.wait_ge(s_xnT_ps, g + 2)
                nc.scalar.copy(xnT[:, :, CLS:SEQ], ps_m0[:, 0:GT * P].rearrange("p (i s) -> p i s", i=GROUP))\
                    .then_inc(s_xnT, 1)

            def attention(g, more):
                act.wait_ge(s_q_ps, g + 1)
                nc.scalar.activation(qT[:], rows(ps_m1), ACT.Identity, bias=bias_cols[:, 0:1]).then_inc(s_q, 1)
                act.wait_ge(s_k_ps, g + 1)
                act.wait_ge(s_kbd, g * GROUP + 1)
                nc.scalar.activation(kT[:], rows(ps_m2), ACT.Identity, bias=bias_cols[:, 1:2]).then_inc(s_k, 1)
                for i in range(GROUP):
                    act.wait_ge(s_sub, g * GROUP + i + 2)
                    nc.scalar.activation(probs[i % 2][0:SEQ], probs[i % 2][0:SEQ], ACT.Exp,
                                         scale=1.0 / DH ** 0.5).then_inc(s_p, 1)
                    act.wait_ge(s_pT_ps, g * GROUP + i + 1)
                    nc.scalar.copy(probsT[i % 2][0:SEQ].rearrange("p (b h) k -> p b h k", b=2), probsT_ps)\
                        .then_inc(s_pT, 1)
                act.wait_ge(s_oT_ps, g + 1)
                nc.scalar.activation(oT_cls[:, ds(g * GROUP, GROUP), :], rows(ps_m0)[:, :, 0:CLS], ACT.Identity,
                                     bias=bias_cols[:, 2:3]).then_inc(s_cls, 1)
                nc.scalar.activation(oT[:].rearrange("p (i s) -> p i s", i=GROUP), rows(ps_m0)[:, :, CLS:SEQ],
                                     ACT.Identity, bias=bias_cols[:, 2:3]).then_inc(s_oT, 1)
                if more:
                    norm_transposed(g + 1)

            act.sem_inc(s_kbd, 1)
            act.wait_ge(s_xnT_ps, 1)
            nc.scalar.copy(xnT[:, :, 0:CLS], ps_m0[:, None, 0:CLS].to_broadcast([P, GROUP, CLS])).then_inc(s_xnT, 1)
            norm_transposed(0)
            act.wait_ge(s_w, 16 * 10)
            with act.Fori(0, LAST) as g:
                attention(g, True)
            attention(LAST, False)

        @block.tensor
        def _(pe):
            def patches(g, t, chunks):
                if chunks[0] == 0:
                    pe.wait_ge(s_x[t], 16 * (g + 1))
                    if t == 0:
                        pe.wait_ge(s_xn, g + 1)
                for c in chunks:
                    mm = nc.tensor.matmul(ps_tok[:, t * D:(t + 1) * D], x_patch[t][0:PK, c, :], w_patch[0:PK, c, :],
                                          start=(c == 0), stop=(c == PC - 1))
                if chunks[-1] == PC - 1:
                    mm.then_inc(s_xfree[t], 1)

            def norm_transposes(g):
                pe.wait_ge(s_xn, g + 2)
                for t in range(GT):
                    mm = nc.tensor.transpose(ps_m0[:, t * P:(t + 1) * P], xn[:, t, :], ident[:])
                mm.then_inc(s_xnT_ps, 1)

            def qkv(g):
                pe.wait_ge(s_xnT, g + 2)
                pe.wait_ge(s_h, g + 1)
                nc.tensor.matmul(rows(ps_m1), wq[:], xnT[:], start=True, stop=True).then_inc(s_q_ps, 1)
                nc.tensor.matmul(rows(ps_m2), wk[:], xnT[:], start=True, stop=True).then_inc(s_k_ps, 1)
                for i in range(GROUP):
                    mm = nc.tensor.matmul(ps_m0[0:SEQ, i * D:(i + 1) * D], xnT[:, i, :], wv[:], start=True, stop=True)
                mm.then_inc(s_v_ps, 1)
                pe.wait_ge(s_q, g + 1)

            def score(g, i):
                pe.wait_ge(s_kbd, g * GROUP + i + 2)
                pe.wait_ge(s_sub, g * GROUP + i + 1)
                for b in range(2):
                    nc.tensor.matmul(scores[:, b], diag125[0:SEQ, :], causal[0:SEQ], start=True, stop=False)
                    mm = nc.tensor.matmul(scores[:, b], qT[:, i, :], kbd[:, i, 4 * b:4 * b + 4, :],
                                          start=False, stop=True)
                mm.then_inc(s_s, 1)

            def transposes(g, i):
                pe.wait_ge(s_p, g * GROUP + i + 1)
                pe.wait_ge(s_pT, g * GROUP + i + 1)
                for h in range(HEADS):
                    mm = nc.tensor.transpose(probsT_ps[:, h // 4, h % 4, :], probs[i % 2][0:SEQ, h, :],
                                             ident[0:SEQ, 0:SEQ])
                mm.then_inc(s_pT_ps, 1)

            def values(g, i):
                pe.wait_ge(s_pT, g * GROUP + i + 2)
                if i == 0:
                    pe.wait_ge(s_v, g + 1)
                if i >= 2:
                    pe.wait_ge(s_o, g * GROUP + i - 1)
                for h in range(HEADS):
                    mm = nc.tensor.matmul(o_ps(i)[:, h, :], probsT[i % 2][0:SEQ, h, :], v1[0:SEQ, i, h, :],
                                          start=True, stop=True)
                mm.then_inc(s_o_ps, 1)

            def project(g):
                pe.wait_ge(s_o, (g + 1) * GROUP)
                for i in range(GROUP):
                    mm = nc.tensor.transpose(ps_m0[:, i * SEQ:(i + 1) * SEQ], o_rows[0:SEQ, i, :],
                                             ident[0:SEQ, 0:SEQ])
                mm.then_inc(s_oT_ps, 1)
                pe.wait_ge(s_oT, g + 1)
                for t in range(GT):
                    mm = nc.tensor.matmul(ps_m1[:, t * D:(t + 1) * D], oT[:, t * P:(t + 1) * P], wo[:],
                                          start=True, stop=True)
                mm.then_inc(s_proj, 1)

            def attention(g, more):
                qkv(g)
                score(g, 0)
                if more:
                    patches(g + 1, 0, range(0, 11))
                transposes(g, 0)
                score(g, 1)
                if more:
                    patches(g + 1, 0, range(11, PC))
                values(g, 0)
                transposes(g, 1)
                score(g, 2)
                if more:
                    patches(g + 1, 1, range(0, 11))
                values(g, 1)
                transposes(g, 2)
                score(g, 3)
                if more:
                    patches(g + 1, 1, range(11, PC))
                values(g, 2)
                transposes(g, 3)
                values(g, 3)
                project(g)
                if more:
                    norm_transposes(g + 1)

            pe.sem_inc(s_sub, 1)
            pe.sem_inc(s_pT, 1)
            pe.sem_inc(s_h, 1)
            pe.sem_inc(s_s, GROUP)
            pe.wait_ge(s_xn, 1)
            nc.tensor.transpose(ps_m0[:, 0:P], xn[:, 0, :], ident[:]).then_inc(s_xnT_ps, 1)
            pe.wait_ge(s_wp, 16)
            for t in range(GT):
                patches(0, t, range(PC))
            pe.wait_ge(s_xnT, 1)
            norm_transposes(0)
            pe.wait_ge(s_w, 16 * 10)
            pe.wait_ge(s_const, 5)
            with pe.Fori(0, LAST) as g:
                attention(g, True)
            attention(LAST, False)
            pe.wait_ge(s_cls, GROUPS)
            nc.tensor.matmul(ps_m2[:, 0:D], oT_cls[:].rearrange("p i c -> p (i c)"), wo[:],
                             start=True, stop=True).then_inc(s_proj, 1)

EXPERTS, HIDDEN, HC = 8, 256, 2
TRIO = 3
TRIOS = TILES // TRIO


def norm_statistics(dve, ch, resid, stats, mean, var, scratch):
    with dve.Fori(0, TRIOS) as i:
        ch.enter(i, TRIO)
        for j in range(TRIO):
            ch.mark(dve.bn_stats(stats[:, i * TRIO + j, :], resid[:, i * TRIO + j, :]))
        ch.leave(TRIOS)
    ch.sync()
    mean_e, mean_o, sq_e, sq_o = stats[:, :, 1], stats[:, :, 4], stats[:, :, 2], stats[:, :, 5]
    ch.mark(dve.tensor_tensor(mean, mean_e, mean_o, ALU.add))
    ch.mark(dve.tensor_tensor(scratch[0], mean_e, mean_o, ALU.subtract))
    ch.step(dve.tensor_tensor(scratch[1], sq_e, sq_o, ALU.add))
    ch.mark(dve.tensor_scalar(mean, mean, 0.5, None, ALU.mult))
    ch.mark(dve.tensor_scalar(scratch[1], scratch[1], 1.0 / D, None, ALU.mult))
    ch.step(dve.tensor_tensor(scratch[0], scratch[0], scratch[0], ALU.mult))
    return dve.scalar_tensor_tensor(out=var, in0=scratch[0], scalar=0.25, in1=scratch[1],
                                    op0=ALU.mult, op1=ALU.add)


def experts(nc, resid, ident, a, tables):
    with ExitStack() as ctx:
        def sb(name, shape, dt=F32):
            return ctx.enter_context(nc.sbuf_tensor(name, shape, dt))

        def sem(name):
            return ctx.enter_context(nc.semaphore(name))

        fc1 = sb("ex_fc1", [P, EXPERTS, 2 * HIDDEN])
        fc2 = sb("ex_fc2", [P, EXPERTS, HC, D])
        b1 = sb("ex_b1", [P, EXPERTS, 2 * HC])
        b2 = sb("ex_b2", [P, D])
        router = sb("ex_router", [P, EXPERTS])
        rb = sb("ex_router_bias", [P, EXPERTS])
        stats = sb("ex_stats", [P, TILES, 6])
        mean, var, veps, newton, rstd, minus_half, t0, t1 = (
            sb(f"ex_{n}", [P, TILES]) for n in ("mean", "var", "veps", "newton", "rstd", "minus_half", "t0", "t1"))
        xs = [sb(f"ex_xs{j}", [P, D]) for j in range(TRIO)]
        xTs = [sb(f"ex_xTs{j}", [P, P]) for j in range(TRIO)]
        xT = sb("ex_xT", [P, TILES * P])
        logits, second, eq, pick1, pick2, cw = (
            sb(f"ex_{n}", [P, TILES, EXPERTS]) for n in ("logits", "second", "eq", "pick1", "pick2", "cw"))
        first_wins = sb("ex_first_wins", [P, EXPERTS])
        m1, m2, f1, f2, dl, den, w1, w2 = (
            sb(f"ex_{n}", [P, TILES]) for n in ("m1", "m2", "f1", "f2", "dl", "den", "w1", "w2"))
        cws = sb("ex_cws", [P, TRIO, EXPERTS])
        cwT = sb("ex_cwT", [P, TRIO * P])
        gate = [sb(f"ex_gate{j}", [P, TRIO * P]) for j in range(HC)]
        act_t = [[sb(f"ex_act{b}{j}", [P, TRIO * P]) for j in range(HC)] for b in range(2)]
        acc = sb("ex_acc", [P, TRIO, D])

        s_w = sem("ex_weights")
        s_dve = sem("ex_dve_chain")
        s_sum = sem("ex_sum_chain")
        s_pool = sem("ex_pool_chain")
        s_turns = [sem(f"ex_turns{e}") for e in range(2)]
        s_const = sem("ex_constants")
        s_stats = sem("ex_stats_ready")
        s_rstd = sem("ex_rstd_ready")
        s_xs = sem("ex_xs_ready")
        s_xT_ps = sem("ex_xT_in_psum")
        s_xT = sem("ex_xT_ready")
        s_copy = sem("ex_xT_kept")
        s_logit = sem("ex_logits_in_psum")
        s_dl = sem("ex_top_difference")
        s_exp = sem("ex_top_exp")
        s_cws = sem("ex_cws_ready")
        s_cwT_ps = sem("ex_cwT_in_psum")
        s_cwT = sem("ex_cwT_ready")
        s_bias = sem("ex_bias_term_in_psum")
        s_init = sem("ex_acc_started")
        s_h1 = sem("ex_h1_in_psum")
        s_h2 = sem("ex_h2_in_psum")
        s_gate = sem("ex_gate_ready")
        s_a = sem("ex_act_ready")
        s_y = sem("ex_y_in_psum")
        s_acc = sem("ex_y_taken")
        STEPS = EXPERTS * HC

        with ExitStack() as prep:
            ps_x = [prep.enter_context(nc.psum_tensor(f"ex_ps_x{j}", [P, 512], F32)) for j in range(TRIO)]
            ps_l = prep.enter_context(nc.psum_tensor("ex_ps_logits", [P, 512], F32))
            block = prep.enter_context(nc.Block())

            @block.sync
            def _(sp):
                for dst, src in [(router[:], a["router"]), (rb[:], row_bc(a["router_b"])), (fc1[:], a["fc1"]),
                                 (fc2[:], a["fc2"]), (b1[:], a["b1"]), (b2[0:EXPERTS, :], a["b2"])]:
                    sp.dma_start(dst, src).then_inc(s_w, 16)

            @block.gpsimd
            def _(pool):
                ch = Chain(pool, s_pool, s_turns[0])
                pool.iota(first_wins[:], pattern=[[-1, EXPERTS]], base=EXPERTS, channel_multiplier=0,
                          allow_small_or_imprecise_dtypes=True).then_inc(s_const, 1)
                ch.step(pool.memset(minus_half[:], -0.5))
                pool.wait_ge(s_stats, 1)
                rsqrt_steps(pool, ch, var[:], minus_half[:], veps[:], newton[:], rstd[:]).then_inc(s_rstd, 1)
                with pool.Fori(0, TRIOS) as i:
                    for j in range(TRIO):
                        pool.wait_ge(s_xT, (i + 1) * TRIO + j + 1)
                        pool.tensor_copy(xT[:, ds((i * TRIO + j) * P, P)], xTs[j][:]).then_inc(s_copy, 1)

            @block.vector
            def _(dve):
                ch = Chain(dve, s_dve, s_turns[1])
                norm_statistics(dve, ch, resid, stats, mean[:], var[:], (t0[:], t1[:])).then_inc(s_stats, 1)
                dve.wait_ge(s_rstd, 1)
                with dve.Fori(0, TRIOS) as i:
                    for j in range(TRIO):
                        t = i * TRIO + j
                        dve.wait_ge(s_xT_ps, t + 1)
                        dve.tensor_scalar(xs[j][:], resid[:, t, :], mean[:, ds(t, 1)], rstd[:, ds(t, 1)],
                                          ALU.subtract, ALU.mult).then_inc(s_xs, 1)
                dve.wait_ge(s_logit, TILES + TRIO)
                dve.wait_ge(s_const, 1)
                dve.wait_ge(s_w, 16 * 6)

                def wide(x):
                    return x[:, :, None].to_broadcast([P, TILES, EXPERTS])

                ch.step(dve.tensor_tensor(logits[:], ps_l[:, 0:TILES * EXPERTS].rearrange("p (t e) -> p t e", e=EXPERTS),
                                          rb[:, None, :].to_broadcast([P, TILES, EXPERTS]), ALU.add))
                for x, m, f, pick in ((logits, m1, f1, pick1), (second, m2, f2, pick2)):
                    ch.step(dve.tensor_reduce(m[:], x[:], AX_X, ALU.max))
                    ch.step(dve.tensor_tensor(eq[:], x[:], wide(m), ALU.is_equal))
                    ch.step(dve.tensor_tensor(eq[:], eq[:], first_wins[:, None, :].to_broadcast([P, TILES, EXPERTS]),
                                              ALU.mult))
                    ch.step(dve.tensor_reduce(f[:], eq[:], AX_X, ALU.max))
                    ch.step(dve.tensor_tensor(pick[:], eq[:], wide(f), ALU.is_equal))
                    if x is logits:
                        ch.step(dve.scalar_tensor_tensor(out=second[:], in0=pick1[:], scalar=-3e38, in1=logits[:],
                                                         op0=ALU.mult, op1=ALU.add))
                dve.tensor_tensor(dl[:], m2[:], m1[:], ALU.subtract).then_inc(s_dl, 1)
                dve.wait_ge(s_exp, 1)
                ch.step(dve.tensor_scalar(den[:], dl[:], 1.0, None, ALU.add))
                ch.step(dve.reciprocal(w1[:], den[:]))
                ch.mark(dve.tensor_tensor(w2[:], dl[:], w1[:], ALU.mult))
                ch.step(dve.tensor_tensor(cw[:], pick1[:], wide(w1), ALU.mult))
                ch.step(dve.tensor_tensor(pick2[:], pick2[:], wide(w2), ALU.mult))
                dve.tensor_tensor(cw[:], cw[:], pick2[:], ALU.add)

            @block.scalar
            def _(act):
                act.sem_inc(s_xT, TRIO)
                with act.Fori(0, TRIOS) as i:
                    for j in range(TRIO):
                        t = i * TRIO + j
                        act.wait_ge(s_xT_ps, t + TRIO + 1)
                        act.wait_ge(s_logit, t + 1)
                        act.wait_ge(s_copy, t + 1)
                        nc.scalar.copy(xTs[j][:], ps_x[j][:, 0:P]).then_inc(s_xT, 1)
                act.wait_ge(s_dl, 1)
                nc.scalar.activation(dl[:], dl[:], ACT.Exp).then_inc(s_exp, 1)

            @block.tensor
            def _(pe):
                for s in (s_xT_ps, s_logit, s_copy):
                    pe.sem_inc(s, TRIO)
                pe.wait_ge(s_w, 16 * 6)
                with pe.Fori(0, TRIOS) as i:
                    for j in range(TRIO):
                        t = i * TRIO + j
                        pe.wait_ge(s_xs, t + 1)
                        pe.wait_ge(s_xT, t + 1)
                        nc.tensor.transpose(ps_x[j][:, 0:P], xs[j][:], ident[:]).then_inc(s_xT_ps, 1)
                    for j in range(TRIO):
                        t = i * TRIO + j
                        pe.wait_ge(s_xT, t + TRIO + 1)
                        nc.tensor.matmul(ps_l[:, ds(t * EXPERTS, EXPERTS)], xTs[j][:], router[:],
                                         start=True, stop=True).then_inc(s_logit, 1)

        with ExitStack() as main:
            ps_h1 = [main.enter_context(nc.psum_tensor(f"ex_ps_h1{j}", [P, 512], F32)) for j in range(HC)]
            ps_h2 = [main.enter_context(nc.psum_tensor(f"ex_ps_h2{j}", [P, 512], F32)) for j in range(HC)]
            ps_y = [main.enter_context(nc.psum_tensor(f"ex_ps_y{b}", [P, 512], F32)) for b in range(2)]
            ps_bias = main.enter_context(nc.psum_tensor("ex_ps_bias", [P, 512], F32))
            ps_cw = main.enter_context(nc.psum_tensor("ex_ps_cw", [P, 512], F32))
            W = TRIO * P
            compact = main.enter_context(nc.sbuf_tensor("ex_tables_compact", [P, SPLINES * 2 * QS], F32))
            rest = main.enter_context(nc.sbuf_tensor("ex_tables_rest", [P, SPLINES * 2 * QS], F32))
            parts = main.enter_context(nc.sbuf_tensor("ex_tables_parts", [P, PARTS, SPLINES * 2 * QS], BF16))
            unit_mask = main.enter_context(nc.sbuf_tensor("ex_unit_mask", [P, HG], F32))
            s_tables = main.enter_context(nc.semaphore("ex_tables_loaded"))
            s_spread = main.enter_context(nc.semaphore("ex_tables_spread"))
            s_tchain = main.enter_context(nc.semaphore("ex_tables_chain"))
            block = main.enter_context(nc.Block())

            @block.sync
            def _(sp):
                sp.dma_start(compact[:], a["spline_tables"]).then_inc(s_tables, 16)

            @block.gpsimd
            def _(pool):
                ch = Chain(pool, s_tchain)
                ch.step(pool.memset(unit_mask[:], 1.0))
                ch.step(pool.affine_select(out=unit_mask[:], in_=unit_mask[:], compare_op=ALU.is_ge, fill=0.0,
                                           base=0, pattern=[[-GRID, HG]], channel_multiplier=1))
                ch.step(pool.affine_select(out=unit_mask[:], in_=unit_mask[:], compare_op=ALU.is_ge, fill=0.0,
                                           base=GRID - 1, pattern=[[GRID, HG]], channel_multiplier=-1))
                spread_tables(pool, ch, compact, parts, rest, unit_mask, tables, s_spread, s_tables)

            @block.vector
            def _(dve):
                ch = Chain(dve, s_sum)
                dve.sem_inc(s_acc, 2)
                dve.sem_inc(s_a, HC)
                dve.sem_inc(s_init, 1)
                with dve.Fori(0, TRIOS) as i:
                    ch.enter(i, 2 * EXPERTS + 1)

                    def activated(e, j):
                        m = e * HC + j
                        dve.wait_ge(s_gate, i * STEPS + m + 1)
                        dve.wait_ge(s_h2, i * STEPS + m + 1)
                        dve.scalar_tensor_tensor(out=act_t[e % 2][j][:], in0=ps_h2[j][:, 0:W],
                                                 scalar=b1[:, e, HC + j:HC + j + 1], in1=gate[j][:],
                                                 op0=ALU.add, op1=ALU.mult).then_inc(s_a, 1)

                    def accumulate(e):
                        dve.wait_ge(s_y, i * EXPERTS + e + 1)
                        dve.wait_ge(s_acc, i * EXPERTS + e + 2)
                        ch.sync()
                        for s in range(TRIO):
                            out = acc[:, s, :] if e < EXPERTS - 1 else resid[:, i * TRIO + s, :]
                            ins = dve.scalar_tensor_tensor(out=out, in0=ps_y[e % 2][:, s * D:(s + 1) * D],
                                                           scalar=cws[:, s, e:e + 1], in1=acc[:, s, :],
                                                           op0=ALU.mult, op1=ALU.add)
                            if s < TRIO - 1:
                                ch.mark(ins)
                        ins.then_inc(s_acc, 1)

                    dve.wait_ge(s_acc, i * EXPERTS + 2)
                    dve.tensor_copy(cws[:], cw[:, ds(i * TRIO, TRIO), :]).then_inc(s_cws, 1)
                    activated(0, 0)
                    activated(0, 1)
                    activated(1, 0)
                    activated(1, 1)
                    dve.wait_ge(s_bias, i + 1)
                    dve.wait_ge(s_cws, i + 1)
                    ch.mark(dve.tensor_tensor(acc[:], ps_bias[:, 0:TRIO * D].rearrange("p (s d) -> p s d", s=TRIO),
                                              resid[:, ds(i * TRIO, TRIO), :], ALU.add))
                    ch.sync()
                    dve.sem_inc(s_init, 1)
                    for e in range(EXPERTS):
                        if e >= 1 and e + 1 < EXPERTS:
                            activated(e + 1, 0)
                            activated(e + 1, 1)
                        accumulate(e)
                    ch.leave(TRIOS)

            @block.scalar
            def _(act):
                act.sem_inc(s_cwT, 1)
                with act.Fori(0, TRIOS) as i:
                    for e in range(EXPERTS):
                        for j in range(HC):
                            m = e * HC + j
                            act.wait_ge(s_h1, i * STEPS + m + 1)
                            act.wait_ge(s_a, i * STEPS + m + 1)
                            nc.scalar.activation(gate[j][:], ps_h1[j][:, 0:W], ACT.Silu,
                                                 bias=b1[:, e, j:j + 1]).then_inc(s_gate, 1)
                        if e == 0:
                            act.wait_ge(s_cwT_ps, i + 1)
                            nc.scalar.copy(cwT[0:EXPERTS, :], ps_cw[0:EXPERTS, 0:W]).then_inc(s_cwT, 1)

            @block.tensor
            def _(pe):
                with pe.Fori(0, TRIOS) as i:
                    x = xT[:, ds(i * W, W)]

                    def hidden(e):
                        for j in range(HC):
                            pe.wait_ge(s_a, i * STEPS + e * HC + j + 1)
                            nc.tensor.matmul(ps_h1[j][:, 0:W], fc1[:, e, j * P:(j + 1) * P], x,
                                             start=True, stop=True).then_inc(s_h1, 1)
                            nc.tensor.matmul(ps_h2[j][:, 0:W], fc1[:, e, HIDDEN + j * P:HIDDEN + (j + 1) * P], x,
                                             start=True, stop=True).then_inc(s_h2, 1)

                    def outputs(e):
                        pe.wait_ge(s_a, i * STEPS + e * HC + HC + HC)
                        pe.wait_ge(s_acc, i * EXPERTS + e + 1)
                        for s in range(TRIO):
                            for j in range(HC):
                                mm = nc.tensor.matmul(ps_y[e % 2][:, s * D:(s + 1) * D],
                                                      act_t[e % 2][j][:, s * P:(s + 1) * P], fc2[:, e, j, :],
                                                      start=(j == 0), stop=(j == HC - 1))
                        mm.then_inc(s_y, 1)

                    hidden(0)
                    pe.wait_ge(s_cws, i + 1)
                    pe.wait_ge(s_cwT, i + 1)
                    for s in range(TRIO):
                        mm = nc.tensor.transpose(ps_cw[0:EXPERTS, s * P:(s + 1) * P], cws[:, s, :], ident[:])
                    mm.then_inc(s_cwT_ps, 1)
                    hidden(1)
                    pe.wait_ge(s_cwT, i + 2)
                    pe.wait_ge(s_init, i + 1)
                    for s in range(TRIO):
                        mm = nc.tensor.matmul(ps_bias[:, s * D:(s + 1) * D], cwT[0:EXPERTS, s * P:(s + 1) * P],
                                              b2[0:EXPERTS, :], start=True, stop=True)
                    mm.then_inc(s_bias, 1)
                    for e in range(EXPERTS):
                        if e >= 1 and e + 1 < EXPERTS:
                            hidden(e + 1)
                        outputs(e)


def attention(nc, resid, ident, a):
    with ExitStack() as ctx:
        def sb(name, shape, dt=F32):
            return ctx.enter_context(nc.sbuf_tensor(name, shape, dt))

        def sem(name):
            return ctx.enter_context(nc.semaphore(name))

        def psum(name):
            return ctx.enter_context(nc.psum_tensor(name, [P, 512], F32))

        ps_x, ps_q, ps_k, ps_v, ps_s, ps_pt, ps_o, ps_c = (
            psum(f"at_ps_{n}") for n in ("x", "q", "k", "v", "scores", "probsT", "o", "cls"))
        w_qkv = sb("at_w_qkv", [P, 3, D])
        stats = sb("at_stats", [P, TILES, 6])
        mean, var, veps, newton, rstd, minus_half, t0, t1 = (
            sb(f"at_{n}", [P, TILES]) for n in ("mean", "var", "veps", "newton", "rstd", "minus_half", "t0", "t1"))
        xs = sb("at_xs", [P, GT, D])
        xT_cls = sb("at_xT_cls", [P, IMAGES, CLS])
        xT = sb("at_xT", [P, GROUP, SEQ])
        qT = sb("at_qT", [P, GROUP, SEQ])
        kT = sb("at_kT", [P, GROUP, SEQ])
        v = sb("at_v", [P, GROUP, D])
        top, rsum = sb("at_top", [P, GROUP]), sb("at_rsum", [P, GROUP])
        probs = sb("at_probs", [P, GROUP, SEQ])
        probsT = sb("at_probsT", [P, GROUP, SEQ])
        o_cls = sb("at_o_cls", [P, IMAGES, D])
        o_cls_rows = sb("at_o_cls_rows", [P, D])

        s_w = sem("at_weights")
        s_dve = sem("at_dve_chain")
        s_pool = sem("at_pool_chain")
        s_turns = [sem(f"at_turns{e}") for e in range(2)]
        s_stats = sem("at_stats_ready")
        s_rstd = sem("at_rstd_ready")
        s_xs = sem("at_xs_ready")
        s_xT_ps = sem("at_xT_in_psum")
        s_xT = sem("at_xT_ready")
        s_xc = sem("at_xT_cls_ready")
        s_q_ps = sem("at_q_in_psum")
        s_k_ps = sem("at_k_in_psum")
        s_v_ps = sem("at_v_in_psum")
        s_q = sem("at_q_ready")
        s_k = sem("at_k_ready")
        s_v = sem("at_v_ready")
        s_s = sem("at_scores_ready")
        s_sub = sem("at_scores_taken")
        s_e = sem("at_exp_ready")
        s_p = sem("at_probs_ready")
        s_pT_ps = sem("at_probsT_in_psum")
        s_pT = sem("at_probsT_ready")
        s_o = sem("at_o_in_psum")
        s_h = sem("at_o_taken")
        s_c = sem("at_o_cls_taken")
        s_rows = sem("at_o_cls_rows_moved")

        def images(ps, rows=P):
            return ps[0:rows, 0:GROUP * SEQ].rearrange("p (i s) -> p i s", i=GROUP)

        LAST = GROUPS - 1
        block = ctx.enter_context(nc.Block())

        @block.sync
        def _(sp):
            sp.dma_start(w_qkv[:], a["w_qkv"]).then_inc(s_w, 16)
            sp.wait_ge(s_c, GROUPS + 1)
            for c in range(CLS):
                sp.dma_start(o_cls_rows[c::CLS, :], o_cls[c:c + 1, :, :]).then_inc(s_rows, 16)

        @block.gpsimd
        def _(pool):
            ch = Chain(pool, s_pool, s_turns[0])
            ch.step(pool.memset(minus_half[:], -0.5))
            pool.wait_ge(s_stats, 1)
            rsqrt_steps(pool, ch, var[:], minus_half[:], veps[:], newton[:], rstd[:]).then_inc(s_rstd, 1)
            pool.wait_ge(s_xT, 1)
            with pool.Fori(0, GROUPS) as g:
                pool.wait_ge(s_v_ps, g + 1)
                pool.tensor_copy(xT[:, :, 0:CLS], xT_cls[:, ds(g * GROUP, GROUP), :]).then_inc(s_xc, 1)

        @block.vector
        def _(dve):
            ch = Chain(dve, s_dve, s_turns[1])
            norm_statistics(dve, ch, resid, stats, mean[:], var[:], (t0[:], t1[:])).then_inc(s_stats, 1)
            dve.wait_ge(s_rstd, 1)

            def normalise(slot, tile):
                return dve.tensor_scalar(xs[:, slot, :], resid[:, tile, :], mean[:, ds(tile, 1)], rstd[:, ds(tile, 1)],
                                         ALU.subtract, ALU.mult)

            def normalise_group(g):
                dve.wait_ge(s_xT_ps, g + 1)
                for t in range(GT - 1):
                    ch.mark(normalise(t, g * GT + t))
                ch.sync()
                normalise(GT - 1, g * GT + GT - 1).then_inc(s_xs, 1)

            def keep_values(g):
                dve.wait_ge(s_v_ps, g + 2)
                dve.tensor_copy(v[0:SEQ],
                                ps_v[0:SEQ, :].rearrange("p (i d) -> p i d", i=GROUP)).then_inc(s_v, 1)

            def wide(x):
                return x[0:SEQ, :, None].to_broadcast([SEQ, GROUP, SEQ])

            def group(g, more):
                if more:
                    normalise_group(g + 1)
                dve.wait_ge(s_s, g + 1)
                ch.step(dve.tensor_reduce(top[0:SEQ, :], images(ps_s, SEQ), AX_X, ALU.max))
                dve.tensor_tensor(probs[0:SEQ], images(ps_s, SEQ), wide(top), ALU.subtract).then_inc(s_sub, 1)
                dve.wait_ge(s_e, g + 1)
                ch.step(dve.tensor_reduce(rsum[0:SEQ, :], probs[0:SEQ], AX_X, ALU.add))
                ch.step(dve.reciprocal(rsum[0:SEQ, :], rsum[0:SEQ, :]))
                dve.tensor_tensor(probs[0:SEQ], probs[0:SEQ], wide(rsum), ALU.mult).then_inc(s_p, 1)
                dve.wait_ge(s_o, g + 1)
                tiles = resid[:, ds(g * GT, GT), :]
                dve.tensor_tensor(tiles, tiles, ps_o[:, 0:GT * D].rearrange("p (t d) -> p t d", t=GT),
                                  ALU.add).then_inc(s_h, 1)
                if more:
                    keep_values(g + 1)

            normalise(0, PTILES).then_inc(s_xs, 1)
            normalise_group(0)
            keep_values(0)
            with dve.Fori(0, LAST) as g:
                ch.enter(g, 3 + GT - 1)
                group(g, True)
                ch.leave(LAST)
            group(LAST, False)
            dve.wait_ge(s_rows, 16 * CLS)
            dve.tensor_tensor(resid[:, PTILES, :], resid[:, PTILES, :], o_cls_rows[:], ALU.add)

        @block.scalar
        def _(act):
            def project(g):
                act.wait_ge(s_xT_ps, g + 2)
                nc.scalar.copy(xT[:, :, CLS:SEQ], ps_x[:, 0:GT * P].rearrange("p (i s) -> p i s", i=GROUP))\
                    .then_inc(s_xT, 1)
                act.wait_ge(s_q_ps, g + 1)
                nc.scalar.copy(qT[:], images(ps_q)).then_inc(s_q, 1)
                act.wait_ge(s_k_ps, g + 1)
                nc.scalar.copy(kT[:], images(ps_k)).then_inc(s_k, 1)

            def group(g, more):
                act.wait_ge(s_sub, g + 2)
                nc.scalar.activation(probs[0:SEQ], probs[0:SEQ], ACT.Exp, scale=1.0 / D ** 0.5).then_inc(s_e, 1)
                if more:
                    project(g + 1)
                act.wait_ge(s_pT_ps, g + 1)
                nc.scalar.copy(probsT[0:SEQ], images(ps_pt, SEQ)).then_inc(s_pT, 1)
                act.wait_ge(s_o, g + 1)
                nc.scalar.copy(o_cls[0:CLS, ds(g * GROUP, GROUP), :],
                               ps_c[0:CLS, :].rearrange("p (i d) -> p i d", i=GROUP)).then_inc(s_c, 1)

            act.wait_ge(s_xT_ps, 1)
            nc.scalar.copy(xT_cls[:].rearrange("p i c -> p (i c)"), ps_x[:, 0:P]).then_inc(s_xT, 1)
            project(0)
            with act.Fori(0, LAST) as g:
                group(g, True)
            group(LAST, False)

        @block.tensor
        def _(pe):
            def project(g):
                pe.wait_ge(s_xs, g + 2)
                pe.wait_ge(s_xT, g + 1)
                for t in range(GT):
                    mm = nc.tensor.transpose(ps_x[:, t * P:(t + 1) * P], xs[:, t, :], ident[:])
                mm.then_inc(s_xT_ps, 1)
                pe.wait_ge(s_xT, g + 2)
                pe.wait_ge(s_xc, g + 1)
                pe.wait_ge(s_q, g + 1)
                nc.tensor.matmul(images(ps_q), w_qkv[:, 0, :], xT[:], start=True, stop=True).then_inc(s_q_ps, 1)
                pe.wait_ge(s_k, g + 1)
                nc.tensor.matmul(images(ps_k), w_qkv[:, 1, :], xT[:], start=True, stop=True).then_inc(s_k_ps, 1)
                pe.wait_ge(s_v, g + 1)
                for i in range(GROUP):
                    mm = nc.tensor.matmul(ps_v[0:SEQ, i * D:(i + 1) * D], xT[:, i, :], w_qkv[:, 2, :],
                                          start=True, stop=True)
                mm.then_inc(s_v_ps, 1)

            def group(g, more):
                pe.wait_ge(s_q, g + 2)
                pe.wait_ge(s_k, g + 2)
                pe.wait_ge(s_sub, g + 1)
                for i in range(GROUP):
                    mm = nc.tensor.matmul(images(ps_s, SEQ)[:, i, :], qT[:, i, :], kT[:, i, :], start=True, stop=True)
                mm.then_inc(s_s, 1)
                if more:
                    project(g + 1)
                pe.wait_ge(s_p, g + 1)
                pe.wait_ge(s_pT, g + 1)
                for i in range(GROUP):
                    mm = nc.tensor.transpose(images(ps_pt, SEQ)[:, i, :], probs[0:SEQ, i, :], ident[0:SEQ, 0:SEQ])
                mm.then_inc(s_pT_ps, 1)
                pe.wait_ge(s_pT, g + 2)
                pe.wait_ge(s_v, g + 2)
                pe.wait_ge(s_h, g + 1)
                pe.wait_ge(s_c, g + 1)
                for i in range(GROUP):
                    values = v[0:SEQ, i, :]
                    rows = (i % 2) * PATCHES
                    nc.tensor.matmul(ps_o[rows:rows + PATCHES, (i // 2) * D:(i // 2 + 1) * D],
                                     probsT[0:SEQ, i, CLS:SEQ], values, start=True, stop=True)
                    mm = nc.tensor.matmul(ps_c[0:CLS, i * D:(i + 1) * D], probsT[0:SEQ, i, 0:CLS], values,
                                          start=True, stop=True)
                mm.then_inc(s_o, 1)

            for s in (s_v_ps, s_q, s_k, s_v, s_sub, s_pT, s_h, s_c):
                pe.sem_inc(s, 1)
            pe.wait_ge(s_w, 16)
            pe.wait_ge(s_xs, 1)
            nc.tensor.transpose(ps_x[:, 0:P], xs[:, 0, :], ident[:]).then_inc(s_xT_ps, 1)
            project(0)
            with pe.Fori(0, LAST) as g:
                group(g, True)
            group(LAST, False)


SPLINES, CLUSTERS, PER_CLUSTER, GRID = 64, 8, 8, 16
BLOCK = 64
MAX_BLOCKS = (TILES * P + SPLINES * (BLOCK - 1)) // BLOCK
RING = 5
PAIRS = -(-MAX_BLOCKS // (2 * RING)) * RING
ROWS = PAIRS * 2 * BLOCK
HG = P // GRID
QS = P // HG
PARTS = 3


def spread_tables(pool, ch, compact, hi_lo, rest, unit_mask, tables, s_tab, tables_loaded):
    pool.wait_ge(tables_loaded, 16)
    ch.step(pool.tensor_copy(hi_lo[:, 0, :], compact[:]))
    for n in range(1, PARTS):
        ch.step(pool.tensor_tensor(rest[:], compact[:] if n == 1 else rest[:], hi_lo[:, n - 1, :], ALU.subtract))
        ch.step(pool.tensor_copy(hi_lo[:, n, :], rest[:]))
    with pool.Fori(0, SPLINES) as t:
        for n in range(PARTS):
            pool.tensor_tensor(tables[:, t, :, n, :, :],
                               hi_lo[:, n, ds(t * 2 * QS, 2 * QS)].rearrange("p (q c) -> p q c", c=2)[:, :, :, None]
                               .to_broadcast([P, QS, 2, HG]),
                               unit_mask[:, None, None, :].to_broadcast([P, QS, 2, HG]), ALU.mult).then_inc(s_tab, 1)


def splines(nc, resid, ident, a, scratch, out, spread):
    x_rows, y_rows, s_zeroed = scratch
    with ExitStack() as ctx:
        def sb(name, shape, dt=F32):
            return ctx.enter_context(nc.sbuf_tensor(name, shape, dt))

        def sem(name):
            return ctx.enter_context(nc.semaphore(name))

        gb_cols = sb("sp_gamma_beta", [P, 2])
        dest_i = sb("sp_dest_int", [P, TILES], U32)
        tile_of = sb("sp_tile_of_block", [P, 2 * P], I32)
        s_w = sem("sp_weights")
        s_dve = sem("sp_dve_chain")
        s_pool = sem("sp_pool_chain")
        s_turns = [sem(f"sp_turns{e}") for e in range(2)]
        s_scat = sem("sp_scattered")

        with ExitStack() as prep:
            def sb(name, shape, dt=F32):
                return prep.enter_context(nc.sbuf_tensor(name, shape, dt))

            ps_x = [prep.enter_context(nc.psum_tensor(f"sp_ps_x{j}", [P, 512], F32)) for j in range(TRIO)]
            ps_r = prep.enter_context(nc.psum_tensor("sp_ps_rank", [P, 5, 512], F32))
            wd = sb("sp_wd", [P, SPLINES // 2, P])
            wd_sum = sb("sp_wd_sum", [P, SPLINES])
            pos_part, cl_sum = sb("sp_positive", [P, SPLINES]), sb("sp_cluster_sum", [P, CLUSTERS])
            sigs = sb("sp_signatures", [P, SPLINES + CLUSTERS], BF16)
            sig_f = sb("sp_signatures_f", [P, SPLINES + CLUSTERS])
            stats = sb("sp_stats", [P, TILES, 6])
            mean, var, veps, newton, rstd, minus_half, t0, t1 = (
                sb(f"sp_{n}", [P, TILES]) for n in ("mean", "var", "veps", "newton", "rstd", "minus_half", "t0", "t1"))
            xs = [sb(f"sp_xs{j}", [P, D]) for j in range(TRIO)]
            xn = sb("sp_xn", [P, TILES, D])
            signs = [sb(f"sp_signs{j}", [P, P], BF16) for j in range(TRIO)]
            score = sb("sp_score", [P, TILES, SPLINES + CLUSTERS])
            c_index, l_index = sb("sp_cluster_index", [P, CLUSTERS]), sb("sp_local_index", [P, CLUSTERS, PER_CLUSTER])
            c_key, t_key = sb("sp_cluster_key", [P, TILES, CLUSTERS]), sb("sp_tile_key", [P, TILES, SPLINES])
            c_max, t_max = sb("sp_cluster_max", [P, TILES]), sb("sp_tile_max", [P, TILES])
            chosen = sb("sp_chosen", [P, TILES, SPLINES], BF16)
            before = sb("sp_before", [P, TILES + 1, SPLINES], BF16)
            below, ones = sb("sp_below", [P, P], BF16), sb("sp_ones", [P, P], BF16)
            count, whole, ends, starts = (sb(f"sp_{n}", [P, SPLINES]) for n in ("count", "whole", "ends", "starts"))
            count_i = sb("sp_count_int", [P, SPLINES], I32)
            zero64 = sb("sp_zero64", [P, SPLINES])
            rank = sb("sp_rank", [P, TILES, SPLINES])
            dest = sb("sp_dest", [P, TILES])
            first_row = sb("sp_first_row", [P, 2])
            past = sb("sp_past", [P, 2, SPLINES])
            block_tile = sb("sp_block_tile", [P, 2])

            def psem(name):
                return prep.enter_context(nc.semaphore(name))

            s_wd = [psem(f"sp_wd_loaded{n}") for n in range(2)]
            s_wdfree = psem("sp_wd_used")
            s_const = psem("sp_constants")
            s_stats = psem("sp_stats_ready")
            s_rstd = psem("sp_rstd_ready")
            s_normed = psem("sp_stream_normed")
            s_sigs = psem("sp_signatures_ready")
            s_xs = psem("sp_xs_ready")
            s_xT_ps = psem("sp_xT_in_psum")
            s_sign = psem("sp_signs_ready")
            s_copy = psem("sp_xn_kept")
            s_score = psem("sp_scores_in_psum")
            s_taken = psem("sp_scores_taken")
            s_chosen = psem("sp_chosen_ready")
            s_before = psem("sp_before_ready")
            s_rank = psem("sp_rank_in_psum")
            s_bt = psem("sp_block_tile_ready")
            s_bt_ps = psem("sp_block_tile_in_psum")
            s_dest = psem("sp_dest_ready")
            block = prep.enter_context(nc.Block())
            CH = 8
            ps_s = [ps_r[:, j, 0:SPLINES + CLUSTERS] for j in range(TRIO)]

            @block.sync
            def _(sp):
                sp.dma_start(gb_cols[:], a["gamma_beta"]).then_inc(s_w, 16)
                sp.dma_start(wd[:], a["wd_sums"][:, 0:SPLINES // 2, :]).then_inc(s_wd[0], 16)
                sp.wait_ge(s_wdfree, 1)
                sp.dma_start(wd[:], a["wd_sums"][:, SPLINES // 2:SPLINES, :]).then_inc(s_wd[1], 16)

            @block.gpsimd
            def _(pool):
                ch = Chain(pool, s_pool, s_turns[0])
                ch.mark(pool.memset(below[:], 1.0))
                ch.mark(pool.memset(minus_half[:], -0.5))
                pool.memset(ones[:], 1.0).then_inc(s_const, 1)
                pool.memset(before[:, 0, :], 0.0).then_inc(s_const, 1)
                pool.memset(zero64[:], 0.0).then_inc(s_const, 1)
                ch.sync()
                pool.affine_select(out=below[:], in_=below[:], compare_op=ALU.is_ge, fill=0.0, base=-1,
                                   pattern=[[1, P]], channel_multiplier=-1).then_inc(s_const, 1)
                pool.iota(c_index[:], pattern=[[1, CLUSTERS]], base=0, channel_multiplier=0,
                          allow_small_or_imprecise_dtypes=True).then_inc(s_const, 1)
                pool.iota(l_index[:], pattern=[[0, CLUSTERS], [1, PER_CLUSTER]], base=0, channel_multiplier=0,
                          allow_small_or_imprecise_dtypes=True).then_inc(s_const, 1)
                pool.iota(first_row[:], pattern=[[P * BLOCK, 2]], base=0, channel_multiplier=BLOCK,
                          allow_small_or_imprecise_dtypes=True).then_inc(s_const, 1)
                pool.wait_ge(s_stats, 1)
                rsqrt_steps(pool, ch, var[:], minus_half[:], veps[:], newton[:], rstd[:]).then_inc(s_rstd, 1)
                pool.wait_ge(s_normed, 1)
                ch.step(pool.tensor_tensor(resid[:], resid[:], xn[:], ALU.add))
                pool.wait_ge(s_stats, 2)
                rsqrt_steps(pool, ch, var[:], minus_half[:], veps[:], newton[:], rstd[:]).then_inc(s_rstd, 1)
                with pool.Fori(0, TRIOS) as i:
                    for j in range(TRIO):
                        t = i * TRIO + j
                        pool.wait_ge(s_xs, t + 1)
                        pool.tensor_copy(xn[:, t, :], xs[j][:]).then_inc(s_copy, 1)
                pool.wait_ge(s_dest, 1)
                pool.wait_ge(s_copy, TILES + TRIO)
                pool.wait_ge(s_zeroed, 16)
                for t in range(TILES):
                    pool.indirect_dma_start(out=x_rows, out_offset=bass.IndirectOffsetOnAxis(ap=dest_i[:, t:t + 1], axis=0),
                                            in_=xn[:, t, :], in_offset=None).then_inc(s_scat, 16)
                pool.wait_ge(s_scat, 16 * TILES)

            @block.vector
            def _(dve):
                ch = Chain(dve, s_dve, s_turns[1])
                norm_statistics(dve, ch, resid, stats, mean[:], var[:], (t0[:], t1[:])).then_inc(s_stats, 1)
                half = SPLINES // 2
                dve.wait_ge(s_wd[0], 16)
                dve.tensor_reduce(wd_sum[:, 0:half], wd[:], AX_X, ALU.add).then_inc(s_wdfree, 1)
                dve.wait_ge(s_wd[1], 16)
                ch.step(dve.tensor_reduce(wd_sum[:, half:SPLINES], wd[:], AX_X, ALU.add))
                dve.wait_ge(s_wdfree, 1)
                for src, n, at in ((wd_sum, SPLINES, 0), (cl_sum, CLUSTERS, SPLINES)):
                    ch.step(dve.tensor_scalar(pos_part[:, 0:n], src[:], 0.0, None, ALU.is_gt))
                    ch.step(dve.scalar_tensor_tensor(out=sig_f[:, at:at + n], in0=src[:], scalar=0.0,
                                                     in1=pos_part[:, 0:n], op0=ALU.is_lt, op1=ALU.subtract))
                    ch.step(dve.tensor_scalar(sig_f[:, at:at + n], sig_f[:, at:at + n], -1.0, None, ALU.mult))
                    if at == 0:
                        ch.step(dve.tensor_reduce(cl_sum[:], sig_f[:, 0:SPLINES].rearrange("p (c l) -> p c l", c=CLUSTERS),
                                                  AX_X, ALU.add))
                dve.tensor_copy(sigs[:], sig_f[:]).then_inc(s_sigs, 1)
                dve.wait_ge(s_rstd, 1)
                ch.step(dve.tensor_tensor(xn[:], resid[:], mean[:, :, None].to_broadcast([P, TILES, D]), ALU.subtract))
                ch.mark(dve.tensor_tensor(xn[:], xn[:], rstd[:, :, None].to_broadcast([P, TILES, D]), ALU.mult))
                ch.sync()
                dve.sem_inc(s_normed, 1)
                norm_statistics(dve, ch, xn, stats, mean[:], var[:], (t0[:], t1[:])).then_inc(s_stats, 1)
                dve.wait_ge(s_rstd, 2)
                with dve.Fori(0, TRIOS) as i:
                    for j in range(TRIO):
                        t = i * TRIO + j
                        dve.wait_ge(s_xT_ps, t + 1)
                        dve.wait_ge(s_copy, t + 1)
                        dve.tensor_scalar(xs[j][:], xn[:, t, :], mean[:, ds(t, 1)], rstd[:, ds(t, 1)],
                                          ALU.subtract, ALU.mult).then_inc(s_xs, 1)
                    for j in range(TRIO):
                        t = i * TRIO + j
                        dve.wait_ge(s_score, t + TRIO + 1)
                        dve.tensor_copy(score[:, t, :], ps_s[j]).then_inc(s_taken, 1)
                dve.wait_ge(s_taken, TILES + TRIO)
                dve.wait_ge(s_const, 7)
                tiles_s = score[:, :, 0:SPLINES]
                ch.step(dve.scalar_tensor_tensor(out=c_key[:], in0=score[:, :, SPLINES:], scalar=float(CLUSTERS),
                                                 in1=c_index[:, None, :].to_broadcast([P, TILES, CLUSTERS]),
                                                 op0=ALU.mult, op1=ALU.subtract))
                ch.step(dve.tensor_reduce(c_max[:], c_key[:], AX_X, ALU.max))
                ch.mark(dve.tensor_tensor(c_key[:], c_key[:], c_max[:, :, None].to_broadcast([P, TILES, CLUSTERS]),
                                          ALU.is_equal))
                ch.step(dve.scalar_tensor_tensor(out=t_key[:], in0=tiles_s, scalar=float(PER_CLUSTER),
                                                 in1=l_index[:].rearrange("p c l -> p (c l)")[:, None, :]
                                                 .to_broadcast([P, TILES, SPLINES]),
                                                 op0=ALU.mult, op1=ALU.subtract))
                keys = t_key[:].rearrange("p t (c l) -> p (t c) l", l=PER_CLUSTER)
                ch.step(dve.scalar_tensor_tensor(out=keys, in0=c_key[:].rearrange("p t c -> p (t c)")[:, :, None]
                                                 .to_broadcast([P, TILES * CLUSTERS, PER_CLUSTER]), scalar=4096.0,
                                                 in1=keys, op0=ALU.mult, op1=ALU.add))
                ch.step(dve.tensor_reduce(t_max[:], t_key[:], AX_X, ALU.max))
                dve.tensor_tensor(chosen[:], t_key[:], t_max[:, :, None].to_broadcast([P, TILES, SPLINES]),
                                  ALU.is_equal).then_inc(s_chosen, 1)
                dve.wait_ge(s_chosen, 1)
                with dve.Fori(0, TILES) as t:
                    ch.enter(t, 1)
                    ch.step(dve.tensor_tensor(before[:, t + 1, :], before[:, t, :], chosen[:, t, :], ALU.add))
                    ch.leave(TILES)
                dve.sem_inc(s_before, 1)
                dve.wait_ge(s_rank, 1)
                ch.step(dve.tensor_scalar(count_i[:], ps_x[0][:, 0:SPLINES], float(BLOCK - 1), None, ALU.add))
                ch.step(dve.tensor_scalar(count_i[:], count_i[:], -BLOCK, None, ALU.bitwise_and))
                ch.step(dve.tensor_copy(whole[:], count_i[:]))
                ch.step(dve.tensor_tensor_scan(ends[:], whole[:], zero64[:], 0.0, ALU.add, ALU.add))
                ch.mark(dve.tensor_tensor(starts[:], ends[:], whole[:], ALU.subtract))
                ch.step(dve.tensor_tensor(past[:], ends[:, None, :].to_broadcast([P, 2, SPLINES]),
                                          first_row[:, :, None].to_broadcast([P, 2, SPLINES]), ALU.is_le))
                ch.step(dve.tensor_reduce(block_tile[:], past[:], AX_X, ALU.add))
                dve.tensor_scalar(block_tile[:], block_tile[:], float(SPLINES - 1), None, ALU.min).then_inc(s_bt, 1)
                for c in range(5):
                    n = min(CH, TILES - c * CH)
                    dve.wait_ge(s_rank, c + 2)
                    ch.mark(dve.tensor_tensor(rank[:, c * CH:c * CH + n, :],
                                              ps_r[:, c, 0:n * SPLINES].rearrange("p (t s) -> p t s", t=n),
                                              starts[:, None, :].to_broadcast([P, n, SPLINES]), ALU.add))
                ch.sync()
                ch.step(dve.tensor_tensor(rank[:], rank[:], chosen[:], ALU.mult))
                ch.step(dve.tensor_reduce(dest[:], rank[:], AX_X, ALU.add))
                dve.tensor_copy(dest_i[:], dest[:]).then_inc(s_dest, 1)
                dve.wait_ge(s_bt_ps, 1)
                dve.tensor_copy(tile_of[0:1, :], ps_x[1][0:1, 0:2 * P])

            @block.scalar
            def _(act):
                act.sem_inc(s_sign, TRIO)
                act.wait_ge(s_w, 16)
                with act.Fori(0, TRIOS) as i:
                    for j in range(TRIO):
                        t = i * TRIO + j
                        act.wait_ge(s_xT_ps, t + TRIO + 1)
                        act.wait_ge(s_score, t + 1)
                        nc.scalar.activation(signs[j][:], ps_x[j][:, 0:P], ACT.Sign, bias=gb_cols[:, 1:2],
                                             scale=gb_cols[:, 0:1]).then_inc(s_sign, 1)

            @block.tensor
            def _(pe):
                for s in (s_xT_ps, s_copy, s_score, s_taken):
                    pe.sem_inc(s, TRIO)
                pe.wait_ge(s_sigs, 1)
                with pe.Fori(0, TRIOS) as i:
                    for j in range(TRIO):
                        t = i * TRIO + j
                        pe.wait_ge(s_xs, t + 1)
                        pe.wait_ge(s_sign, t + 1)
                        nc.tensor.transpose(ps_x[j][:, 0:P], xs[j][:], ident[:]).then_inc(s_xT_ps, 1)
                    for j in range(TRIO):
                        t = i * TRIO + j
                        pe.wait_ge(s_sign, t + TRIO + 1)
                        pe.wait_ge(s_taken, t + 1)
                        nc.tensor.matmul(ps_s[j], signs[j][:], sigs[:], start=True, stop=True).then_inc(s_score, 1)
                pe.wait_ge(s_before, 1)
                pe.wait_ge(s_const, 7)
                pe.wait_ge(s_taken, TILES + TRIO)
                nc.tensor.matmul(ps_x[0][:, 0:SPLINES], ones[:], before[:, TILES, :], start=True, stop=True)\
                    .then_inc(s_rank, 1)
                for c in range(5):
                    n = min(CH, TILES - c * CH)
                    nc.tensor.matmul(ps_r[:, c, 0:n * SPLINES], below[:], chosen[:, c * CH:c * CH + n, :],
                                     start=True, stop=False)
                    nc.tensor.matmul(ps_r[:, c, 0:n * SPLINES], ones[:], before[:, c * CH:c * CH + n, :],
                                     start=False, stop=True).then_inc(s_rank, 1)
                pe.wait_ge(s_bt, 1)
                for c in range(2):
                    mm = nc.tensor.matmul(ps_x[1][0:1, c * P:(c + 1) * P], block_tile[:, c:c + 1], ident[:],
                                          start=True, stop=True)
                mm.then_inc(s_bt_ps, 1)

        spline_blocks(nc, resid, ident, a, scratch, spread, gb_cols, tile_of)

        with ExitStack() as last:
            got = last.enter_context(nc.sbuf_tensor("sp_gathered", [P, TILES, D], F32))
            s_got = last.enter_context(nc.semaphore("sp_rows_gathered"))
            s_sum = last.enter_context(nc.semaphore("sp_rows_added"))
            s_out = last.enter_context(nc.semaphore("sp_stored"))
            block = last.enter_context(nc.Block())

            @block.gpsimd
            def _(pool):
                for t in range(TILES):
                    pool.indirect_dma_start(out=got[:, t, :], out_offset=None, in_=y_rows,
                                            in_offset=bass.IndirectOffsetOnAxis(ap=dest_i[:, t:t + 1], axis=0))\
                        .then_inc(s_got, 16)

            cuts = [0, 8, 16, 24, TILES]

            @block.vector
            def _(dve):
                dve.wait_ge(s_got, 16 * TILES)
                for t0, t1 in zip(cuts, cuts[1:]):
                    dve.tensor_tensor(got[:, t0:t1, :], got[:, t0:t1, :], resid[:, t0:t1, :], ALU.add)\
                        .then_inc(s_sum, 1)

            @block.sync
            def _(sp):
                tiles = out.rearrange("(t i) s d -> i s t d", i=2)
                for n, (t0, t1) in enumerate(zip(cuts, cuts[1:])):
                    sp.wait_ge(s_sum, n + 1)
                    t1 = min(t1, PTILES)
                    for i in range(2):
                        sp.dma_start(tiles[i, CLS:SEQ, t0:t1, :], got[i * PATCHES:(i + 1) * PATCHES, t0:t1, :])\
                            .then_inc(s_out, 16)
                sp.dma_start(out[:, 0:CLS, :], got[:, PTILES, :]).then_inc(s_out, 16)
                sp.wait_ge(s_out, 16 * (2 * len(cuts) - 1))


def spline_blocks(nc, resid, ident, a, scratch, tables, gb_cols, tile_of):
    x_rows, y_rows, _ = scratch
    with ExitStack() as ctx:
        def sb(name, shape, dt=F32):
            return ctx.enter_context(nc.sbuf_tensor(name, shape, dt))

        def ring(name, shape, dt=F32):
            return [sb(f"bl_{name}{z}", shape, dt) for z in range(RING)]

        def sem(name):
            return ctx.enter_context(nc.semaphore(name))

        def psum(name, shape):
            return ctx.enter_context(nc.psum_tensor(name, shape, F32))

        CHUNKS = 4
        QB = QS // CHUNKS
        ps_r = psum("bl_ps_spread", [P, 2, 512])
        ps_l = psum("bl_ps_looked_up", [P, 2, 512])
        ps_x = psum("bl_ps_x", [P, 512])
        ps_h = psum("bl_ps_h", [P, 512])
        ps_t = psum("bl_ps_t", [P, 512])
        ps_y = psum("bl_ps_y", [P, 512])
        expand = sb("bl_expand", [P, QS, P], BF16)
        grid = sb("bl_grid", [P, 1])
        grid_i = sb("bl_grid_i", [P, 1], I32)
        x = ring("x", [P, D])
        w = [ring(f"w{b}_", [P, 2 * P + 2]) for b in range(2)]
        table = [ring(f"table{b}_", [P, QS, PARTS, 2 * HG], BF16) for b in range(2)]
        xT, sig, pos, posT, hs, hsT, y = (ring(n, [P, P]) for n in ("xT", "sig", "pos", "posT", "hs", "hsT", "y"))
        at = ring("at", [P, P], BF16)
        r, above, tmp = (sb(f"bl_{n}", [P, P]) for n in ("r", "above", "tmp"))
        hot = sb("bl_hot", [P, QS, P], BF16)
        looked = sb("bl_looked", [P, QS, 2, HG])

        s_const = sem("bl_constants")
        s_dve = sem("bl_dve_chain")
        s_ld = [sem(f"bl_loaded{z}") for z in range(RING)]
        s_tab = sem("bl_table_ready")
        s_xT_ps = sem("bl_xT_in_psum")
        s_xT = sem("bl_xT_ready")
        s_h = sem("bl_h_in_psum")
        s_sig = sem("bl_sigmoid_ready")
        s_at = sem("bl_cell_ready")
        s_pos = sem("bl_position_ready")
        s_r = sem("bl_spread_in_psum")
        s_hot = sem("bl_hot_ready")
        s_posT_ps = sem("bl_posT_in_psum")
        s_posT = sem("bl_posT_ready")
        s_look = sem("bl_looked_up")
        s_taken = sem("bl_looked_up_taken")
        s_hs = sem("bl_hs_ready")
        s_hsT_ps = sem("bl_hsT_in_psum")
        s_hsT = sem("bl_hsT_ready")
        s_y = sem("bl_y_in_psum")
        s_yh = [sem(f"bl_y_half_ready{b}") for b in range(2)]
        s_yev = sem("bl_y_ready")
        s_st = [sem(f"bl_stored{z}") for z in range(RING)]
        TURNS = PAIRS // RING
        MAGIC = 8388608.0
        halves = [slice(b * BLOCK, (b + 1) * BLOCK) for b in range(2)]
        block = ctx.enter_context(nc.Block())

        def in_turns(eng, step):
            step(0, lambda k: k % RING, lambda k: k // RING, False)
            with eng.Fori(0, TURNS - 1) as i:
                for j in range(1, RING + 1):
                    step(i * RING + j, lambda k, j=j: (j + k) % RING, lambda k, j=j: i + (j + k) // RING, i)
            for p in range(PAIRS - RING + 1, PAIRS):
                step(p, lambda k, p=p: (p + k) % RING, lambda k, p=p: (p + k) // RING, False)

        @block.sync
        def _(sp):
            with sp.Fori(0, TURNS) as i:
                for z in range(RING):
                    p = i * RING + z
                    ts = [sp.value_load(tile_of[0:1, ds(p * 2 + b, 1)], min_val=0, max_val=SPLINES - 1) for b in range(2)]
                    sp.wait_ge(s_yev, p + 1)
                    sp.dma_start(x[z][:], x_rows[ds(p * P, P), :]).then_inc(s_ld[z], 16)
                    for b in range(2):
                        sp.dma_start(w[b][z][:], a["spline_w"][ts[b]]).then_inc(s_ld[z], 16)

        @block.gpsimd
        def _(pool):
            pool.memset(expand[:], 1.0).then_inc(s_const, 1)
            pool.wait_ge(s_const, 1)
            pool.affine_select(out=expand[:], in_=expand[:], compare_op=ALU.is_ge, fill=0.0, base=0,
                               pattern=[[P, QS], [1, P]], channel_multiplier=-GRID).then_inc(s_const, 1)
            pool.wait_ge(s_const, 2)
            pool.affine_select(out=expand[:], in_=expand[:], compare_op=ALU.is_ge, fill=0.0, base=GRID - 1,
                               pattern=[[-P, QS], [-1, P]], channel_multiplier=GRID).then_inc(s_const, 1)
            pool.iota(grid_i[:], pattern=[[0, 1]], base=0, channel_multiplier=1).then_inc(s_const, 1)
            with pool.Fori(0, TURNS) as i:
                for z in range(RING):
                    p = i * RING + z
                    for b in range(2):
                        t = pool.value_load(tile_of[0:1, ds(p * 2 + b, 1)], min_val=0, max_val=SPLINES - 1)
                        if b == 0:
                            pool.wait_ge(s_look, p * 2 + 2)
                        pool.tensor_copy(table[b][z][:].rearrange("p q n c -> p (q n c)").bitcast(U32),
                                         tables[:, t].rearrange("p q n c u -> p (q n c u)").bitcast(U32))\
                            .then_inc(s_tab, 1)

        @block.vector
        def _(dve):
            ch = Chain(dve, s_dve)
            dve.wait_ge(s_const, 4)
            ch.step(dve.tensor_scalar(grid_i[:], grid_i[:], GRID - 1, None, ALU.bitwise_and))
            ch.step(dve.tensor_copy(grid[:], grid_i[:]))

            def positions(p, z, part):
                if part == 0:
                    dve.wait_ge(s_sig, p + 1)
                    ch.mark(dve.tensor_scalar(r[:], sig[z][:], float(GRID), MAGIC, ALU.mult, ALU.add))
                elif part == 1:
                    ch.sync()
                    ch.mark(dve.tensor_scalar(r[:], r[:], MAGIC, float(GRID - 1), ALU.subtract, ALU.min))
                elif part == 2:
                    ch.sync()
                    ch.mark(dve.scalar_tensor_tensor(out=above[:], in0=sig[z][:], scalar=float(GRID), in1=r[:],
                                                     op0=ALU.mult, op1=ALU.is_lt))
                    ch.sync()
                    dve.tensor_tensor(at[z][:], r[:], above[:], ALU.subtract).then_inc(s_at, 1)
                else:
                    dve.wait_ge(s_at, p + 1)
                    dve.scalar_tensor_tensor(out=pos[z][:], in0=sig[z][:], scalar=float(GRID), in1=at[z][:],
                                             op0=ALU.mult, op1=ALU.subtract).then_inc(s_pos, 1)

            def step(p, z, turn, i):
                more = not isinstance(p, int) or p + 1 < PAIRS
                for c in range(CHUNKS):
                    dve.wait_ge(s_r, p * CHUNKS + c + 1)
                    dve.tensor_scalar(hot[:, c * QB:(c + 1) * QB, :], ps_r[:, c % 2, :].rearrange("p (q n) -> p q n", q=QB),
                                      grid[:], None, ALU.is_equal).then_inc(s_hot, 1)
                    if more and c > 0:
                        positions(p + 1, z(1), c - 1)
                if more:
                    positions(p + 1, z(1), 3)
                for half in range(2):
                    dve.wait_ge(s_look, p * 2 + 2 * RING + half + 1)
                    ch.mark(dve.tensor_reduce(
                        looked[:, half * QS // 2:(half + 1) * QS // 2].rearrange("p q c u -> p q (c u)"),
                        ps_l[:, half, 0:QS // 2 * PARTS * 2 * HG].rearrange("p (q n k) -> p q k n", q=QS // 2, n=PARTS),
                        AX_X, ALU.add))
                ch.sync()
                dve.sem_inc(s_taken, 1)
                dve.wait_ge(s_posT, p + 1)
                ch.step(dve.tensor_tensor(tmp[:].rearrange("p (q u) -> p q u", u=HG), looked[:, :, 1, :],
                                          posT[z(0)][:].rearrange("p (q u) -> p q u", u=HG), ALU.mult))
                dve.tensor_tensor(hs[z(0)][:].rearrange("p (q u) -> p q u", u=HG), looked[:, :, 0, :],
                                  tmp[:].rearrange("p (q u) -> p q u", u=HG), ALU.add).then_inc(s_hs, 1)

            for part in range(4):
                positions(0, 0, part)
            step(0, lambda k: k, None, False)
            with dve.Fori(0, TURNS - 1) as i:
                ch.enter(i, RING * 6)
                for j in range(1, RING + 1):
                    step(i * RING + j, lambda k, j=j: (j + k) % RING, None, i)
                ch.leave(TURNS - 1)
            for p in range(PAIRS - RING + 1, PAIRS):
                step(p, lambda k, p=p: (p + k) % RING, None, False)

        @block.scalar
        def _(act):
            for z in range(RING):
                act.sem_inc(s_st[z], 16)

            def normed(p, z):
                act.wait_ge(s_xT_ps, p + 1)
                nc.scalar.activation(xT[z][:], ps_x[:, 0:P], ACT.Identity, bias=gb_cols[:, 1:2],
                                     scale=gb_cols[:, 0:1]).then_inc(s_xT, 1)

            def hidden(p, z):
                act.wait_ge(s_h, p + 1)
                nc.scalar.activation(sig[z][:], ps_h[:, 0:P], ACT.Sigmoid).then_inc(s_sig, 1)

            def finish(p, z, turn):
                act.wait_ge(s_hsT_ps, p + 1)
                nc.scalar.copy(hsT[z][:], ps_t[:, P:2 * P]).then_inc(s_hsT, 1)
                act.wait_ge(s_y, p + 1)
                act.wait_ge(s_st[z], turn * 16 + 16)
                for b in range(2):
                    nc.scalar.activation(y[z][halves[b], :], ps_y[halves[b], 0:D], ACT.Identity,
                                         scale=w[b][z][halves[b], 2 * P:2 * P + 1]).then_inc(s_yh[b], 1)
                act.wait_ge(s_yh[0], p + 1)
                act.wait_ge(s_yh[1], p + 1)
                act.sem_inc(s_yev, 1)
                act.dma_start(y_rows[ds(p * P, P), :], y[z][:]).then_inc(s_st[z], 16)

            def step(p, z, turn, i):
                known = isinstance(p, int)
                if not known or p + 1 < PAIRS:
                    hidden(p + 1, z(1))
                if not known or p + 2 < PAIRS:
                    normed(p + 2, z(2))
                if not known or p > 0:
                    finish(p - 1, z(-1), turn(-1))
                act.wait_ge(s_posT_ps, p + 1)
                nc.scalar.copy(posT[z(0)][:], ps_t[:, 0:P]).then_inc(s_posT, 1)

            normed(0, 0)
            normed(1, 1)
            hidden(0, 0)
            in_turns(act, step)
            finish(PAIRS - 1, (PAIRS - 1) % RING, (PAIRS - 1) // RING)
            for z in range(RING):
                act.wait_ge(s_st[z], 16 * (TURNS + 1))

        @block.tensor
        def _(pe):
            def transpose_x(p, z, turn):
                pe.wait_ge(s_ld[z], turn * 48 + 48)
                nc.tensor.transpose(ps_x[:, 0:P], x[z][:], ident[:]).then_inc(s_xT_ps, 1)

            def hidden(p, z):
                for b in range(2):
                    mm = nc.tensor.matmul(ps_h[:, halves[b]], w[b][z][:, 0:P], xT[z][:, halves[b]],
                                          start=True, stop=True)
                mm.then_inc(s_h, 1)

            def spread(p, z, c):
                pe.wait_ge(s_hot, p * CHUNKS + c + 1)
                for q in range(QB):
                    mm = nc.tensor.matmul(ps_r[:, c % 2, q * P:(q + 1) * P], expand[:, c * QB + q, :], at[z][:],
                                          start=True, stop=True)
                mm.then_inc(s_r, 1)

            def turn_hs(p, z):
                pe.wait_ge(s_hs, p + 1)
                nc.tensor.transpose(ps_t[:, P:2 * P], hs[z][:], ident[:]).then_inc(s_hsT_ps, 1)

            def finish(p, z):
                pe.wait_ge(s_hsT, p + 1)
                pe.wait_ge(s_yev, p + RING)
                for b in range(2):
                    mm = nc.tensor.matmul(ps_y[halves[b], 0:D], hsT[z][:, halves[b]], w[b][z][:, P:2 * P],
                                          start=True, stop=True)
                mm.then_inc(s_y, 1)

            def step(p, z, turn, i):
                known = isinstance(p, int)
                if not known or p + 1 < PAIRS:
                    pe.wait_ge(s_xT, p + 2)
                    pe.wait_ge(s_sig, p + 1)
                    hidden(p + 1, z(1))
                pe.wait_ge(s_at, p + 1)
                spread(p, z(0), 0)
                spread(p, z(0), 1)
                if not known or p + 2 < PAIRS:
                    transpose_x(p + 2, z(2), turn(2))
                if not known or p > 0:
                    turn_hs(p - 1, z(-1))
                spread(p, z(0), 2)
                if not known or p > 0:
                    finish(p - 1, z(-1))
                spread(p, z(0), 3)
                pe.wait_ge(s_pos, p + 1)
                nc.tensor.transpose(ps_t[:, 0:P], pos[z(0)][:], ident[:]).then_inc(s_posT_ps, 1)
                pe.wait_ge(s_tab, p * 2 + 2)
                pe.wait_ge(s_taken, p + 1)
                for c in range(CHUNKS):
                    pe.wait_ge(s_hot, p * CHUNKS + c + 3)
                    for q in range(c * QB, (c + 1) * QB):
                        at_q = slice(q % (QS // 2) * PARTS * 2 * HG, (q % (QS // 2) + 1) * PARTS * 2 * HG)
                        for b in range(2):
                            mm = nc.tensor.matmul(ps_l[halves[b], q // (QS // 2), at_q], hot[:, q, halves[b]],
                                                  table[b][z(0)][:, q].rearrange("p n c -> p (n c)"),
                                                  start=True, stop=True)
                    if c % 2 == 1:
                        mm.then_inc(s_look, 1)

            pe.sem_inc(s_yev, RING)
            pe.sem_inc(s_look, 2 * RING)
            pe.sem_inc(s_hot, 2)
            pe.sem_inc(s_taken, 1)
            pe.wait_ge(s_const, 4)
            transpose_x(0, 0, 0)
            pe.wait_ge(s_xT, 1)
            transpose_x(1, 1, 0)
            hidden(0, 0)
            in_turns(pe, step)
            turn_hs(PAIRS - 1, (PAIRS - 1) % RING)
            finish(PAIRS - 1, (PAIRS - 1) % RING)


def build(nc, a, out):
    with ExitStack() as ctx:
        resid = ctx.enter_context(nc.sbuf_tensor("resid", [P, TILES, D], F32))
        ident = ctx.enter_context(nc.sbuf_tensor("ident", [P, P], F32))
        tables = ctx.enter_context(nc.sbuf_tensor("tables", [P, SPLINES, QS, PARTS, 2, HG], BF16))
        x_rows = nc.dram_tensor("x_rows", (ROWS, D), F32).ap()
        y_rows = nc.dram_tensor("y_rows", (ROWS, D), F32).ap()
        s_zeroed = ctx.enter_context(nc.semaphore("x_rows_zeroed"))
        scratch = (x_rows, y_rows, s_zeroed)
        with ExitStack() as setup:
            zeros = setup.enter_context(nc.sbuf_tensor("zeros", [P, D], F32))
            s_zero = setup.enter_context(nc.semaphore("zeros_set"))
            block = setup.enter_context(nc.Block())

            @block.gpsimd
            def _(pool):
                pool.memset(ident[:], 0.0).then_inc(s_zero, 1)
                pool.memset(zeros[:], 0.0).then_inc(s_zero, 1)
                pool.wait_ge(s_zero, 2)
                pool.affine_select(out=ident[:], in_=ident[:], compare_op=ALU.not_equal, fill=1.0,
                                   base=0, pattern=[[-1, P]], channel_multiplier=1)

            @block.sync
            def _(sp):
                sp.wait_ge(s_zero, 2)
                sp.dma_start(x_rows.rearrange("(n p) d -> p n d", p=P),
                             zeros[:, None, :].to_broadcast([P, ROWS // P, D])).then_inc(s_zeroed, 16)
                sp.wait_ge(s_zeroed, 16)

        patch_attention(nc, resid, ident, a)
        experts(nc, resid, ident, a, tables)
        attention(nc, resid, ident, a)
        splines(nc, resid, ident, a, scratch, out, tables)


def kernel(**inputs):
    import numpy as np
    import concourse.bacc as bacc
    from concourse.bass_utils import run_bass_kernel_spmd as run

    v = {k: np.asarray(x) for k, x in inputs.items()}

    def flat(x, *shape):
        return np.ascontiguousarray(x.reshape(shape) if shape else x)

    x = v["x"].reshape(GROUPS, GT, 2, 3, 8, 28, 8, 28).transpose(0, 1, 3, 5, 7, 2, 4, 6)
    x = x.reshape(GROUPS, GT, PC, PK, P).transpose(0, 1, 3, 2, 4)
    arrays = {
        "x": flat(x),
        "w_patch": flat(v["L0_tok_W"].T.reshape(PC, PK, D).transpose(1, 0, 2)),
        "wq": flat(v["L0_attn_Wq"]), "wk": flat(v["L0_attn_Wk"]),
        "wv": flat(v["L0_attn_Wv"]), "wo": flat(v["L0_attn_Wo"]),
        "bias_cols": flat(np.stack([v["L0_attn_bq"], v["L0_attn_bk"], v["L0_attn_bv"]], 1)),
        "b_patch": flat(v["L0_tok_b"]),
        "bo": flat(v["L0_attn_bo"]),
        "cls_rows": flat(np.tile(np.stack([v["cls_tok"][0, 0], v["L0_tok_class_token"][0]]), (IMAGES, 1))),
        "cls_mul": flat(np.tile(np.stack([np.ones(D, np.float32), v["L0_tok_pos_embed"][0]]), (IMAGES, 1))),
        "pos": flat(v["L0_tok_pos_embed"][1:]),
        "gamma_beta": flat(np.stack([v["L1_ffn_gamma"], v["L1_ffn_beta"]], 1)),
        "wd_sums": flat(v["L1_ffn_Wd"].transpose(2, 0, 1)),
        "spline_w": flat(np.concatenate([v["L1_ffn_Wd"].transpose(0, 2, 1), v["L1_ffn_Wu"].transpose(0, 2, 1),
                                         np.tile(v["L1_ffn_scale"][:, None, None], (1, P, 2))], 2)),
        "spline_tables": flat(np.stack([v["L1_ffn_spline_bases"], v["L1_ffn_spline_slopes"]])
                              .reshape(2, SPLINES, QS, HG, GRID).transpose(3, 4, 1, 2, 0), P, SPLINES * 2 * QS),
        "w_qkv": flat(v["L1_attn_w_qkv"].reshape(D, 3, D)),
        "router": flat(v["L0_ffn_router_w"].T),
        "router_b": flat(v["L0_ffn_router_b"]),
        "fc1": flat(v["L0_ffn_fc1_w"].transpose(2, 0, 1)),
        "fc2": flat(v["L0_ffn_fc2_w"].reshape(EXPERTS, D, HC, P).transpose(3, 0, 2, 1)),
        "b1": flat(v["L0_ffn_fc1_b"].reshape(EXPERTS, 2 * HC, P).transpose(2, 0, 1)),
        "b2": flat(v["L0_ffn_fc2_b"]),
    }
    nc = bacc.Bacc("TRN2", target_bir_lowering=False, num_devices=1)
    aps = {n: nc.dram_tensor("in_" + n, x.shape, mybir.dt.from_np(x.dtype), kind="ExternalInput").ap()
           for n, x in arrays.items()}
    out = nc.dram_tensor("out", (IMAGES, SEQ, D), F32, kind="ExternalOutput").ap()
    build(nc, aps, out)
    r = run(nc, [{"in_" + n: x for n, x in arrays.items()}], core_ids=[0])
    return r.results[0]["out"]
```

```python
from contextlib import ExitStack

import concourse.bass as bass
from concourse import mybir

P = 128
IMAGES = 64
PATCHES = 64
CLS = 2
SEQ = CLS + PATCHES
D = 128
TILES = IMAGES * SEQ // P
PTILES = TILES - 1
GROUP = 4
GROUPS = IMAGES // GROUP
GT = GROUP * PATCHES // P
PK, PC = 112, 21
HEADS, DH = 8, 16
EPS = 1e-5

ALU = mybir.AluOpType
ACT = mybir.ActivationFunctionType
F32 = mybir.dt.float32
BF16 = mybir.dt.bfloat16
I32 = mybir.dt.int32
U32 = mybir.dt.uint32
AX_X = mybir.AxisListType.X
ds = bass.ds


class Chain:

    def __init__(self, eng, sem, turns=None):
        self.turns = turns
        self.eng, self.sem, self.count, self.made = eng, sem, 0, 0

    def mark(self, ins):
        ins.then_inc(self.sem, 1)
        self.count = self.count + 1
        self.made += 1
        return ins

    def sync(self):
        self.eng.wait_ge(self.sem, self.count)

    def apart(self):
        self.sync()
        self.eng.sem_inc(self.turns, 1)

    def step(self, ins):
        self.mark(ins)
        self.sync()

    def enter(self, i, marks):
        self.base, self.marks, self.made = self.count, marks, 0
        self.count = self.base + i * marks

    def leave(self, trips):
        assert self.made == self.marks, (self.made, self.marks)
        self.count = self.base + trips * self.marks


def row_bc(dram_row):
    return dram_row.rearrange("(o d) -> o d", o=1).to_broadcast([P, dram_row.shape[0]])


def rsqrt_steps(pool, chain, var, minus_half, veps, t, r):
    g = pool
    chain.eng.sem_inc(chain.turns, 1)
    chain.step(g.tensor_scalar(veps, var, EPS, None, ALU.add))
    chain.step(g.tensor_tensor(r, veps, minus_half, ALU.pow))
    chain.step(g.tensor_tensor(t, r, r, ALU.mult))
    chain.step(g.tensor_tensor(t, t, veps, ALU.mult))
    chain.eng.sem_inc(chain.turns, 1)
    chain.step(g.tensor_scalar(t, t, -0.5, 1.5, ALU.mult, ALU.add))
    return g.tensor_tensor(r, r, t, ALU.mult)


RSQRT_MARKS = 5


def tile_statistics(ch, stats, x, tiles):
    for t in tiles:
        ch.mark(ch.eng.bn_stats(stats[:, t, :], x[:, t, :]))


def patch_attention(nc, resid, ident, a, s_turns, token_stats):
    with ExitStack() as ctx:
        def sb(name, shape, dt=F32):
            return ctx.enter_context(nc.sbuf_tensor(name, shape, dt))

        def psum(name, shape):
            return ctx.enter_context(nc.psum_tensor(name, shape, F32))

        def sem(name):
            return ctx.enter_context(nc.semaphore(name))

        ps_s = psum("pa_scores", [P, 2, 512])
        ps_pt = psum("pa_probsT", [P, 2, 512])
        ps_tok = psum("pa_tokens", [P, 512])
        ps_m0 = psum("pa_m0", [P, 512])
        ps_m1 = psum("pa_m1", [P, 512])
        ps_m2 = psum("pa_m2", [P, 512])

        w_patch = sb("pa_w_patch", [P, PC, D])
        x_patch = [sb(f"pa_x{t}", [P, PC, P]) for t in range(GT)]
        wq, wk, wv, wo = (sb(f"pa_w{n}", [P, D]) for n in "qkvo")
        bias_cols = sb("pa_bias_cols", [P, 3])
        b_patch = sb("pa_b_patch", [P, D])
        b_out = sb("pa_b_out", [P, D])
        pos = sb("pa_pos", [P, D])
        cls_mul = sb("pa_cls_mul", [P, D])
        head_mask = sb("pa_head_mask", [P, HEADS])
        diag125 = sb("pa_diag125", [P, SEQ], BF16)
        causal = sb("pa_causal", [P, 4, SEQ], BF16)
        minus_half = sb("pa_minus_half", [P, GT])
        stats = sb("pa_stats", [P, GT, 6])
        mv = sb("pa_mv", [P, GT, 2])
        veps, newton, rstd = (sb(f"pa_{n}", [P, GT]) for n in ("veps", "newton", "rstd"))
        xn = sb("pa_xn", [P, GT, D])
        xnT = sb("pa_xnT", [P, GROUP, SEQ])
        qT = sb("pa_qT", [P, GROUP, SEQ])
        kT = sb("pa_kT", [P, GROUP, SEQ])
        kbd = sb("pa_kbd", [P, GROUP, HEADS, SEQ])
        v1 = sb("pa_v1", [P, GROUP, HEADS, DH + 1])
        top = sb("pa_top", [P, GROUP, HEADS])
        probs = [sb(f"pa_probs{b}", [P, HEADS, SEQ]) for b in range(2)]
        probsT = [sb(f"pa_probsT{b}", [P, HEADS, SEQ]) for b in range(2)]
        rsum = sb("pa_rsum", [P, GROUP, HEADS])
        o_rows = sb("pa_o_rows", [P, GROUP, D])
        oT = sb("pa_oT", [P, GROUP * PATCHES])
        oT_cls = sb("pa_oT_cls", [P, IMAGES, CLS])

        s_w = sem("pa_weights")
        s_w2 = sem("pa_weights_act")
        s_wp = sem("pa_patch_weights")
        s_x = [sem(f"pa_x_loaded{t}") for t in range(GT)]
        s_xfree = [sem(f"pa_x_used{t}") for t in range(GT)]
        s_const = sem("pa_constants")
        s_pool = sem("pa_pool_chain")
        s_dve = sem("pa_dve_chain")
        s_tok = sem("pa_tokens_taken")
        s_stats = sem("pa_stats_ready")
        s_rstd = sem("pa_rstd_ready")
        s_xn = sem("pa_xn_ready")
        s_xnT_ps = sem("pa_xnT_in_psum")
        s_xnT = sem("pa_xnT_ready")
        s_q_ps = sem("pa_q_in_psum")
        s_k_ps = sem("pa_k_in_psum")
        s_v_ps = sem("pa_v_in_psum")
        s_q = sem("pa_q_ready")
        s_k = sem("pa_k_ready")
        s_v = sem("pa_v_ready")
        s_kbd = sem("pa_kbd_ready")
        s_s = sem("pa_scores_ready")
        s_sub = sem("pa_scores_taken")
        s_p = sem("pa_probs_ready")
        s_pT_ps = sem("pa_probsT_in_psum")
        s_pT = sem("pa_probsT_ready")
        s_o_ps = sem("pa_o_in_psum")
        s_o = sem("pa_o_ready")
        s_oT_ps = sem("pa_oT_in_psum")
        s_oT = sem("pa_oT_ready")
        s_cls = sem("pa_oT_cls_kept")
        s_proj = sem("pa_projection_ready")
        s_bo = sem("pa_bias_added")
        s_h = sem("pa_projection_taken")

        scores = ps_s[0:SEQ, :, 0:4 * SEQ].rearrange("p b (h k) -> p b h k", h=4)
        probsT_ps = ps_pt[0:SEQ, :, 0:4 * SEQ].rearrange("p b (h k) -> p b h k", h=4)

        def rows(n):
            return n[:, 0:GROUP * SEQ].rearrange("p (i s) -> p i s", i=GROUP)

        def o_ps(i):
            return (ps_m1, ps_m2)[i % 2][0:SEQ, 0:HEADS * (DH + 1)].rearrange("p (h d) -> p h d", h=HEADS)

        LAST = GROUPS - 1

        block = ctx.enter_context(nc.Block())

        @block.sync
        def _(sp):
            sp.dma_start(w_patch[0:PK, :, :], a["w_patch"]).then_inc(s_wp, 16)
            for t in range(GT):
                sp.dma_start(x_patch[t][0:PK, :, :], a["x"][0, t]).then_inc(s_x[t], 16)
            with sp.Fori(1, GROUPS) as g:
                for t in range(GT):
                    sp.wait_ge(s_xfree[t], g)
                    sp.dma_start(x_patch[t][0:PK, :, :], a["x"][g, t]).then_inc(s_x[t], 16)

        @block.gpsimd
        def _(pool):
            ch = Chain(pool, s_pool, s_turns)
            ch.mark(pool.memset(head_mask[:], 1.0))
            ch.mark(pool.memset(diag125[:], 0.0))
            ch.mark(pool.memset(causal[:], 0.0))
            ch.sync()
            ch.step(pool.affine_select(out=head_mask[:], in_=head_mask[:], compare_op=ALU.is_ge, fill=0.0,
                                       base=0, pattern=[[-DH, HEADS]], channel_multiplier=1))
            pool.affine_select(out=head_mask[:], in_=head_mask[:], compare_op=ALU.is_ge, fill=0.0,
                               base=DH - 1, pattern=[[DH, HEADS]], channel_multiplier=-1).then_inc(s_const, 1)
            pool.affine_select(out=diag125[:], in_=diag125[:], compare_op=ALU.not_equal, fill=125.0,
                               base=0, pattern=[[-1, SEQ]], channel_multiplier=1).then_inc(s_const, 1)
            pool.affine_select(out=causal[:], in_=causal[:], compare_op=ALU.is_ge, fill=-800.0,
                               base=0, pattern=[[0, 4], [-1, SEQ]], channel_multiplier=1).then_inc(s_const, 1)
            pool.memset(v1[:], 1.0).then_inc(s_const, 1)
            pool.memset(minus_half[:], -0.5).then_inc(s_const, 1)
            pool.wait_ge(s_const, 5)

            def norm_scale(n):
                pool.wait_ge(s_stats, n)
                rsqrt_steps(pool, ch, mv[:, :, 1], minus_half[:], veps[:], newton[:], rstd[:]).then_inc(s_rstd, 1)

            def add_output_bias(g):
                pool.wait_ge(s_xn, g + 2)
                tiles = resid[:, ds(g * GT, GT), :]
                pool.tensor_tensor(tiles, tiles, b_out[:, None, :].to_broadcast([P, GT, D]),
                                   ALU.add).then_inc(s_bo, 1)

            def attention(g, more):
                pool.wait_ge(s_k, g + 1)
                for i in range(GROUP):
                    pool.wait_ge(s_s, g * GROUP + i + 1)
                    pool.tensor_tensor(kbd[:, i], kT[:, i, None, :].to_broadcast([P, HEADS, SEQ]),
                                       head_mask[:, :, None].to_broadcast([P, HEADS, SEQ]),
                                       ALU.mult).then_inc(s_kbd, 1)
                if more:
                    norm_scale(g + 3)
                    add_output_bias(g + 1)

            norm_scale(1)
            norm_scale(2)
            pool.wait_ge(s_w2, 16)
            pool.wait_ge(s_xn, 1)
            pool.tensor_tensor(resid[:, PTILES, :], resid[:, PTILES, :], b_out[:], ALU.add).then_inc(s_bo, 1)
            add_output_bias(0)
            with pool.Fori(0, LAST) as g:
                ch.enter(g, RSQRT_MARKS)
                attention(g, True)
                ch.leave(LAST)
            attention(LAST, False)

        @block.vector
        def _(dve):
            ch = Chain(dve, s_dve, s_turns)

            def norm_apply(t, tile):
                return dve.tensor_scalar(xn[:, t, :], resid[:, tile, :], mv[:, t, 0:1], rstd[:, t:t + 1],
                                         ALU.subtract, ALU.mult)

            dve.wait_ge(s_w, 16 * 10)
            ch.step(dve.tensor_tensor(resid[:, PTILES, :], resid[:, PTILES, :], cls_mul[:], ALU.mult))
            for t in range(GT):
                ch.mark(dve.bn_stats(stats[:, t, :], resid[:, PTILES, :]))
            ch.sync()
            for t in range(GT):
                ins = dve.bn_aggr(mv[:, t, :], stats[:, t, :])
                if t < GT - 1:
                    ch.mark(ins)
            ch.sync()
            ins.then_inc(s_stats, 1)
            dve.wait_ge(s_rstd, 1)
            norm_apply(0, PTILES).then_inc(s_xn, 1)

            def tokens(g, n):
                tiles = resid[:, ds(g * GT, GT), :]
                dve.wait_ge(s_xfree[GT - 1], g + 1)
                dve.tensor_tensor(tiles, ps_tok[:, 0:GT * D].rearrange("p (t d) -> p t d", t=GT),
                                  b_patch[:, None, :].to_broadcast([P, GT, D]), ALU.add).then_inc(s_tok, 1)
                dve.wait_ge(s_tok, g + 1)
                ch.step(dve.tensor_tensor(tiles, tiles, pos[:, None, :].to_broadcast([P, GT, D]), ALU.mult))
                ch.apart()
                for t in range(GT):
                    ch.mark(dve.bn_stats(stats[:, t, :], resid[:, g * GT + t, :]))
                ch.apart()
                for t in range(GT - 1):
                    ch.mark(dve.bn_aggr(mv[:, t, :], stats[:, t, :]))
                dve.bn_aggr(mv[:, GT - 1, :], stats[:, GT - 1, :]).then_inc(s_stats, 1)

            TOKEN_MARKS = 1 + GT + GT - 1

            def normalise(g):
                dve.wait_ge(s_rstd, g + 2)
                dve.wait_ge(s_xnT_ps, g + 1)
                for t in range(GT - 1):
                    ch.mark(norm_apply(t, g * GT + t))
                ch.sync()
                norm_apply(GT - 1, g * GT + GT - 1).then_inc(s_xn, 1)

            def softmax(g, i):
                dve.wait_ge(s_s, (g + 1) * GROUP + i + 1)
                ch.step(dve.tensor_reduce(top[0:SEQ, i, :].rearrange("p (b h) -> p b h", b=2), scores, AX_X, ALU.max))
                dve.tensor_tensor(probs[i % 2][0:SEQ].rearrange("p (b h) k -> p b h k", b=2), scores,
                                  top[0:SEQ, i, :].rearrange("p (b h) -> p b h", b=2)[:, :, :, None]
                                  .to_broadcast([SEQ, 2, 4, SEQ]), ALU.subtract).then_inc(s_sub, 1)

            def divide(g, i):
                dve.wait_ge(s_o_ps, g * GROUP + i + 1)
                ch.step(dve.reciprocal(rsum[0:SEQ, i, :], o_ps(i)[:, :, DH]))
                dve.tensor_tensor(o_rows[0:SEQ, i, :].rearrange("p (h d) -> p h d", h=HEADS), o_ps(i)[:, :, 0:DH],
                                  rsum[0:SEQ, i, :, None].to_broadcast([SEQ, HEADS, DH]), ALU.mult).then_inc(s_o, 1)

            def attention(g, more):
                dve.wait_ge(s_v_ps, g + 1)
                dve.tensor_copy(v1[0:SEQ, :, :, 0:DH],
                                ps_m0[0:SEQ, :].rearrange("p (i h d) -> p i h d", i=GROUP, h=HEADS)).then_inc(s_v, 1)
                softmax(g, 0)
                softmax(g, 1)
                divide(g, 0)
                softmax(g, 2)
                divide(g, 1)
                if more:
                    tokens(g + 1, 0)
                softmax(g, 3)
                divide(g, 2)
                if more:
                    normalise(g + 1)
                divide(g, 3)
                dve.wait_ge(s_proj, g + 1)
                dve.wait_ge(s_bo, g + 2)
                tiles = resid[:, ds(g * GT, GT), :]
                dve.tensor_tensor(tiles, tiles, ps_m1[:, 0:GT * D].rearrange("p (t d) -> p t d", t=GT),
                                  ALU.add).then_inc(s_h, 1)
                dve.wait_ge(s_h, g + 2)
                dve.sem_inc(s_turns, 1)
                tile_statistics(ch, token_stats, resid, [g * GT + t for t in range(GT)])

            tokens(0, 0)
            normalise(0)
            dve.wait_ge(s_const, 5)
            with dve.Fori(0, LAST) as g:
                ch.enter(g, 2 * GROUP + TOKEN_MARKS + GT - 1 + GT)
                attention(g, True)
                ch.leave(LAST)
            attention(LAST, False)
            dve.wait_ge(s_proj, GROUPS + 1)
            dve.wait_ge(s_bo, GROUPS + 1)
            ch.step(dve.tensor_tensor(resid[:, PTILES, :], resid[:, PTILES, :], ps_m2[:, 0:D], ALU.add))
            tile_statistics(ch, token_stats, resid, [PTILES])

        @block.scalar
        def _(act):
            for dst, src in [(wq[:], a["wq"]), (wk[:], a["wk"]), (wv[:], a["wv"]), (wo[:], a["wo"]),
                             (bias_cols[:], a["bias_cols"]), (b_patch[:], row_bc(a["b_patch"])),
                             (resid[:, PTILES, :], a["cls_rows"]), (cls_mul[:], a["cls_mul"]),
                             (pos[0:PATCHES, :], a["pos"]), (pos[PATCHES:P, :], a["pos"])]:
                act.dma_start(dst, src).then_inc(s_w, 16)
            act.dma_start(b_out[:], row_bc(a["bo"])).then_inc(s_w2, 16)

            def norm_transposed(g):
                act.wait_ge(s_xnT_ps, g + 2)
                nc.scalar.copy(xnT[:, :, CLS:SEQ], ps_m0[:, 0:GT * P].rearrange("p (i s) -> p i s", i=GROUP))\
                    .then_inc(s_xnT, 1)

            def attention(g, more):
                act.wait_ge(s_q_ps, g + 1)
                nc.scalar.activation(qT[:], rows(ps_m1), ACT.Identity, bias=bias_cols[:, 0:1]).then_inc(s_q, 1)
                act.wait_ge(s_k_ps, g + 1)
                act.wait_ge(s_kbd, g * GROUP + 1)
                nc.scalar.activation(kT[:], rows(ps_m2), ACT.Identity, bias=bias_cols[:, 1:2]).then_inc(s_k, 1)
                for i in range(GROUP):
                    act.wait_ge(s_sub, g * GROUP + i + 2)
                    nc.scalar.activation(probs[i % 2][0:SEQ], probs[i % 2][0:SEQ], ACT.Exp,
                                         scale=1.0 / DH ** 0.5).then_inc(s_p, 1)
                    act.wait_ge(s_pT_ps, g * GROUP + i + 1)
                    nc.scalar.copy(probsT[i % 2][0:SEQ].rearrange("p (b h) k -> p b h k", b=2), probsT_ps)\
                        .then_inc(s_pT, 1)
                if more:
                    norm_transposed(g + 1)
                act.wait_ge(s_oT_ps, g + 1)
                nc.scalar.activation(oT_cls[:, ds(g * GROUP, GROUP), :], rows(ps_m0)[:, :, 0:CLS], ACT.Identity,
                                     bias=bias_cols[:, 2:3]).then_inc(s_cls, 1)
                nc.scalar.activation(oT[:].rearrange("p (i s) -> p i s", i=GROUP), rows(ps_m0)[:, :, CLS:SEQ],
                                     ACT.Identity, bias=bias_cols[:, 2:3]).then_inc(s_oT, 1)

            act.sem_inc(s_kbd, 1)
            act.wait_ge(s_xnT_ps, 1)
            nc.scalar.copy(xnT[:, :, 0:CLS], ps_m0[:, None, 0:CLS].to_broadcast([P, GROUP, CLS])).then_inc(s_xnT, 1)
            norm_transposed(0)
            act.wait_ge(s_w, 16 * 10)
            with act.Fori(0, LAST) as g:
                attention(g, True)
            attention(LAST, False)

        @block.tensor
        def _(pe):
            def patches(g, t, chunks):
                if chunks[0] == 0:
                    pe.wait_ge(s_x[t], 16 * (g + 1))
                    if t == 0 and not (isinstance(g, int) and g == 0):
                        pe.wait_ge(s_tok, g)
                for c in chunks:
                    mm = nc.tensor.matmul(ps_tok[:, t * D:(t + 1) * D], x_patch[t][0:PK, c, :], w_patch[0:PK, c, :],
                                          start=(c == 0), stop=(c == PC - 1))
                if chunks[-1] == PC - 1:
                    mm.then_inc(s_xfree[t], 1)

            def norm_transposes(g):
                pe.wait_ge(s_xn, g + 2)
                for t in range(GT):
                    mm = nc.tensor.transpose(ps_m0[:, t * P:(t + 1) * P], xn[:, t, :], ident[:])
                mm.then_inc(s_xnT_ps, 1)

            def qkv(g):
                pe.wait_ge(s_xnT, g + 2)
                pe.wait_ge(s_h, g + 1)
                nc.tensor.matmul(rows(ps_m1), wq[:], xnT[:], start=True, stop=True).then_inc(s_q_ps, 1)
                nc.tensor.matmul(rows(ps_m2), wk[:], xnT[:], start=True, stop=True).then_inc(s_k_ps, 1)
                for i in range(GROUP):
                    mm = nc.tensor.matmul(ps_m0[0:SEQ, i * D:(i + 1) * D], xnT[:, i, :], wv[:], start=True, stop=True)
                mm.then_inc(s_v_ps, 1)
                pe.wait_ge(s_q, g + 1)

            def score(g, i):
                pe.wait_ge(s_kbd, g * GROUP + i + 2)
                pe.wait_ge(s_sub, g * GROUP + i + 1)
                for b in range(2):
                    nc.tensor.matmul(scores[:, b], diag125[0:SEQ, :], causal[0:SEQ], start=True, stop=False)
                    mm = nc.tensor.matmul(scores[:, b], qT[:, i, :], kbd[:, i, 4 * b:4 * b + 4, :],
                                          start=False, stop=True)
                mm.then_inc(s_s, 1)

            def transposes(g, i):
                pe.wait_ge(s_p, g * GROUP + i + 1)
                pe.wait_ge(s_pT, g * GROUP + i + 1)
                for h in range(HEADS):
                    mm = nc.tensor.transpose(probsT_ps[:, h // 4, h % 4, :], probs[i % 2][0:SEQ, h, :],
                                             ident[0:SEQ, 0:SEQ])
                mm.then_inc(s_pT_ps, 1)

            def values(g, i):
                pe.wait_ge(s_pT, g * GROUP + i + 2)
                if i == 0:
                    pe.wait_ge(s_v, g + 1)
                if i >= 2:
                    pe.wait_ge(s_o, g * GROUP + i - 1)
                for h in range(HEADS):
                    mm = nc.tensor.matmul(o_ps(i)[:, h, :], probsT[i % 2][0:SEQ, h, :], v1[0:SEQ, i, h, :],
                                          start=True, stop=True)
                mm.then_inc(s_o_ps, 1)

            def turn_output(g, more):
                pe.wait_ge(s_o, (g + 1) * GROUP)
                pe.wait_ge(s_xnT, g + (3 if more else 2))
                for i in range(GROUP):
                    mm = nc.tensor.transpose(ps_m0[:, i * SEQ:(i + 1) * SEQ], o_rows[0:SEQ, i, :],
                                             ident[0:SEQ, 0:SEQ])
                mm.then_inc(s_oT_ps, 1)

            def project(g):
                pe.wait_ge(s_oT, g + 1)
                for t in range(GT):
                    mm = nc.tensor.matmul(ps_m1[:, t * D:(t + 1) * D], oT[:, t * P:(t + 1) * P], wo[:],
                                          start=True, stop=True)
                mm.then_inc(s_proj, 1)

            def attention(g, more, second):
                def ahead(start, stop):
                    if more:
                        patches(g + 1, 1, range(start, stop))

                def two_ahead(start, stop):
                    if second:
                        patches(g + 2, 0, range(start, stop))

                qkv(g)
                ahead(0, 4)
                score(g, 0)
                ahead(4, 14)
                transposes(g, 0)
                score(g, 1)
                ahead(14, 18)
                values(g, 0)
                transposes(g, 1)
                score(g, 2)
                ahead(18, PC)
                values(g, 1)
                transposes(g, 2)
                score(g, 3)
                two_ahead(0, 6)
                values(g, 2)
                transposes(g, 3)
                if more:
                    norm_transposes(g + 1)
                two_ahead(6, 9)
                values(g, 3)
                two_ahead(9, 13)
                turn_output(g, more)
                two_ahead(13, 17)
                project(g)
                two_ahead(17, PC)

            pe.sem_inc(s_sub, 1)
            pe.sem_inc(s_pT, 1)
            pe.sem_inc(s_h, 1)
            pe.sem_inc(s_s, GROUP)
            pe.wait_ge(s_wp, 16)
            patches(0, 0, range(PC))
            patches(0, 1, range(PC))
            pe.wait_ge(s_xn, 1)
            nc.tensor.transpose(ps_m0[:, 0:P], xn[:, 0, :], ident[:]).then_inc(s_xnT_ps, 1)
            patches(1, 0, range(PC))
            pe.wait_ge(s_xnT, 1)
            norm_transposes(0)
            pe.wait_ge(s_w, 16 * 10)
            pe.wait_ge(s_const, 5)
            with pe.Fori(0, LAST - 1) as g:
                attention(g, True, True)
            attention(LAST - 1, True, False)
            attention(LAST, False, False)
            pe.wait_ge(s_cls, GROUPS)
            nc.tensor.matmul(ps_m2[:, 0:D], oT_cls[:].rearrange("p i c -> p (i c)"), wo[:],
                             start=True, stop=True).then_inc(s_proj, 1)


def rstd_steps(dve, ch, var, veps, root, t, r, s_veps, s_root, n):
    dve.tensor_scalar(veps, var, EPS, None, ALU.add).then_inc(s_veps, 1)
    dve.wait_ge(s_root, n)
    ch.step(dve.reciprocal(r, root))
    ch.step(dve.tensor_tensor(t, r, r, ALU.mult))
    ch.step(dve.tensor_tensor(t, t, veps, ALU.mult))
    ch.step(dve.tensor_scalar(t, t, -0.5, 1.5, ALU.mult, ALU.add))
    return dve.tensor_tensor(r, r, t, ALU.mult)


EXPERTS, HIDDEN, HC = 8, 256, 2
TRIO = 3
TRIOS = TILES // TRIO


def norm_statistics(dve, ch, stats, mean, var, scratch):
    mean_e, mean_o, sq_e, sq_o = stats[:, :, 1], stats[:, :, 4], stats[:, :, 2], stats[:, :, 5]
    ch.mark(dve.tensor_tensor(mean, mean_e, mean_o, ALU.add))
    ch.mark(dve.tensor_tensor(scratch[0], mean_e, mean_o, ALU.subtract))
    ch.step(dve.tensor_tensor(scratch[1], sq_e, sq_o, ALU.add))
    ch.mark(dve.tensor_scalar(mean, mean, 0.5, None, ALU.mult))
    ch.mark(dve.tensor_scalar(scratch[1], scratch[1], 1.0 / D, None, ALU.mult))
    ch.step(dve.tensor_tensor(scratch[0], scratch[0], scratch[0], ALU.mult))
    return dve.scalar_tensor_tensor(out=var, in0=scratch[0], scalar=0.25, in1=scratch[1],
                                    op0=ALU.mult, op1=ALU.add)


def experts(nc, resid, ident, a, tables, s_turns, stats, scratch):
    with ExitStack() as ctx:
        def sb(name, shape, dt=F32):
            return ctx.enter_context(nc.sbuf_tensor(name, shape, dt))

        def sem(name):
            return ctx.enter_context(nc.semaphore(name))

        fc1 = sb("ex_fc1", [P, EXPERTS, 2 * HIDDEN])
        fc2 = sb("ex_fc2", [P, EXPERTS, HC, D])
        b1 = sb("ex_b1", [P, EXPERTS, 2 * HC])
        b2 = sb("ex_b2", [P, D])
        router = sb("ex_router", [P, EXPERTS])
        rb = sb("ex_router_bias", [P, EXPERTS])
        mean, var, veps, root, rstd, t0, t1 = (
            sb(f"ex_{n}", [P, TILES]) for n in ("mean", "var", "veps", "root", "rstd", "t0", "t1"))
        xs = [sb(f"ex_xs{j}", [P, D]) for j in range(TRIO)]
        xTs = [sb(f"ex_xTs{j}", [P, P]) for j in range(TRIO)]
        xT = sb("ex_xT", [P, TILES * P])
        logits, second, eq, pick1, pick2, cw = (
            sb(f"ex_{n}", [P, TILES, EXPERTS]) for n in ("logits", "second", "eq", "pick1", "pick2", "cw"))
        first_wins = sb("ex_first_wins", [P, EXPERTS])
        m1, m2, f1, f2, dl, den, w1, w2 = (
            sb(f"ex_{n}", [P, TILES]) for n in ("m1", "m2", "f1", "f2", "dl", "den", "w1", "w2"))
        cws = sb("ex_cws", [P, TRIO, EXPERTS])
        cwT = sb("ex_cwT", [P, TRIO * P])
        gate = [sb(f"ex_gate{j}", [P, TRIO * P]) for j in range(HC)]
        act_t = [[sb(f"ex_act{b}{j}", [P, TRIO * P]) for j in range(HC)] for b in range(2)]
        acc = sb("ex_acc", [P, TRIO, D])

        s_w = sem("ex_weights")
        s_router = sem("ex_router_loaded")
        s_dve = sem("ex_dve_chain")
        s_sum = sem("ex_sum_chain")
        s_const = sem("ex_constants")
        s_veps = sem("ex_variances_ready")
        s_root = sem("ex_roots_ready")
        s_rstd = sem("ex_rstd_ready")
        s_xs = sem("ex_xs_ready")
        s_xT_ps = sem("ex_xT_in_psum")
        s_xT = sem("ex_xT_ready")
        s_copy = sem("ex_xT_kept")
        s_logit = sem("ex_logits_in_psum")
        s_dl = sem("ex_top_difference")
        s_exp = sem("ex_top_exp")
        s_cws = sem("ex_cws_ready")
        s_cwT_ps = sem("ex_cwT_in_psum")
        s_cwT = sem("ex_cwT_ready")
        s_bias = sem("ex_bias_term_in_psum")
        s_init = sem("ex_acc_started")
        s_h1 = sem("ex_h1_in_psum")
        s_h2 = sem("ex_h2_in_psum")
        s_gate = sem("ex_gate_ready")
        s_a = sem("ex_act_ready")
        s_y = sem("ex_y_in_psum")
        s_acc = sem("ex_y_taken")
        STEPS = EXPERTS * HC

        with ExitStack() as prep:
            ps_x = [prep.enter_context(nc.psum_tensor(f"ex_ps_x{j}", [P, 512], F32)) for j in range(TRIO)]
            ps_l = prep.enter_context(nc.psum_tensor("ex_ps_logits", [P, 512], F32))
            block = prep.enter_context(nc.Block())

            @block.sync
            def _(sp):
                sp.dma_start(router[:], a["router"]).then_inc(s_router, 16)
                for dst, src in [(rb[:], row_bc(a["router_b"])), (fc1[:], a["fc1"]),
                                 (fc2[:], a["fc2"]), (b1[:], a["b1"]), (b2[0:EXPERTS, :], a["b2"])]:
                    sp.dma_start(dst, src).then_inc(s_w, 16)

            @block.gpsimd
            def _(pool):
                pool.iota(first_wins[:], pattern=[[-1, EXPERTS]], base=EXPERTS, channel_multiplier=0,
                          allow_small_or_imprecise_dtypes=True).then_inc(s_const, 1)
                with pool.Fori(0, TRIOS) as i:
                    for j in range(TRIO):
                        pool.wait_ge(s_xT, (i + 1) * TRIO + j + 1)
                        pool.tensor_copy(xT[:, ds((i * TRIO + j) * P, P)], xTs[j][:]).then_inc(s_copy, 1)

            @block.vector
            def _(dve):
                ch = Chain(dve, s_dve, s_turns)
                ch.step(norm_statistics(dve, ch, stats, mean[:], var[:], (t0[:], t1[:])))
                rstd_steps(dve, ch, var[:], veps[:], root[:], t0[:], rstd[:], s_veps, s_root, 1).then_inc(s_rstd, 1)
                dve.wait_ge(s_rstd, 1)
                with dve.Fori(0, TRIOS) as i:
                    for j in range(TRIO):
                        t = i * TRIO + j
                        dve.wait_ge(s_xT_ps, t + 1)
                        dve.tensor_scalar(xs[j][:], resid[:, t, :], mean[:, ds(t, 1)], rstd[:, ds(t, 1)],
                                          ALU.subtract, ALU.mult).then_inc(s_xs, 1)
                dve.wait_ge(s_logit, TILES + TRIO)
                dve.wait_ge(s_const, 1)
                dve.wait_ge(s_w, 16 * 5)

                def wide(x):
                    return x[:, :, None].to_broadcast([P, TILES, EXPERTS])

                ch.step(dve.tensor_tensor(logits[:], ps_l[:, 0:TILES * EXPERTS].rearrange("p (t e) -> p t e", e=EXPERTS),
                                          rb[:, None, :].to_broadcast([P, TILES, EXPERTS]), ALU.add))
                for x, m, f, pick in ((logits, m1, f1, pick1), (second, m2, f2, pick2)):
                    ch.step(dve.tensor_reduce(m[:], x[:], AX_X, ALU.max))
                    ch.step(dve.tensor_tensor(eq[:], x[:], wide(m), ALU.is_equal))
                    ch.step(dve.tensor_tensor(eq[:], eq[:], first_wins[:, None, :].to_broadcast([P, TILES, EXPERTS]),
                                              ALU.mult))
                    ch.step(dve.tensor_reduce(f[:], eq[:], AX_X, ALU.max))
                    ch.step(dve.tensor_tensor(pick[:], eq[:], wide(f), ALU.is_equal))
                    if x is logits:
                        ch.step(dve.scalar_tensor_tensor(out=second[:], in0=pick1[:], scalar=-3e38, in1=logits[:],
                                                         op0=ALU.mult, op1=ALU.add))
                dve.tensor_tensor(dl[:], m2[:], m1[:], ALU.subtract).then_inc(s_dl, 1)
                dve.wait_ge(s_exp, 1)
                ch.step(dve.tensor_scalar(den[:], dl[:], 1.0, None, ALU.add))
                ch.step(dve.reciprocal(w1[:], den[:]))
                ch.mark(dve.tensor_tensor(w2[:], dl[:], w1[:], ALU.mult))
                ch.step(dve.tensor_tensor(cw[:], pick1[:], wide(w1), ALU.mult))
                ch.step(dve.tensor_tensor(pick2[:], pick2[:], wide(w2), ALU.mult))
                dve.tensor_tensor(cw[:], cw[:], pick2[:], ALU.add)

            @block.scalar
            def _(act):
                act.wait_ge(s_veps, 1)
                nc.scalar.activation(root[:], veps[:], ACT.Sqrt).then_inc(s_root, 1)
                act.sem_inc(s_xT, TRIO)
                with act.Fori(0, TRIOS) as i:
                    for j in range(TRIO):
                        t = i * TRIO + j
                        act.wait_ge(s_xT_ps, t + TRIO + 1)
                        act.wait_ge(s_logit, t + 1)
                        act.wait_ge(s_copy, t + 1)
                        nc.scalar.copy(xTs[j][:], ps_x[j][:, 0:P]).then_inc(s_xT, 1)
                act.wait_ge(s_dl, 1)
                nc.scalar.activation(dl[:], dl[:], ACT.Exp).then_inc(s_exp, 1)

            @block.tensor
            def _(pe):
                for s in (s_xT_ps, s_logit, s_copy):
                    pe.sem_inc(s, TRIO)
                pe.wait_ge(s_router, 16)
                with pe.Fori(0, TRIOS) as i:
                    for j in range(TRIO):
                        t = i * TRIO + j
                        pe.wait_ge(s_xs, t + 1)
                        pe.wait_ge(s_xT, t + 1)
                        nc.tensor.transpose(ps_x[j][:, 0:P], xs[j][:], ident[:]).then_inc(s_xT_ps, 1)
                    for j in range(TRIO):
                        t = i * TRIO + j
                        pe.wait_ge(s_xT, t + TRIO + 1)
                        nc.tensor.matmul(ps_l[:, ds(t * EXPERTS, EXPERTS)], xTs[j][:], router[:],
                                         start=True, stop=True).then_inc(s_logit, 1)

        with ExitStack() as main:
            ps_h1 = [main.enter_context(nc.psum_tensor(f"ex_ps_h1{j}", [P, 512], F32)) for j in range(HC)]
            ps_h2 = [main.enter_context(nc.psum_tensor(f"ex_ps_h2{j}", [P, 512], F32)) for j in range(HC)]
            ps_y = [main.enter_context(nc.psum_tensor(f"ex_ps_y{b}", [P, 512], F32)) for b in range(2)]
            ps_bias = main.enter_context(nc.psum_tensor("ex_ps_bias", [P, 512], F32))
            ps_cw = main.enter_context(nc.psum_tensor("ex_ps_cw", [P, 512], F32))
            W = TRIO * P
            compact = main.enter_context(nc.sbuf_tensor("ex_tables_compact", [P, SPLINES * 2 * QS], F32))
            rest = main.enter_context(nc.sbuf_tensor("ex_tables_rest", [P, SPLINES * 2 * QS], F32))
            parts = main.enter_context(nc.sbuf_tensor("ex_tables_parts", [P, PARTS, SPLINES * 2 * QS], BF16))
            unit_mask = main.enter_context(nc.sbuf_tensor("ex_unit_mask", [P, HG], F32))
            s_tables = main.enter_context(nc.semaphore("ex_tables_loaded"))
            s_spread = main.enter_context(nc.semaphore("ex_tables_spread"))
            s_tchain = main.enter_context(nc.semaphore("ex_tables_chain"))
            block = main.enter_context(nc.Block())

            x_rows, _, s_zeroed = scratch
            zeros = main.enter_context(nc.sbuf_tensor("ex_zeros", [P, D], F32))
            s_zero = main.enter_context(nc.semaphore("ex_zeros_set"))

            @block.sync
            def _(sp):
                sp.dma_start(compact[:], a["spline_tables"]).then_inc(s_tables, 16)
                sp.wait_ge(s_zero, 1)
                sp.dma_start(x_rows.rearrange("(n p) d -> p n d", p=P),
                             zeros[:, None, :].to_broadcast([P, ROWS // P, D])).then_inc(s_zeroed, 16)
                sp.wait_ge(s_zeroed, 16)

            @block.gpsimd
            def _(pool):
                ch = Chain(pool, s_tchain)
                pool.memset(zeros[:], 0.0).then_inc(s_zero, 1)
                ch.step(pool.memset(unit_mask[:], 1.0))
                ch.step(pool.affine_select(out=unit_mask[:], in_=unit_mask[:], compare_op=ALU.is_ge, fill=0.0,
                                           base=0, pattern=[[-GRID, HG]], channel_multiplier=1))
                ch.step(pool.affine_select(out=unit_mask[:], in_=unit_mask[:], compare_op=ALU.is_ge, fill=0.0,
                                           base=GRID - 1, pattern=[[GRID, HG]], channel_multiplier=-1))
                spread_tables(pool, ch, compact, parts, rest, unit_mask, tables, s_spread, s_tables)

            @block.vector
            def _(dve):
                ch = Chain(dve, s_sum)
                dve.sem_inc(s_acc, 2)
                dve.sem_inc(s_a, HC)
                dve.sem_inc(s_init, 1)
                with dve.Fori(0, TRIOS) as i:
                    ch.enter(i, 2 * EXPERTS + 1 + TRIO)

                    def activated(e, j):
                        m = e * HC + j
                        dve.wait_ge(s_gate, i * STEPS + m + 1)
                        dve.wait_ge(s_h2, i * STEPS + m + 1)
                        dve.scalar_tensor_tensor(out=act_t[e % 2][j][:], in0=ps_h2[j][:, 0:W],
                                                 scalar=b1[:, e, HC + j:HC + j + 1], in1=gate[j][:],
                                                 op0=ALU.add, op1=ALU.mult).then_inc(s_a, 1)

                    def accumulate(e):
                        dve.wait_ge(s_y, i * EXPERTS + e + 1)
                        dve.wait_ge(s_acc, i * EXPERTS + e + 2)
                        ch.sync()
                        for s in range(TRIO):
                            out = acc[:, s, :] if e < EXPERTS - 1 else resid[:, i * TRIO + s, :]
                            ins = dve.scalar_tensor_tensor(out=out, in0=ps_y[e % 2][:, s * D:(s + 1) * D],
                                                           scalar=cws[:, s, e:e + 1], in1=acc[:, s, :],
                                                           op0=ALU.mult, op1=ALU.add)
                            if s < TRIO - 1:
                                ch.mark(ins)
                        ins.then_inc(s_acc, 1)

                    dve.wait_ge(s_acc, i * EXPERTS + 2)
                    dve.tensor_copy(cws[:], cw[:, ds(i * TRIO, TRIO), :]).then_inc(s_cws, 1)
                    activated(0, 0)
                    activated(0, 1)
                    activated(1, 0)
                    activated(1, 1)
                    dve.wait_ge(s_bias, i + 1)
                    dve.wait_ge(s_cws, i + 1)
                    ch.mark(dve.tensor_tensor(acc[:], ps_bias[:, 0:TRIO * D].rearrange("p (s d) -> p s d", s=TRIO),
                                              resid[:, ds(i * TRIO, TRIO), :], ALU.add))
                    ch.sync()
                    dve.sem_inc(s_init, 1)
                    for e in range(EXPERTS):
                        if e >= 1 and e + 1 < EXPERTS:
                            activated(e + 1, 0)
                            activated(e + 1, 1)
                        accumulate(e)
                    ch.sync()
                    dve.wait_ge(s_acc, (i + 1) * EXPERTS + 2)
                    dve.sem_inc(s_turns, 1)
                    tile_statistics(ch, stats, resid, [i * TRIO + s for s in range(TRIO)])
                    ch.leave(TRIOS)

            @block.scalar
            def _(act):
                act.sem_inc(s_cwT, 1)
                with act.Fori(0, TRIOS) as i:
                    for e in range(EXPERTS):
                        for j in range(HC):
                            m = e * HC + j
                            act.wait_ge(s_h1, i * STEPS + m + 1)
                            act.wait_ge(s_a, i * STEPS + m + 1)
                            nc.scalar.activation(gate[j][:], ps_h1[j][:, 0:W], ACT.Silu,
                                                 bias=b1[:, e, j:j + 1]).then_inc(s_gate, 1)
                        if e == 0:
                            act.wait_ge(s_cwT_ps, i + 1)
                            nc.scalar.copy(cwT[0:EXPERTS, :], ps_cw[0:EXPERTS, 0:W]).then_inc(s_cwT, 1)

            @block.tensor
            def _(pe):
                with pe.Fori(0, TRIOS) as i:
                    x = xT[:, ds(i * W, W)]

                    def hidden(e):
                        for j in range(HC):
                            pe.wait_ge(s_a, i * STEPS + e * HC + j + 1)
                            nc.tensor.matmul(ps_h1[j][:, 0:W], fc1[:, e, j * P:(j + 1) * P], x,
                                             start=True, stop=True).then_inc(s_h1, 1)
                            nc.tensor.matmul(ps_h2[j][:, 0:W], fc1[:, e, HIDDEN + j * P:HIDDEN + (j + 1) * P], x,
                                             start=True, stop=True).then_inc(s_h2, 1)

                    def outputs(e):
                        pe.wait_ge(s_a, i * STEPS + e * HC + HC + HC)
                        pe.wait_ge(s_acc, i * EXPERTS + e + 1)
                        for s in range(TRIO):
                            for j in range(HC):
                                mm = nc.tensor.matmul(ps_y[e % 2][:, s * D:(s + 1) * D],
                                                      act_t[e % 2][j][:, s * P:(s + 1) * P], fc2[:, e, j, :],
                                                      start=(j == 0), stop=(j == HC - 1))
                        mm.then_inc(s_y, 1)

                    hidden(0)
                    pe.wait_ge(s_cws, i + 1)
                    pe.wait_ge(s_cwT, i + 1)
                    for s in range(TRIO):
                        mm = nc.tensor.transpose(ps_cw[0:EXPERTS, s * P:(s + 1) * P], cws[:, s, :], ident[:])
                    mm.then_inc(s_cwT_ps, 1)
                    hidden(1)
                    pe.wait_ge(s_cwT, i + 2)
                    pe.wait_ge(s_init, i + 1)
                    for s in range(TRIO):
                        mm = nc.tensor.matmul(ps_bias[:, s * D:(s + 1) * D], cwT[0:EXPERTS, s * P:(s + 1) * P],
                                              b2[0:EXPERTS, :], start=True, stop=True)
                    mm.then_inc(s_bias, 1)
                    for e in range(EXPERTS):
                        if e >= 1 and e + 1 < EXPERTS:
                            hidden(e + 1)
                        outputs(e)


def attention(nc, resid, ident, a, s_turns, stats, wd_sum):
    with ExitStack() as ctx:
        def sb(name, shape, dt=F32):
            return ctx.enter_context(nc.sbuf_tensor(name, shape, dt))

        def sem(name):
            return ctx.enter_context(nc.semaphore(name))

        def psum(name):
            return ctx.enter_context(nc.psum_tensor(name, [P, 512], F32))

        ps_x, ps_q, ps_k, ps_v, ps_s, ps_pt, ps_o, ps_c = (
            psum(f"at_ps_{n}") for n in ("x", "q", "k", "v", "scores", "probsT", "o", "cls"))
        w_qkv = sb("at_w_qkv", [P, 3, D])
        wd = sb("at_wd", [P, SPLINES, P])
        EACH = SPLINES // GROUPS
        mean, var, veps, root, rstd, t0, t1 = (
            sb(f"at_{n}", [P, TILES]) for n in ("mean", "var", "veps", "root", "rstd", "t0", "t1"))
        xs = sb("at_xs", [P, GT, D])
        warm = sb("at_warm", [P, 1])
        xT_cls = sb("at_xT_cls", [P, IMAGES, CLS])
        xT = sb("at_xT", [P, GROUP, SEQ])
        qT = sb("at_qT", [P, GROUP, SEQ])
        kT = sb("at_kT", [P, GROUP, SEQ])
        v = sb("at_v", [P, GROUP, D])
        top, rsum = sb("at_top", [P, GROUP]), sb("at_rsum", [P, GROUP])
        probs = sb("at_probs", [P, GROUP, SEQ])
        probsT = sb("at_probsT", [P, GROUP, SEQ])
        o_cls = sb("at_o_cls", [P, IMAGES, D])
        o_cls_rows = sb("at_o_cls_rows", [P, D])

        s_w = sem("at_weights")
        s_wd = sem("at_wd_loaded")
        s_dve = sem("at_dve_chain")
        s_veps = sem("at_variances_ready")
        s_root = sem("at_roots_ready")
        s_rstd = sem("at_rstd_ready")
        s_xs = sem("at_xs_ready")
        s_xT_ps = sem("at_xT_in_psum")
        s_xT = sem("at_xT_ready")
        s_xc = sem("at_xT_cls_ready")
        s_q_ps = sem("at_q_in_psum")
        s_k_ps = sem("at_k_in_psum")
        s_v_ps = sem("at_v_in_psum")
        s_q = sem("at_q_ready")
        s_k = sem("at_k_ready")
        s_v = sem("at_v_ready")
        s_s = sem("at_scores_ready")
        s_sub = sem("at_scores_taken")
        s_e = sem("at_exp_ready")
        s_p = sem("at_probs_ready")
        s_pT_ps = sem("at_probsT_in_psum")
        s_pT = sem("at_probsT_ready")
        s_o = sem("at_o_in_psum")
        s_h = sem("at_o_taken")
        s_c = sem("at_o_cls_taken")
        s_rows = sem("at_o_cls_rows_moved")

        def images(ps, rows=P):
            return ps[0:rows, 0:GROUP * SEQ].rearrange("p (i s) -> p i s", i=GROUP)

        LAST = GROUPS - 1
        block = ctx.enter_context(nc.Block())

        @block.sync
        def _(sp):
            sp.dma_start(w_qkv[:], a["w_qkv"]).then_inc(s_w, 16)
            sp.dma_start(wd[:], a["wd_sums"]).then_inc(s_wd, 16)
            sp.wait_ge(s_c, GROUPS + 1)
            for c in range(CLS):
                sp.dma_start(o_cls_rows[c::CLS, :], o_cls[c:c + 1, :, :]).then_inc(s_rows, 16)

        @block.gpsimd
        def _(pool):
            pool.wait_ge(s_xT, 1)
            with pool.Fori(0, GROUPS) as g:
                pool.wait_ge(s_v_ps, g + 1)
                pool.tensor_copy(xT[:, :, 0:CLS], xT_cls[:, ds(g * GROUP, GROUP), :]).then_inc(s_xc, 1)

        @block.vector
        def _(dve):
            ch = Chain(dve, s_dve, s_turns)
            ch.step(norm_statistics(dve, ch, stats, mean[:], var[:], (t0[:], t1[:])))
            rstd_steps(dve, ch, var[:], veps[:], root[:], t0[:], rstd[:], s_veps, s_root, 1).then_inc(s_rstd, 1)
            dve.wait_ge(s_rstd, 1)

            def normalise(slot, tile):
                return dve.tensor_scalar(xs[:, slot, :], resid[:, tile, :], mean[:, ds(tile, 1)], rstd[:, ds(tile, 1)],
                                         ALU.subtract, ALU.mult)

            def normalise_group(g):
                dve.wait_ge(s_xT_ps, g + 1)
                for t in range(GT - 1):
                    ch.mark(normalise(t, g * GT + t))
                ch.sync()
                normalise(GT - 1, g * GT + GT - 1).then_inc(s_xs, 1)

            def keep_values(g):
                dve.wait_ge(s_v_ps, g + 2)
                dve.tensor_copy(v[0:SEQ],
                                ps_v[0:SEQ, :].rearrange("p (i d) -> p i d", i=GROUP)).then_inc(s_v, 1)

            def wide(x):
                return x[0:SEQ, :, None].to_broadcast([SEQ, GROUP, SEQ])

            def softmax(g):
                dve.wait_ge(s_s, g + 1)
                ch.step(dve.tensor_reduce(top[0:SEQ, :], images(ps_s, SEQ), AX_X, ALU.max))
                dve.tensor_tensor(probs[0:SEQ], images(ps_s, SEQ), wide(top), ALU.subtract).then_inc(s_sub, 1)
                dve.wait_ge(s_e, g + 1)
                ch.step(dve.tensor_reduce(rsum[0:SEQ, :], probs[0:SEQ], AX_X, ALU.add))
                ch.step(dve.reciprocal(rsum[0:SEQ, :], rsum[0:SEQ, :]))
                dve.tensor_tensor(probs[0:SEQ], probs[0:SEQ], wide(rsum), ALU.mult).then_inc(s_p, 1)

            def group(g, more, second):
                if second:
                    normalise_group(g + 2)
                if more:
                    softmax(g + 1)
                now = ds(g * EACH, EACH)
                ch.mark(dve.tensor_reduce(wd_sum[:, now], wd[:, now, :], AX_X, ALU.add))
                dve.wait_ge(s_o, g + 1)
                if more:
                    keep_values(g + 1)
                tiles = resid[:, ds(g * GT, GT), :]
                dve.tensor_tensor(tiles, tiles, ps_o[:, 0:GT * D].rearrange("p (t d) -> p t d", t=GT),
                                  ALU.add).then_inc(s_h, 1)
                dve.wait_ge(s_h, g + 2)
                dve.sem_inc(s_turns, 1)
                tile_statistics(ch, stats, resid, [g * GT + t for t in range(GT)])

            normalise(0, PTILES).then_inc(s_xs, 1)
            normalise_group(0)
            keep_values(0)
            normalise_group(1)
            softmax(0)
            dve.wait_ge(s_wd, 16)
            with dve.Fori(0, LAST - 1) as g:
                ch.enter(g, 1 + GT + 3 + GT - 1)
                group(g, True, True)
                ch.leave(LAST - 1)
            group(LAST - 1, True, False)
            group(LAST, False, False)
            dve.wait_ge(s_rows, 16 * CLS)
            ch.step(dve.tensor_tensor(resid[:, PTILES, :], resid[:, PTILES, :], o_cls_rows[:], ALU.add))
            tile_statistics(ch, stats, resid, [PTILES])

        @block.scalar
        def _(act):
            def transposed(g):
                act.wait_ge(s_xT_ps, g + 2)
                nc.scalar.copy(xT[:, :, CLS:SEQ], ps_x[:, 0:GT * P].rearrange("p (i s) -> p i s", i=GROUP))\
                    .then_inc(s_xT, 1)

            def project(g):
                act.wait_ge(s_q_ps, g + 1)
                nc.scalar.copy(qT[:], images(ps_q)).then_inc(s_q, 1)
                act.wait_ge(s_k_ps, g + 1)
                nc.scalar.copy(kT[:], images(ps_k)).then_inc(s_k, 1)

            def exps(g):
                act.wait_ge(s_sub, g + 2)
                nc.scalar.activation(probs[0:SEQ], probs[0:SEQ], ACT.Exp, scale=1.0 / D ** 0.5).then_inc(s_e, 1)

            def group(g, more, second):
                if more:
                    project(g + 1)
                act.wait_ge(s_pT_ps, g + 1)
                nc.scalar.copy(probsT[0:SEQ], images(ps_pt, SEQ)).then_inc(s_pT, 1)
                if second:
                    transposed(g + 2)
                if more:
                    exps(g + 1)
                act.wait_ge(s_o, g + 1)
                nc.scalar.copy(o_cls[0:CLS, ds(g * GROUP, GROUP), :],
                               ps_c[0:CLS, :].rearrange("p (i d) -> p i d", i=GROUP)).then_inc(s_c, 1)

            act.wait_ge(s_veps, 1)
            nc.scalar.activation(root[:], veps[:], ACT.Sqrt).then_inc(s_root, 1)
            act.wait_ge(s_rstd, 1)
            nc.scalar.activation(warm[:, 0:1], rstd[:, 0:1], ACT.Exp)
            act.wait_ge(s_xT_ps, 1)
            nc.scalar.copy(xT_cls[:].rearrange("p i c -> p (i c)"), ps_x[:, 0:P]).then_inc(s_xT, 1)
            transposed(0)
            project(0)
            transposed(1)
            exps(0)
            with act.Fori(0, LAST - 1) as g:
                group(g, True, True)
            group(LAST - 1, True, False)
            group(LAST, False, False)

        @block.tensor
        def _(pe):
            def turn_x(g):
                pe.wait_ge(s_xs, g + 2)
                pe.wait_ge(s_xT, g + 1)
                for t in range(GT):
                    mm = nc.tensor.transpose(ps_x[:, t * P:(t + 1) * P], xs[:, t, :], ident[:])
                mm.then_inc(s_xT_ps, 1)

            def project(g):
                pe.wait_ge(s_xT, g + 2)
                pe.wait_ge(s_xc, g + 1)
                pe.wait_ge(s_q, g + 1)
                nc.tensor.matmul(images(ps_q), w_qkv[:, 0, :], xT[:], start=True, stop=True).then_inc(s_q_ps, 1)
                pe.wait_ge(s_k, g + 1)
                nc.tensor.matmul(images(ps_k), w_qkv[:, 1, :], xT[:], start=True, stop=True).then_inc(s_k_ps, 1)
                pe.wait_ge(s_v, g + 1)
                for i in range(GROUP):
                    mm = nc.tensor.matmul(ps_v[0:SEQ, i * D:(i + 1) * D], xT[:, i, :], w_qkv[:, 2, :],
                                          start=True, stop=True)
                mm.then_inc(s_v_ps, 1)

            def scores(g):
                pe.wait_ge(s_q, g + 2)
                pe.wait_ge(s_k, g + 2)
                pe.wait_ge(s_sub, g + 1)
                for i in range(GROUP):
                    mm = nc.tensor.matmul(images(ps_s, SEQ)[:, i, :], qT[:, i, :], kT[:, i, :], start=True, stop=True)
                mm.then_inc(s_s, 1)

            def group(g, more, second):
                if more:
                    project(g + 1)
                pe.wait_ge(s_p, g + 1)
                pe.wait_ge(s_pT, g + 1)
                for i in range(GROUP):
                    mm = nc.tensor.transpose(images(ps_pt, SEQ)[:, i, :], probs[0:SEQ, i, :], ident[0:SEQ, 0:SEQ])
                mm.then_inc(s_pT_ps, 1)
                if more:
                    scores(g + 1)
                if second:
                    turn_x(g + 2)
                pe.wait_ge(s_pT, g + 2)
                pe.wait_ge(s_v, g + 2)
                pe.wait_ge(s_h, g + 1)
                pe.wait_ge(s_c, g + 1)
                for i in range(GROUP):
                    values = v[0:SEQ, i, :]
                    rows = (i % 2) * PATCHES
                    nc.tensor.matmul(ps_o[rows:rows + PATCHES, (i // 2) * D:(i // 2 + 1) * D],
                                     probsT[0:SEQ, i, CLS:SEQ], values, start=True, stop=True)
                    mm = nc.tensor.matmul(ps_c[0:CLS, i * D:(i + 1) * D], probsT[0:SEQ, i, 0:CLS], values,
                                          start=True, stop=True)
                mm.then_inc(s_o, 1)

            for s in (s_v_ps, s_q, s_k, s_v, s_sub, s_pT, s_h, s_c):
                pe.sem_inc(s, 1)
            pe.wait_ge(s_w, 16)
            pe.wait_ge(s_xs, 1)
            nc.tensor.transpose(ps_x[:, 0:P], xs[:, 0, :], ident[:]).then_inc(s_xT_ps, 1)
            turn_x(0)
            project(0)
            turn_x(1)
            scores(0)
            with pe.Fori(0, LAST - 1) as g:
                group(g, True, True)
            group(LAST - 1, True, False)
            group(LAST, False, False)


SPLINES, CLUSTERS, PER_CLUSTER, GRID = 64, 8, 8, 16
BLOCK = 64
MAX_BLOCKS = (TILES * P + SPLINES * (BLOCK - 1)) // BLOCK
RING = 5
PAIRS = -(-MAX_BLOCKS // (2 * RING)) * RING
ROWS = PAIRS * 2 * BLOCK
BANK_TILES = 7
BANKS = -(-TILES // BANK_TILES)
KEYS = BANKS * BANK_TILES
HG = P // GRID
QS = P // HG
PARTS = 3


def spread_tables(pool, ch, compact, hi_lo, rest, unit_mask, tables, s_tab, tables_loaded):
    pool.wait_ge(tables_loaded, 16)
    ch.step(pool.tensor_copy(hi_lo[:, 0, :], compact[:]))
    for n in range(1, PARTS):
        ch.step(pool.tensor_tensor(rest[:], compact[:] if n == 1 else rest[:], hi_lo[:, n - 1, :], ALU.subtract))
        ch.step(pool.tensor_copy(hi_lo[:, n, :], rest[:]))
    with pool.Fori(0, SPLINES) as t:
        for n in range(PARTS):
            pool.tensor_tensor(tables[:, t, :, n, :, :],
                               hi_lo[:, n, ds(t * 2 * QS, 2 * QS)].rearrange("p (q c) -> p q c", c=2)[:, :, :, None]
                               .to_broadcast([P, QS, 2, HG]),
                               unit_mask[:, None, None, :].to_broadcast([P, QS, 2, HG]), ALU.mult).then_inc(s_tab, 1)


def splines(nc, resid, ident, a, scratch, out, spread, s_turns, stats, wd_sum):
    x_rows, y_rows, s_zeroed = scratch
    with ExitStack() as ctx:
        def sb(name, shape, dt=F32):
            return ctx.enter_context(nc.sbuf_tensor(name, shape, dt))

        def sem(name):
            return ctx.enter_context(nc.semaphore(name))

        gb_cols = sb("sp_gamma_beta", [P, 2])
        dest_i = sb("sp_dest_int", [P, TILES], U32)
        tile_of = sb("sp_tile_of_block", [P, 2 * P], I32)
        expand = sb("sp_expand", [P, QS, P], BF16)
        s_w = sem("sp_weights")
        s_dve = sem("sp_dve_chain")
        s_pool = sem("sp_pool_chain")
        s_scat = sem("sp_scattered")

        with ExitStack() as prep:
            def sb(name, shape, dt=F32):
                return prep.enter_context(nc.sbuf_tensor(name, shape, dt))

            ps_x = [prep.enter_context(nc.psum_tensor(f"sp_ps_x{j}", [P, 512], F32)) for j in range(TRIO)]
            ps_r = prep.enter_context(nc.psum_tensor("sp_ps_rank", [P, 5, 512], F32))
            pos_part, cl_sum = sb("sp_positive", [P, SPLINES]), sb("sp_cluster_sum", [P, CLUSTERS])
            sigs = sb("sp_signatures", [P, SPLINES + CLUSTERS], BF16)
            less_index = sb("sp_less_index", [P, SPLINES + CLUSTERS], BF16)
            sig_f = sb("sp_signatures_f", [P, SPLINES + CLUSTERS])
            mean, var, veps, root, rstd, t0, t1 = (
                sb(f"sp_{n}", [P, TILES]) for n in ("mean", "var", "veps", "root", "rstd", "t0", "t1"))
            xs = [sb(f"sp_xs{j}", [P, D]) for j in range(BANK_TILES)]
            xn = sb("sp_xn", [P, TILES, D])
            signs = [sb(f"sp_signs{j}", [P, P], BF16) for j in range(BANK_TILES)]
            c_key, t_key = sb("sp_cluster_key", [P, KEYS, CLUSTERS]), sb("sp_tile_key", [P, KEYS, SPLINES])
            c_max, t_max = sb("sp_cluster_max", [P, KEYS]), sb("sp_tile_max", [P, KEYS])
            chosen = sb("sp_chosen", [P, SPLINES, KEYS], BF16)
            so_far = sb("sp_so_far", [P, SPLINES, KEYS], BF16)
            after_first = sb("sp_after_first", [P, SPLINES, KEYS], BF16)
            start_blocks = sb("sp_start_blocks", [P, SPLINES], BF16)
            block_ones = sb("sp_block_ones", [P, P], BF16)
            minus_rest, ones = sb("sp_minus_rest", [P, P], BF16), sb("sp_ones", [P, P], BF16)
            count, whole, ends, starts = (sb(f"sp_{n}", [P, SPLINES]) for n in ("count", "whole", "ends", "starts"))
            count_i = sb("sp_count_int", [P, SPLINES], I32)
            zero64 = sb("sp_zero64", [P, SPLINES])
            rank = sb("sp_rank", [P, TILES, SPLINES])
            dest = sb("sp_dest", [P, TILES])
            first_row = sb("sp_first_row", [P, 2])
            past = sb("sp_past", [P, 2, SPLINES])
            block_tile = sb("sp_block_tile", [P, 2])

            def psem(name):
                return prep.enter_context(nc.semaphore(name))

            s_centred = psem("sp_stream_centred")
            s_const = psem("sp_constants")
            s_veps = psem("sp_variances_ready")
            s_root = psem("sp_roots_ready")
            s_rstd = psem("sp_rstd_ready")
            s_normed = psem("sp_stream_normed")
            s_sigs = psem("sp_signatures_ready")
            s_xs = psem("sp_xs_ready")
            s_xT_ps = psem("sp_xT_in_psum")
            s_sign = psem("sp_signs_ready")
            s_copy = psem("sp_xn_kept")
            s_score = psem("sp_scores_in_psum")
            s_taken = psem("sp_scores_taken")
            s_starts = psem("sp_starts_ready")
            s_chosen = psem("sp_chosen_ready")
            s_before = psem("sp_before_ready")
            s_rank = psem("sp_rank_in_psum")
            s_bt = psem("sp_block_tile_ready")
            s_bt_ps = psem("sp_block_tile_in_psum")
            s_dest = psem("sp_dest_ready")
            block = prep.enter_context(nc.Block())
            CH = 8
            WIDTH = SPLINES + CLUSTERS

            def bank_loop(eng, body):
                with eng.Fori(0, BANKS - 1) as i:
                    body(i, BANK_TILES)
                body(BANKS - 1, TILES - (BANKS - 1) * BANK_TILES)

            @block.sync
            def _(sp):
                sp.dma_start(gb_cols[:], a["gamma_beta"]).then_inc(s_w, 16)
            @block.gpsimd
            def _(pool):
                ch = Chain(pool, s_pool, s_turns)
                ch.mark(pool.memset(minus_rest[:], -1.0))
                ch.mark(pool.memset(after_first[:], 1.0))
                pool.memset(ones[:], 1.0).then_inc(s_const, 1)
                pool.memset(block_ones[:], float(BLOCK)).then_inc(s_const, 1)
                pool.memset(zero64[:], 0.0).then_inc(s_const, 1)
                ch.sync()
                pool.memset(after_first[:, :, 0], 0.0).then_inc(s_const, 1)
                pool.affine_select(out=minus_rest[:], in_=minus_rest[:], compare_op=ALU.is_ge, fill=0.0, base=0,
                                   pattern=[[-1, P]], channel_multiplier=1).then_inc(s_const, 1)
                pool.iota(less_index[:, 0:SPLINES].rearrange("p (c l) -> p c l", c=CLUSTERS),
                          pattern=[[0, CLUSTERS], [-1, PER_CLUSTER]], base=0, channel_multiplier=0,
                          allow_small_or_imprecise_dtypes=True).then_inc(s_const, 1)
                pool.iota(less_index[:, SPLINES:WIDTH], pattern=[[-1, CLUSTERS]], base=0, channel_multiplier=0,
                          allow_small_or_imprecise_dtypes=True).then_inc(s_const, 1)
                pool.iota(first_row[:], pattern=[[P * BLOCK, 2]], base=0, channel_multiplier=BLOCK,
                          allow_small_or_imprecise_dtypes=True).then_inc(s_const, 1)
                ch.step(pool.memset(expand[:], 1.0))
                ch.step(pool.affine_select(out=expand[:], in_=expand[:], compare_op=ALU.is_ge, fill=0.0, base=0,
                                           pattern=[[P, QS], [1, P]], channel_multiplier=-GRID))
                ch.step(pool.affine_select(out=expand[:], in_=expand[:], compare_op=ALU.is_ge, fill=0.0, base=GRID - 1,
                                           pattern=[[-P, QS], [-1, P]], channel_multiplier=GRID))
                for t in range(0, TILES, TILES // 3):
                    pool.wait_ge(s_normed, t + TILES // 3)
                    now = slice(t, t + TILES // 3)
                    ch.mark(pool.tensor_tensor(resid[:, now, :], resid[:, now, :], xn[:, now, :], ALU.add))
                ch.sync()

                def keep(i, n):
                    for j in range(n):
                        t = i * BANK_TILES + j
                        pool.wait_ge(s_xs, t + 1)
                        pool.tensor_copy(xn[:, t, :], xs[j][:]).then_inc(s_copy, 1)

                bank_loop(pool, keep)
                pool.wait_ge(s_dest, 1)
                pool.wait_ge(s_copy, TILES + BANK_TILES)
                pool.wait_ge(s_zeroed, 16)
                for t in range(TILES):
                    pool.indirect_dma_start(out=x_rows, out_offset=bass.IndirectOffsetOnAxis(ap=dest_i[:, t:t + 1], axis=0),
                                            in_=xn[:, t, :], in_offset=None).then_inc(s_scat, 16)
                pool.wait_ge(s_scat, 16 * TILES)

            @block.vector
            def _(dve):
                ch = Chain(dve, s_dve, s_turns)
                ch.step(norm_statistics(dve, ch, stats, mean[:], var[:], (t0[:], t1[:])))
                rstd_steps(dve, ch, var[:], veps[:], root[:], t0[:], rstd[:], s_veps, s_root, 1).then_inc(s_rstd, 1)
                dve.wait_ge(s_rstd, 1)
                dve.tensor_tensor(xn[:], resid[:], mean[:, :, None].to_broadcast([P, TILES, D]), ALU.subtract)\
                    .then_inc(s_centred, 1)
                for src, n, at in ((wd_sum, SPLINES, 0), (cl_sum, CLUSTERS, SPLINES)):
                    ch.step(dve.tensor_scalar(pos_part[:, 0:n], src[:], 0.0, None, ALU.is_gt))
                    ch.step(dve.scalar_tensor_tensor(out=sig_f[:, at:at + n], in0=src[:], scalar=0.0,
                                                     in1=pos_part[:, 0:n], op0=ALU.is_lt, op1=ALU.subtract))
                    ch.step(dve.tensor_scalar(sig_f[:, at:at + n], sig_f[:, at:at + n], -1.0, None, ALU.mult))
                    if at == 0:
                        ch.step(dve.tensor_reduce(cl_sum[:], sig_f[:, 0:SPLINES].rearrange("p (c l) -> p c l", c=CLUSTERS),
                                                  AX_X, ALU.add))
                dve.tensor_scalar(sigs[:], sig_f[:], float(PER_CLUSTER), None, ALU.mult).then_inc(s_sigs, 1)
                for t in range(TILES):
                    dve.wait_ge(s_normed, t + 1)
                    tile_statistics(ch, stats, xn, [t])
                ch.sync()
                ch.step(norm_statistics(dve, ch, stats, mean[:], var[:], (t0[:], t1[:])))
                rstd_steps(dve, ch, var[:], veps[:], root[:], t0[:], rstd[:], s_veps, s_root, 2).then_inc(s_rstd, 1)
                dve.wait_ge(s_rstd, 2)

                def normalise(i, n):
                    for j in range(n):
                        t = i * BANK_TILES + j
                        dve.wait_ge(s_xT_ps, t + 1)
                        dve.wait_ge(s_copy, t + 1)
                        dve.tensor_scalar(xs[j][:], xn[:, t, :], mean[:, ds(t, 1)], rstd[:, ds(t, 1)],
                                          ALU.subtract, ALU.mult).then_inc(s_xs, 1)

                bank_loop(dve, normalise)
                dve.wait_ge(s_taken, 2 * BANKS)
                dve.wait_ge(s_const, 8)
                ch.step(dve.tensor_reduce(c_max[:], c_key[:], AX_X, ALU.max))
                ch.step(dve.tensor_tensor(c_key[:], c_key[:], c_max[:, :, None].to_broadcast([P, KEYS, CLUSTERS]),
                                          ALU.is_equal))
                keys = t_key[:].rearrange("p t (c l) -> p (t c) l", l=PER_CLUSTER)
                ch.step(dve.scalar_tensor_tensor(out=keys, in0=c_key[:].rearrange("p t c -> p (t c)")[:, :, None]
                                                 .to_broadcast([P, KEYS * CLUSTERS, PER_CLUSTER]), scalar=4096.0,
                                                 in1=keys, op0=ALU.mult, op1=ALU.add))
                ch.step(dve.tensor_reduce(t_max[:], t_key[:], AX_X, ALU.max))
                dve.tensor_tensor(chosen[:].rearrange("p s t -> p t s"), t_key[:],
                                  t_max[:, :, None].to_broadcast([P, KEYS, SPLINES]), ALU.is_equal).then_inc(s_chosen, 1)
                dve.wait_ge(s_chosen, 1)
                ch.step(dve.tensor_tensor_scan(so_far[:].rearrange("p s t -> p (s t)"),
                                               after_first[:].rearrange("p s t -> p (s t)"),
                                               chosen[:].rearrange("p s t -> p (s t)"), 0.0, ALU.mult, ALU.add))
                dve.sem_inc(s_before, 1)
                dve.wait_ge(s_rank, 1)
                ch.step(dve.tensor_scalar(count_i[:], ps_x[0][:, 0:SPLINES], float(BLOCK - 1), None, ALU.add))
                ch.step(dve.tensor_scalar(count_i[:], count_i[:], -BLOCK, None, ALU.bitwise_and))
                ch.step(dve.tensor_copy(whole[:], count_i[:]))
                ch.step(dve.tensor_tensor_scan(ends[:], whole[:], zero64[:], 0.0, ALU.add, ALU.add))
                ch.step(dve.tensor_tensor(starts[:], ends[:], whole[:], ALU.subtract))
                dve.tensor_scalar(start_blocks[:], starts[:], 1.0 / BLOCK, None, ALU.mult).then_inc(s_starts, 1)
                ch.step(dve.tensor_tensor(past[:], ends[:, None, :].to_broadcast([P, 2, SPLINES]),
                                          first_row[:, :, None].to_broadcast([P, 2, SPLINES]), ALU.is_le))
                ch.step(dve.tensor_reduce(block_tile[:], past[:], AX_X, ALU.add))
                dve.tensor_scalar(block_tile[:], block_tile[:], float(SPLINES - 1), None, ALU.min).then_inc(s_bt, 1)
                for c in range(5):
                    n = min(CH, TILES - c * CH)
                    dve.wait_ge(s_rank, c + 2)
                    ch.mark(dve.tensor_tensor(rank[:, c * CH:c * CH + n, :],
                                              ps_r[:, c, 0:n * SPLINES].rearrange("p (t s) -> p t s", t=n),
                                              chosen[:, :, c * CH:c * CH + n].rearrange("p s t -> p t s"), ALU.mult))
                ch.sync()
                ch.step(dve.tensor_reduce(dest[:], rank[:], AX_X, ALU.add))
                dve.tensor_copy(dest_i[:], dest[:]).then_inc(s_dest, 1)
                dve.wait_ge(s_bt_ps, 1)
                dve.tensor_copy(tile_of[0:1, :], ps_x[1][0:1, 0:2 * P])

            @block.scalar
            def _(act):
                act.sem_inc(s_sign, TRIO)
                act.wait_ge(s_w, 16)
                act.wait_ge(s_veps, 1)
                nc.scalar.activation(root[:], veps[:], ACT.Sqrt).then_inc(s_root, 1)
                act.wait_ge(s_centred, 1)
                for t in range(TILES):
                    nc.scalar.activation(xn[:, t, :], xn[:, t, :], ACT.Identity, scale=rstd[:, t:t + 1])\
                        .then_inc(s_normed, 1)

                act.wait_ge(s_veps, 2)
                nc.scalar.activation(root[:], veps[:], ACT.Sqrt).then_inc(s_root, 1)

                def take_signs(i, n):
                    for j in range(n):
                        t = i * BANK_TILES + j
                        act.wait_ge(s_xT_ps, t + BANK_TILES + 1)
                        act.wait_ge(s_score, t + 1)
                        nc.scalar.activation(signs[j][:], ps_x[j % TRIO][:, 0:P], ACT.Sign, bias=gb_cols[:, 1:2],
                                             scale=gb_cols[:, 0:1]).then_inc(s_sign, 1)
                    act.wait_ge(s_score, (i + 1) * BANK_TILES + BANK_TILES)
                    scores = ps_r[:, i, 0:BANK_TILES * WIDTH].rearrange("p (t s) -> p t s", t=BANK_TILES)
                    now = ds(i * BANK_TILES, BANK_TILES)
                    nc.scalar.copy(t_key[:, now, :], scores[:, :, 0:SPLINES]).then_inc(s_taken, 1)
                    nc.scalar.copy(c_key[:, now, :], scores[:, :, SPLINES:WIDTH]).then_inc(s_taken, 1)

                bank_loop(act, take_signs)

            @block.tensor
            def _(pe):
                for s in (s_xT_ps, s_copy, s_score):
                    pe.sem_inc(s, BANK_TILES)
                pe.wait_ge(s_sigs, 1)
                pe.wait_ge(s_const, 8)

                def turn_and_score(i, n):
                    def score(j):
                        if j < n:
                            pe.wait_ge(s_sign, i * BANK_TILES + j + TRIO + 1)
                        out = ps_r[:, i, j * WIDTH:(j + 1) * WIDTH]
                        nc.tensor.matmul(out, signs[min(j, n - 1)][:], sigs[:], start=True, stop=False)
                        nc.tensor.matmul(out, ones[0:1, :], less_index[0:1, :], start=False, stop=True)\
                            .then_inc(s_score, 1)

                    for j in range(n):
                        t = i * BANK_TILES + j
                        pe.wait_ge(s_xs, t + 1)
                        since = TRIO if j >= TRIO else 1 + j + (BANK_TILES - 1 - j) % TRIO
                        pe.wait_ge(s_sign, t - since + 1 + TRIO)
                        nc.tensor.transpose(ps_x[j % TRIO][:, 0:P], xs[j][:], ident[:]).then_inc(s_xT_ps, 1)
                        if j >= 2:
                            score(j - 2)
                    for j in range(n - 2, BANK_TILES):
                        score(j)

                bank_loop(pe, turn_and_score)
                pe.wait_ge(s_before, 1)
                pe.wait_ge(s_taken, 2 * BANKS)
                nc.tensor.matmul(ps_x[0][:, 0:SPLINES], ones[:], so_far[:, :, TILES - 1], start=True, stop=True)\
                    .then_inc(s_rank, 1)
                for c in range(5):
                    n = min(CH, TILES - c * CH)
                    nc.tensor.matmul(ps_r[:, c, 0:n * SPLINES], minus_rest[:],
                                     chosen[:, :, c * CH:c * CH + n].rearrange("p s t -> p t s"),
                                     start=True, stop=False)
                    nc.tensor.matmul(ps_r[:, c, 0:n * SPLINES], ones[:],
                                     so_far[:, :, c * CH:c * CH + n].rearrange("p s t -> p t s"),
                                     start=False, stop=False)
                pe.wait_ge(s_starts, 1)
                for c in range(5):
                    n = min(CH, TILES - c * CH)
                    nc.tensor.matmul(ps_r[:, c, 0:n * SPLINES], block_ones[0:1, :],
                                     start_blocks[0:1, None, :].to_broadcast([1, n, SPLINES]),
                                     start=False, stop=True).then_inc(s_rank, 1)
                pe.wait_ge(s_bt, 1)
                for c in range(2):
                    mm = nc.tensor.matmul(ps_x[1][0:1, c * P:(c + 1) * P], block_tile[:, c:c + 1], ident[:],
                                          start=True, stop=True)
                mm.then_inc(s_bt_ps, 1)

        spline_blocks(nc, resid, ident, a, scratch, spread, gb_cols, tile_of, expand)

        with ExitStack() as last:
            got = last.enter_context(nc.sbuf_tensor("sp_gathered", [P, TILES, D], F32))
            cuts = [0, 8, 16, 24, TILES]
            s_got = [last.enter_context(nc.semaphore(f"sp_rows_gathered{n}")) for n in range(len(cuts) - 1)]
            s_sum = last.enter_context(nc.semaphore("sp_rows_added"))
            s_out = last.enter_context(nc.semaphore("sp_stored"))
            block = last.enter_context(nc.Block())

            @block.gpsimd
            def _(pool):
                for t in range(TILES):
                    pool.indirect_dma_start(out=got[:, t, :], out_offset=None, in_=y_rows,
                                            in_offset=bass.IndirectOffsetOnAxis(ap=dest_i[:, t:t + 1], axis=0))\
                        .then_inc(s_got[sum(t >= c for c in cuts[1:])], 16)

            @block.vector
            def _(dve):
                for t0, t1 in zip(cuts, cuts[1:]):
                    dve.wait_ge(s_got[cuts.index(t0)], 16 * (t1 - t0))
                    dve.tensor_tensor(got[:, t0:t1, :], got[:, t0:t1, :], resid[:, t0:t1, :], ALU.add)\
                        .then_inc(s_sum, 1)

            @block.sync
            def _(sp):
                tiles = out.rearrange("(t i) s d -> i s t d", i=2)
                for n, (t0, t1) in enumerate(zip(cuts, cuts[1:])):
                    sp.wait_ge(s_sum, n + 1)
                    t1 = min(t1, PTILES)
                    for i in range(2):
                        sp.dma_start(tiles[i, CLS:SEQ, t0:t1, :], got[i * PATCHES:(i + 1) * PATCHES, t0:t1, :])\
                            .then_inc(s_out, 16)
                sp.dma_start(out[:, 0:CLS, :], got[:, PTILES, :]).then_inc(s_out, 16)
                sp.wait_ge(s_out, 16 * (2 * len(cuts) - 1))


def spline_blocks(nc, resid, ident, a, scratch, tables, gb_cols, tile_of, expand):
    x_rows, y_rows, _ = scratch
    with ExitStack() as ctx:
        def sb(name, shape, dt=F32):
            return ctx.enter_context(nc.sbuf_tensor(name, shape, dt))

        def ring(name, shape, dt=F32):
            return [sb(f"bl_{name}{z}", shape, dt) for z in range(RING)]

        def sem(name):
            return ctx.enter_context(nc.semaphore(name))

        def psum(name, shape):
            return ctx.enter_context(nc.psum_tensor(name, shape, F32))

        CHUNKS = 4
        QB = QS // CHUNKS
        ps_r = psum("bl_ps_spread", [P, 2, 512])
        ps_l = psum("bl_ps_looked_up", [P, 2, 512])
        ps_x = psum("bl_ps_x", [P, 512])
        ps_h = psum("bl_ps_h", [P, 512])
        ps_t = psum("bl_ps_t", [P, 512])
        ps_y = psum("bl_ps_y", [P, 512])
        grid = sb("bl_grid", [P, 1])
        grid_i = sb("bl_grid_i", [P, 1], I32)
        x = ring("x", [P, D])
        w = [ring(f"w{b}_", [P, 2 * P + 2]) for b in range(2)]
        table = [ring(f"table{b}_", [P, QS, PARTS, 2 * HG], BF16) for b in range(2)]
        xT, sig, pos, posT, hs, hsT, y = (ring(n, [P, P]) for n in ("xT", "sig", "pos", "posT", "hs", "hsT", "y"))
        at = ring("at", [P, P], BF16)
        r, above, tmp = (sb(f"bl_{n}", [P, P]) for n in ("r", "above", "tmp"))
        hot = sb("bl_hot", [P, QS, P], BF16)
        looked = sb("bl_looked", [P, QS, 2, HG])

        s_const = sem("bl_constants")
        s_dve = sem("bl_dve_chain")
        s_ld = [sem(f"bl_loaded{z}") for z in range(RING)]
        s_tab = sem("bl_table_ready")
        s_xT_ps = sem("bl_xT_in_psum")
        s_xT = sem("bl_xT_ready")
        s_h = sem("bl_h_in_psum")
        s_sig = sem("bl_sigmoid_ready")
        s_at = sem("bl_cell_ready")
        s_pos = sem("bl_position_ready")
        s_r = sem("bl_spread_in_psum")
        s_hot = sem("bl_hot_ready")
        s_posT_ps = sem("bl_posT_in_psum")
        s_posT = sem("bl_posT_ready")
        s_look = sem("bl_looked_up")
        s_taken = sem("bl_looked_up_taken")
        s_hs = sem("bl_hs_ready")
        s_hsT_ps = sem("bl_hsT_in_psum")
        s_hsT = sem("bl_hsT_ready")
        s_y = sem("bl_y_in_psum")
        s_yh = sem("bl_y_half_ready")
        s_yev = sem("bl_y_ready")
        s_st = [sem(f"bl_stored{z}") for z in range(RING)]
        TURNS = PAIRS // RING
        MAGIC = 8388608.0
        halves = [slice(b * BLOCK, (b + 1) * BLOCK) for b in range(2)]
        block = ctx.enter_context(nc.Block())

        def in_turns(eng, step):
            step(0, lambda k: k % RING, lambda k: k // RING, False)
            with eng.Fori(0, TURNS - 1) as i:
                for j in range(1, RING + 1):
                    step(i * RING + j, lambda k, j=j: (j + k) % RING, lambda k, j=j: i + (j + k) // RING, i)
            for p in range(PAIRS - RING + 1, PAIRS):
                step(p, lambda k, p=p: (p + k) % RING, lambda k, p=p: (p + k) // RING, False)

        @block.sync
        def _(sp):
            with sp.Fori(0, TURNS) as i:
                for z in range(RING):
                    p = i * RING + z
                    ts = [sp.value_load(tile_of[0:1, ds(p * 2 + b, 1)], min_val=0, max_val=SPLINES - 1) for b in range(2)]
                    sp.wait_ge(s_yev, p + 1)
                    sp.dma_start(x[z][:], x_rows[ds(p * P, P), :]).then_inc(s_ld[z], 16)
                    for b in range(2):
                        sp.dma_start(w[b][z][:], a["spline_w"][ts[b]]).then_inc(s_ld[z], 16)

        @block.gpsimd
        def _(pool):
            pool.iota(grid_i[:], pattern=[[0, 1]], base=0, channel_multiplier=1).then_inc(s_const, 1)
            with pool.Fori(0, TURNS) as i:
                for z in range(RING):
                    p = i * RING + z
                    for b in range(2):
                        t = pool.value_load(tile_of[0:1, ds(p * 2 + b, 1)], min_val=0, max_val=SPLINES - 1)
                        if b == 0:
                            pool.wait_ge(s_look, p * 2 + 2)
                        pool.tensor_copy(table[b][z][:].rearrange("p q n c -> p (q n c)").bitcast(U32),
                                         tables[:, t].rearrange("p q n c u -> p (q n c u)").bitcast(U32))\
                            .then_inc(s_tab, 1)

        @block.vector
        def _(dve):
            ch = Chain(dve, s_dve)
            dve.wait_ge(s_const, 1)
            ch.step(dve.tensor_scalar(grid_i[:], grid_i[:], GRID - 1, None, ALU.bitwise_and))
            ch.step(dve.tensor_copy(grid[:], grid_i[:]))

            def positions(p, z, part):
                if part == 0:
                    dve.wait_ge(s_sig, p + 1)
                    ch.mark(dve.tensor_scalar(r[:], sig[z][:], float(GRID), MAGIC, ALU.mult, ALU.add))
                elif part == 1:
                    ch.sync()
                    ch.mark(dve.tensor_scalar(r[:], r[:], MAGIC, float(GRID - 1), ALU.subtract, ALU.min))
                elif part == 2:
                    ch.sync()
                    ch.mark(dve.scalar_tensor_tensor(out=above[:], in0=sig[z][:], scalar=float(GRID), in1=r[:],
                                                     op0=ALU.mult, op1=ALU.is_lt))
                    ch.sync()
                    dve.tensor_tensor(at[z][:], r[:], above[:], ALU.subtract).then_inc(s_at, 1)
                else:
                    dve.wait_ge(s_at, p + 1)
                    dve.scalar_tensor_tensor(out=pos[z][:], in0=sig[z][:], scalar=float(GRID), in1=at[z][:],
                                             op0=ALU.mult, op1=ALU.subtract).then_inc(s_pos, 1)

            def step(p, z, turn, i):
                more = not isinstance(p, int) or p + 1 < PAIRS
                for c in range(CHUNKS):
                    dve.wait_ge(s_r, p * CHUNKS + c + 1)
                    dve.tensor_scalar(hot[:, c * QB:(c + 1) * QB, :], ps_r[:, c % 2, :].rearrange("p (q n) -> p q n", q=QB),
                                      grid[:], None, ALU.is_equal).then_inc(s_hot, 1)
                    if more and c > 0:
                        positions(p + 1, z(1), c - 1)
                if more:
                    positions(p + 1, z(1), 3)
                for half in range(2):
                    dve.wait_ge(s_look, p * 2 + 2 * RING + half + 1)
                    ch.mark(dve.tensor_reduce(
                        looked[:, half * QS // 2:(half + 1) * QS // 2].rearrange("p q c u -> p q (c u)"),
                        ps_l[:, half, 0:QS // 2 * PARTS * 2 * HG].rearrange("p (q n k) -> p q k n", q=QS // 2, n=PARTS),
                        AX_X, ALU.add))
                ch.sync()
                dve.sem_inc(s_taken, 1)
                dve.wait_ge(s_posT, p + 1)
                ch.step(dve.tensor_tensor(tmp[:].rearrange("p (q u) -> p q u", u=HG), looked[:, :, 1, :],
                                          posT[z(0)][:].rearrange("p (q u) -> p q u", u=HG), ALU.mult))
                dve.tensor_tensor(hs[z(0)][:].rearrange("p (q u) -> p q u", u=HG), looked[:, :, 0, :],
                                  tmp[:].rearrange("p (q u) -> p q u", u=HG), ALU.add).then_inc(s_hs, 1)

            for part in range(4):
                positions(0, 0, part)
            step(0, lambda k: k, None, False)
            with dve.Fori(0, TURNS - 1) as i:
                ch.enter(i, RING * 6)
                for j in range(1, RING + 1):
                    step(i * RING + j, lambda k, j=j: (j + k) % RING, None, i)
                ch.leave(TURNS - 1)
            for p in range(PAIRS - RING + 1, PAIRS):
                step(p, lambda k, p=p: (p + k) % RING, None, False)

        @block.scalar
        def _(act):
            for z in range(RING):
                act.sem_inc(s_st[z], 16)

            def normed(p, z):
                act.wait_ge(s_xT_ps, p + 1)
                nc.scalar.activation(xT[z][:], ps_x[:, 0:P], ACT.Identity, bias=gb_cols[:, 1:2],
                                     scale=gb_cols[:, 0:1]).then_inc(s_xT, 1)

            def hidden(p, z):
                act.wait_ge(s_h, p + 1)
                nc.scalar.activation(sig[z][:], ps_h[:, 0:P], ACT.Sigmoid).then_inc(s_sig, 1)

            def finish(p, z, turn):
                act.wait_ge(s_hsT_ps, p + 1)
                nc.scalar.copy(hsT[z][:], ps_t[:, P:2 * P]).then_inc(s_hsT, 1)
                act.wait_ge(s_y, p + 1)
                act.wait_ge(s_st[z], turn * 16 + 16)
                for b in range(2):
                    nc.scalar.activation(y[z][halves[b], :], ps_y[halves[b], 0:D], ACT.Identity,
                                         scale=w[b][z][halves[b], 2 * P:2 * P + 1]).then_inc(s_yh, 1)
                act.wait_ge(s_yh, p * 2 + 2)
                act.sem_inc(s_yev, 1)
                act.dma_start(y_rows[ds(p * P, P), :], y[z][:]).then_inc(s_st[z], 16)

            def step(p, z, turn, i):
                known = isinstance(p, int)
                if not known or p + 1 < PAIRS:
                    hidden(p + 1, z(1))
                if not known or p + 2 < PAIRS:
                    normed(p + 2, z(2))
                if not known or p > 0:
                    finish(p - 1, z(-1), turn(-1))
                act.wait_ge(s_posT_ps, p + 1)
                nc.scalar.copy(posT[z(0)][:], ps_t[:, 0:P]).then_inc(s_posT, 1)

            normed(0, 0)
            normed(1, 1)
            hidden(0, 0)
            in_turns(act, step)
            finish(PAIRS - 1, (PAIRS - 1) % RING, (PAIRS - 1) // RING)
            for z in range(RING):
                act.wait_ge(s_st[z], 16 * (TURNS + 1))

        @block.tensor
        def _(pe):
            def transpose_x(p, z, turn):
                pe.wait_ge(s_ld[z], turn * 48 + 48)
                nc.tensor.transpose(ps_x[:, 0:P], x[z][:], ident[:]).then_inc(s_xT_ps, 1)

            def hidden(p, z):
                for b in range(2):
                    mm = nc.tensor.matmul(ps_h[:, halves[b]], w[b][z][:, 0:P], xT[z][:, halves[b]],
                                          start=True, stop=True)
                mm.then_inc(s_h, 1)

            def spread(p, z, c):
                pe.wait_ge(s_hot, p * CHUNKS + c + 1)
                for q in range(QB):
                    mm = nc.tensor.matmul(ps_r[:, c % 2, q * P:(q + 1) * P], expand[:, c * QB + q, :], at[z][:],
                                          start=True, stop=True)
                mm.then_inc(s_r, 1)

            def turn_hs(p, z):
                pe.wait_ge(s_hs, p + 1)
                nc.tensor.transpose(ps_t[:, P:2 * P], hs[z][:], ident[:]).then_inc(s_hsT_ps, 1)

            def finish(p, z):
                pe.wait_ge(s_hsT, p + 1)
                pe.wait_ge(s_yev, p + RING)
                for b in range(2):
                    mm = nc.tensor.matmul(ps_y[halves[b], 0:D], hsT[z][:, halves[b]], w[b][z][:, P:2 * P],
                                          start=True, stop=True)
                mm.then_inc(s_y, 1)

            def step(p, z, turn, i):
                known = isinstance(p, int)
                if not known or p + 1 < PAIRS:
                    pe.wait_ge(s_xT, p + 2)
                    pe.wait_ge(s_sig, p + 1)
                    hidden(p + 1, z(1))
                pe.wait_ge(s_at, p + 1)
                spread(p, z(0), 0)
                spread(p, z(0), 1)
                if not known or p + 2 < PAIRS:
                    transpose_x(p + 2, z(2), turn(2))
                if not known or p > 0:
                    turn_hs(p - 1, z(-1))
                spread(p, z(0), 2)
                if not known or p > 0:
                    finish(p - 1, z(-1))
                spread(p, z(0), 3)
                pe.wait_ge(s_pos, p + 1)
                nc.tensor.transpose(ps_t[:, 0:P], pos[z(0)][:], ident[:]).then_inc(s_posT_ps, 1)
                pe.wait_ge(s_tab, p * 2 + 2)
                pe.wait_ge(s_taken, p + 1)
                for c in range(CHUNKS):
                    pe.wait_ge(s_hot, p * CHUNKS + c + 3)
                    for q in range(c * QB, (c + 1) * QB):
                        at_q = slice(q % (QS // 2) * PARTS * 2 * HG, (q % (QS // 2) + 1) * PARTS * 2 * HG)
                        for b in range(2):
                            mm = nc.tensor.matmul(ps_l[halves[b], q // (QS // 2), at_q], hot[:, q, halves[b]],
                                                  table[b][z(0)][:, q].rearrange("p n c -> p (n c)"),
                                                  start=True, stop=True)
                    if c % 2 == 1:
                        mm.then_inc(s_look, 1)

            pe.sem_inc(s_yev, RING)
            pe.sem_inc(s_look, 2 * RING)
            pe.sem_inc(s_hot, 2)
            pe.sem_inc(s_taken, 1)
            transpose_x(0, 0, 0)
            pe.wait_ge(s_xT, 1)
            transpose_x(1, 1, 0)
            hidden(0, 0)
            in_turns(pe, step)
            turn_hs(PAIRS - 1, (PAIRS - 1) % RING)
            finish(PAIRS - 1, (PAIRS - 1) % RING)


def build(nc, a, out):
    with ExitStack() as ctx:
        resid = ctx.enter_context(nc.sbuf_tensor("resid", [P, TILES, D], F32))
        ident = ctx.enter_context(nc.sbuf_tensor("ident", [P, P], F32))
        tables = ctx.enter_context(nc.sbuf_tensor("tables", [P, SPLINES, QS, PARTS, 2, HG], BF16))
        stats = ctx.enter_context(nc.sbuf_tensor("token_stats", [P, TILES, 6], F32))
        wd_sum = ctx.enter_context(nc.sbuf_tensor("wd_sum", [P, SPLINES], F32))
        x_rows = nc.dram_tensor("x_rows", (ROWS, D), F32).ap()
        y_rows = nc.dram_tensor("y_rows", (ROWS, D), F32).ap()
        s_zeroed = ctx.enter_context(nc.semaphore("x_rows_zeroed"))
        s_turns = ctx.enter_context(nc.semaphore("turns"))
        scratch = (x_rows, y_rows, s_zeroed)
        with ExitStack() as setup:
            block = setup.enter_context(nc.Block())

            @block.gpsimd
            def _(pool):
                pool.memset(ident[:], 0.0).then_inc(s_turns, 1)
                pool.wait_ge(s_turns, 1)
                pool.affine_select(out=ident[:], in_=ident[:], compare_op=ALU.not_equal, fill=1.0,
                                   base=0, pattern=[[-1, P]], channel_multiplier=1)

        patch_attention(nc, resid, ident, a, s_turns, stats)
        experts(nc, resid, ident, a, tables, s_turns, stats, scratch)
        attention(nc, resid, ident, a, s_turns, stats, wd_sum)
        splines(nc, resid, ident, a, scratch, out, tables, s_turns, stats, wd_sum)


def kernel(**inputs):
    import numpy as np
    import concourse.bacc as bacc
    from concourse.bass_utils import run_bass_kernel_spmd as run

    v = {k: np.asarray(x) for k, x in inputs.items()}

    def flat(x, *shape):
        return np.ascontiguousarray(x.reshape(shape) if shape else x)

    x = v["x"].reshape(GROUPS, GT, 2, 3, 8, 28, 8, 28).transpose(0, 1, 3, 5, 7, 2, 4, 6)
    x = x.reshape(GROUPS, GT, PC, PK, P).transpose(0, 1, 3, 2, 4)
    arrays = {
        "x": flat(x),
        "w_patch": flat(v["L0_tok_W"].T.reshape(PC, PK, D).transpose(1, 0, 2)),
        "wq": flat(v["L0_attn_Wq"]), "wk": flat(v["L0_attn_Wk"]),
        "wv": flat(v["L0_attn_Wv"]), "wo": flat(v["L0_attn_Wo"]),
        "bias_cols": flat(np.stack([v["L0_attn_bq"], v["L0_attn_bk"], v["L0_attn_bv"]], 1)),
        "b_patch": flat(v["L0_tok_b"]),
        "bo": flat(v["L0_attn_bo"]),
        "cls_rows": flat(np.tile(np.stack([v["cls_tok"][0, 0], v["L0_tok_class_token"][0]]), (IMAGES, 1))),
        "cls_mul": flat(np.tile(np.stack([np.ones(D, np.float32), v["L0_tok_pos_embed"][0]]), (IMAGES, 1))),
        "pos": flat(v["L0_tok_pos_embed"][1:]),
        "gamma_beta": flat(np.stack([v["L1_ffn_gamma"], v["L1_ffn_beta"]], 1)),
        "wd_sums": flat(v["L1_ffn_Wd"].transpose(2, 0, 1)),
        "spline_w": flat(np.concatenate([v["L1_ffn_Wd"].transpose(0, 2, 1), v["L1_ffn_Wu"].transpose(0, 2, 1),
                                         np.tile(v["L1_ffn_scale"][:, None, None], (1, P, 2))], 2)),
        "spline_tables": flat(np.stack([v["L1_ffn_spline_bases"], v["L1_ffn_spline_slopes"]])
                              .reshape(2, SPLINES, QS, HG, GRID).transpose(3, 4, 1, 2, 0), P, SPLINES * 2 * QS),
        "w_qkv": flat(v["L1_attn_w_qkv"].reshape(D, 3, D)),
        "router": flat(v["L0_ffn_router_w"].T),
        "router_b": flat(v["L0_ffn_router_b"]),
        "fc1": flat(v["L0_ffn_fc1_w"].transpose(2, 0, 1)),
        "fc2": flat(v["L0_ffn_fc2_w"].reshape(EXPERTS, D, HC, P).transpose(3, 0, 2, 1)),
        "b1": flat(v["L0_ffn_fc1_b"].reshape(EXPERTS, 2 * HC, P).transpose(2, 0, 1)),
        "b2": flat(v["L0_ffn_fc2_b"]),
    }
    nc = bacc.Bacc("TRN2", target_bir_lowering=False, num_devices=1)
    aps = {n: nc.dram_tensor("in_" + n, x.shape, mybir.dt.from_np(x.dtype), kind="ExternalInput").ap()
           for n, x in arrays.items()}
    out = nc.dram_tensor("out", (IMAGES, SEQ, D), F32, kind="ExternalOutput").ap()
    build(nc, aps, out)
    r = run(nc, [{"in_" + n: x for n, x in arrays.items()}], core_ids=[0])
    return r.results[0]["out"]
```

```python
from contextlib import ExitStack

import concourse.bass as bass
from concourse import mybir

P = 128
IMAGES = 64
PATCHES = 64
CLS = 2
SEQ = CLS + PATCHES
D = 128
TILES = IMAGES * SEQ // P
PTILES = TILES - 1
GROUP = 4
GROUPS = IMAGES // GROUP
GT = GROUP * PATCHES // P
PK, PC = 112, 21
HEADS, DH = 8, 16
EPS = 1e-5

ALU = mybir.AluOpType
ACT = mybir.ActivationFunctionType
F32 = mybir.dt.float32
BF16 = mybir.dt.bfloat16
I32 = mybir.dt.int32
U32 = mybir.dt.uint32
AX_X = mybir.AxisListType.X
ds = bass.ds


class Marks:

    def __init__(self, sem):
        self.sem, self.count = sem, 0


class Chain:

    def __init__(self, eng, marks, turns=None):
        self.turns = turns
        self.eng, self.marked, self.made = eng, marks if isinstance(marks, Marks) else Marks(marks), 0

    def mark(self, ins):
        ins.then_inc(self.marked.sem, 1)
        self.marked.count = self.marked.count + 1
        self.made += 1
        return ins

    def sync(self):
        self.eng.wait_ge(self.marked.sem, self.marked.count)

    def apart(self):
        self.sync()
        self.eng.sem_inc(self.turns, 1)

    def step(self, ins):
        self.mark(ins)
        self.sync()

    def enter(self, i, marks):
        self.base, self.marks, self.made = self.marked.count, marks, 0
        self.marked.count = self.base + i * marks

    def leave(self, trips):
        assert self.made == self.marks, (self.made, self.marks)
        self.marked.count = self.base + trips * self.marks


def row_bc(dram_row):
    return dram_row.rearrange("(o d) -> o d", o=1).to_broadcast([P, dram_row.shape[0]])


def rsqrt_steps(pool, chain, var, minus_half, veps, t, r):
    g = pool
    chain.eng.sem_inc(chain.turns, 1)
    chain.step(g.tensor_scalar(veps, var, EPS, None, ALU.add))
    chain.step(g.tensor_tensor(r, veps, minus_half, ALU.pow))
    chain.step(g.tensor_tensor(t, r, r, ALU.mult))
    chain.step(g.tensor_tensor(t, t, veps, ALU.mult))
    chain.eng.sem_inc(chain.turns, 1)
    chain.step(g.tensor_scalar(t, t, -0.5, 1.5, ALU.mult, ALU.add))
    return g.tensor_tensor(r, r, t, ALU.mult)


RSQRT_MARKS = 5


def tile_statistics(ch, stats, x, tiles):
    for t in tiles:
        ch.mark(ch.eng.bn_stats(stats[:, t, :], x[:, t, :]))


def patch_attention(nc, resid, ident, a, s_turns, dve_marks, token_stats):
    with ExitStack() as ctx:
        def sb(name, shape, dt=F32):
            return ctx.enter_context(nc.sbuf_tensor(name, shape, dt))

        def psum(name, shape):
            return ctx.enter_context(nc.psum_tensor(name, shape, F32))

        def sem(name):
            return ctx.enter_context(nc.semaphore(name))

        ps_s = psum("pa_scores", [P, 2, 512])
        ps_pt = psum("pa_probsT", [P, 2, 512])
        ps_tok = psum("pa_tokens", [P, 512])
        ps_m0 = psum("pa_m0", [P, 512])
        ps_m1 = psum("pa_m1", [P, 512])
        ps_m2 = psum("pa_m2", [P, 512])

        w_patch = sb("pa_w_patch", [P, PC, D])
        x_patch = [sb(f"pa_x{t}", [P, PC, P]) for t in range(GT)]
        wq, wk, wv, wo = (sb(f"pa_w{n}", [P, D]) for n in "qkvo")
        bias_cols = sb("pa_bias_cols", [P, 3])
        b_patch = sb("pa_b_patch", [P, D])
        b_out = sb("pa_b_out", [P, D])
        pos = sb("pa_pos", [P, D])
        cls_mul = sb("pa_cls_mul", [P, D])
        head_mask = sb("pa_head_mask", [P, HEADS])
        diag125 = sb("pa_diag125", [P, SEQ], BF16)
        causal = sb("pa_causal", [P, 4, SEQ], BF16)
        minus_half = sb("pa_minus_half", [P, GT])
        stats = sb("pa_stats", [P, GT, 6])
        mv = sb("pa_mv", [P, GT, 2])
        veps, newton, rstd = (sb(f"pa_{n}", [P, GT]) for n in ("veps", "newton", "rstd"))
        xn = sb("pa_xn", [P, GT, D])
        xnT = sb("pa_xnT", [P, GROUP, SEQ])
        qT = sb("pa_qT", [P, GROUP, SEQ])
        kT = sb("pa_kT", [P, GROUP, SEQ])
        kbd = sb("pa_kbd", [P, GROUP, HEADS, SEQ])
        v1 = sb("pa_v1", [P, GROUP, HEADS, DH + 1])
        top = sb("pa_top", [P, GROUP, HEADS])
        probs = [sb(f"pa_probs{b}", [P, HEADS, SEQ]) for b in range(2)]
        probsT = [sb(f"pa_probsT{b}", [P, HEADS, SEQ]) for b in range(2)]
        rsum = sb("pa_rsum", [P, GROUP, HEADS])
        o_rows = sb("pa_o_rows", [P, GROUP, D])
        oT = sb("pa_oT", [P, GROUP * PATCHES])
        oT_cls = sb("pa_oT_cls", [P, IMAGES, CLS])

        s_w = sem("pa_weights")
        s_w2 = sem("pa_weights_act")
        s_wp = sem("pa_patch_weights")
        s_x = [sem(f"pa_x_loaded{t}") for t in range(GT)]
        s_xfree = [sem(f"pa_x_used{t}") for t in range(GT)]
        s_const = sem("pa_constants")
        s_pool = sem("pa_pool_chain")
        s_tok = sem("pa_tokens_taken")
        s_stats = sem("pa_stats_ready")
        s_rstd = sem("pa_rstd_ready")
        s_xn = sem("pa_xn_ready")
        s_xnT_ps = sem("pa_xnT_in_psum")
        s_xnT = sem("pa_xnT_ready")
        s_q_ps = sem("pa_q_in_psum")
        s_k_ps = sem("pa_k_in_psum")
        s_v_ps = sem("pa_v_in_psum")
        s_q = sem("pa_q_ready")
        s_k = sem("pa_k_ready")
        s_v = sem("pa_v_ready")
        s_kbd = sem("pa_kbd_ready")
        s_s = sem("pa_scores_ready")
        s_sub = sem("pa_scores_taken")
        s_p = sem("pa_probs_ready")
        s_pT_ps = sem("pa_probsT_in_psum")
        s_pT = sem("pa_probsT_ready")
        s_o_ps = sem("pa_o_in_psum")
        s_o = sem("pa_o_ready")
        s_oT_ps = sem("pa_oT_in_psum")
        s_oT = sem("pa_oT_ready")
        s_cls = sem("pa_oT_cls_kept")
        s_proj = sem("pa_projection_ready")
        s_bo = sem("pa_bias_added")
        s_h = sem("pa_projection_taken")

        scores = ps_s[0:SEQ, :, 0:4 * SEQ].rearrange("p b (h k) -> p b h k", h=4)
        probsT_ps = ps_pt[0:SEQ, :, 0:4 * SEQ].rearrange("p b (h k) -> p b h k", h=4)

        def rows(n):
            return n[:, 0:GROUP * SEQ].rearrange("p (i s) -> p i s", i=GROUP)

        def o_ps(i):
            return (ps_m1, ps_m2)[i % 2][0:SEQ, 0:HEADS * (DH + 1)].rearrange("p (h d) -> p h d", h=HEADS)

        LAST = GROUPS - 1

        block = ctx.enter_context(nc.Block())

        @block.sync
        def _(sp):
            sp.dma_start(w_patch[0:PK, :, :], a["w_patch"]).then_inc(s_wp, 16)
            for t in range(GT):
                sp.dma_start(x_patch[t][0:PK, :, :], a["x"][0, t]).then_inc(s_x[t], 16)
            with sp.Fori(1, GROUPS) as g:
                for t in range(GT):
                    sp.wait_ge(s_xfree[t], g)
                    sp.dma_start(x_patch[t][0:PK, :, :], a["x"][g, t]).then_inc(s_x[t], 16)

        @block.gpsimd
        def _(pool):
            ch = Chain(pool, s_pool, s_turns)
            ch.mark(pool.memset(head_mask[:], 1.0))
            ch.mark(pool.memset(diag125[:], 0.0))
            ch.mark(pool.memset(causal[:], 0.0))
            ch.sync()
            ch.step(pool.affine_select(out=head_mask[:], in_=head_mask[:], compare_op=ALU.is_ge, fill=0.0,
                                       base=0, pattern=[[-DH, HEADS]], channel_multiplier=1))
            pool.affine_select(out=head_mask[:], in_=head_mask[:], compare_op=ALU.is_ge, fill=0.0,
                               base=DH - 1, pattern=[[DH, HEADS]], channel_multiplier=-1).then_inc(s_const, 1)
            pool.affine_select(out=diag125[:], in_=diag125[:], compare_op=ALU.not_equal, fill=125.0,
                               base=0, pattern=[[-1, SEQ]], channel_multiplier=1).then_inc(s_const, 1)
            pool.affine_select(out=causal[:], in_=causal[:], compare_op=ALU.is_ge, fill=-800.0,
                               base=0, pattern=[[0, 4], [-1, SEQ]], channel_multiplier=1).then_inc(s_const, 1)
            pool.memset(v1[:], 1.0).then_inc(s_const, 1)
            pool.memset(minus_half[:], -0.5).then_inc(s_const, 1)
            pool.wait_ge(s_const, 5)

            def norm_scale(n):
                pool.wait_ge(s_stats, n)
                rsqrt_steps(pool, ch, mv[:, :, 1], minus_half[:], veps[:], newton[:], rstd[:]).then_inc(s_rstd, 1)

            def add_output_bias(g):
                pool.wait_ge(s_xn, g + 2)
                tiles = resid[:, ds(g * GT, GT), :]
                pool.tensor_tensor(tiles, tiles, b_out[:, None, :].to_broadcast([P, GT, D]),
                                   ALU.add).then_inc(s_bo, 1)

            def attention(g, more):
                pool.wait_ge(s_k, g + 1)
                for i in range(GROUP):
                    pool.wait_ge(s_s, g * GROUP + i + 1)
                    pool.tensor_tensor(kbd[:, i], kT[:, i, None, :].to_broadcast([P, HEADS, SEQ]),
                                       head_mask[:, :, None].to_broadcast([P, HEADS, SEQ]),
                                       ALU.mult).then_inc(s_kbd, 1)
                if more:
                    norm_scale(g + 3)
                    add_output_bias(g + 1)

            norm_scale(1)
            norm_scale(2)
            pool.wait_ge(s_w2, 16)
            pool.wait_ge(s_xn, 1)
            pool.tensor_tensor(resid[:, PTILES, :], resid[:, PTILES, :], b_out[:], ALU.add).then_inc(s_bo, 1)
            add_output_bias(0)
            with pool.Fori(0, LAST) as g:
                ch.enter(g, RSQRT_MARKS)
                attention(g, True)
                ch.leave(LAST)
            attention(LAST, False)

        @block.vector
        def _(dve):
            ch = Chain(dve, dve_marks, s_turns)

            def norm_apply(t, tile):
                return dve.tensor_scalar(xn[:, t, :], resid[:, tile, :], mv[:, t, 0:1], rstd[:, t:t + 1],
                                         ALU.subtract, ALU.mult)

            dve.wait_ge(s_w, 16 * 10)
            ch.step(dve.tensor_tensor(resid[:, PTILES, :], resid[:, PTILES, :], cls_mul[:], ALU.mult))
            for t in range(GT):
                ch.mark(dve.bn_stats(stats[:, t, :], resid[:, PTILES, :]))
            ch.sync()
            for t in range(GT):
                ins = dve.bn_aggr(mv[:, t, :], stats[:, t, :])
                if t < GT - 1:
                    ch.mark(ins)
            ch.sync()
            ins.then_inc(s_stats, 1)
            dve.wait_ge(s_rstd, 1)
            norm_apply(0, PTILES).then_inc(s_xn, 1)

            def tokens(g, n):
                tiles = resid[:, ds(g * GT, GT), :]
                dve.wait_ge(s_xfree[GT - 1], g + 1)
                dve.tensor_tensor(tiles, ps_tok[:, 0:GT * D].rearrange("p (t d) -> p t d", t=GT),
                                  b_patch[:, None, :].to_broadcast([P, GT, D]), ALU.add).then_inc(s_tok, 1)
                dve.wait_ge(s_tok, g + 1)
                ch.step(dve.tensor_tensor(tiles, tiles, pos[:, None, :].to_broadcast([P, GT, D]), ALU.mult))
                ch.apart()
                for t in range(GT):
                    ch.mark(dve.bn_stats(stats[:, t, :], resid[:, g * GT + t, :]))
                ch.apart()
                for t in range(GT - 1):
                    ch.mark(dve.bn_aggr(mv[:, t, :], stats[:, t, :]))
                dve.bn_aggr(mv[:, GT - 1, :], stats[:, GT - 1, :]).then_inc(s_stats, 1)

            TOKEN_MARKS = 1 + GT + GT - 1

            def normalise(g):
                dve.wait_ge(s_rstd, g + 2)
                dve.wait_ge(s_xnT_ps, g + 1)
                for t in range(GT - 1):
                    ch.mark(norm_apply(t, g * GT + t))
                ch.sync()
                norm_apply(GT - 1, g * GT + GT - 1).then_inc(s_xn, 1)

            def softmax(g, i):
                dve.wait_ge(s_s, (g + 1) * GROUP + i + 1)
                ch.step(dve.tensor_reduce(top[0:SEQ, i, :].rearrange("p (b h) -> p b h", b=2), scores, AX_X, ALU.max))
                dve.tensor_tensor(probs[i % 2][0:SEQ].rearrange("p (b h) k -> p b h k", b=2), scores,
                                  top[0:SEQ, i, :].rearrange("p (b h) -> p b h", b=2)[:, :, :, None]
                                  .to_broadcast([SEQ, 2, 4, SEQ]), ALU.subtract).then_inc(s_sub, 1)

            def divide(g, i):
                dve.wait_ge(s_o_ps, g * GROUP + i + 1)
                ch.step(dve.reciprocal(rsum[0:SEQ, i, :], o_ps(i)[:, :, DH]))
                dve.tensor_tensor(o_rows[0:SEQ, i, :].rearrange("p (h d) -> p h d", h=HEADS), o_ps(i)[:, :, 0:DH],
                                  rsum[0:SEQ, i, :, None].to_broadcast([SEQ, HEADS, DH]), ALU.mult).then_inc(s_o, 1)

            def attention(g, more):
                dve.wait_ge(s_v_ps, g + 1)
                dve.tensor_copy(v1[0:SEQ, :, :, 0:DH],
                                ps_m0[0:SEQ, :].rearrange("p (i h d) -> p i h d", i=GROUP, h=HEADS)).then_inc(s_v, 1)
                softmax(g, 0)
                softmax(g, 1)
                divide(g, 0)
                softmax(g, 2)
                divide(g, 1)
                if more:
                    tokens(g + 1, 0)
                softmax(g, 3)
                divide(g, 2)
                if more:
                    normalise(g + 1)
                divide(g, 3)
                dve.wait_ge(s_proj, g + 1)
                dve.wait_ge(s_bo, g + 2)
                tiles = resid[:, ds(g * GT, GT), :]
                dve.tensor_tensor(tiles, tiles, ps_m1[:, 0:GT * D].rearrange("p (t d) -> p t d", t=GT),
                                  ALU.add).then_inc(s_h, 1)
                dve.wait_ge(s_h, g + 2)
                dve.sem_inc(s_turns, 1)
                tile_statistics(ch, token_stats, resid, [g * GT + t for t in range(GT)])

            tokens(0, 0)
            normalise(0)
            dve.wait_ge(s_const, 5)
            with dve.Fori(0, LAST) as g:
                ch.enter(g, 2 * GROUP + TOKEN_MARKS + GT - 1 + GT)
                attention(g, True)
                ch.leave(LAST)
            attention(LAST, False)
            dve.wait_ge(s_proj, GROUPS + 1)
            dve.wait_ge(s_bo, GROUPS + 1)
            ch.step(dve.tensor_tensor(resid[:, PTILES, :], resid[:, PTILES, :], ps_m2[:, 0:D], ALU.add))
            tile_statistics(ch, token_stats, resid, [PTILES])

        @block.scalar
        def _(act):
            for dst, src in [(wq[:], a["wq"]), (wk[:], a["wk"]), (wv[:], a["wv"]), (wo[:], a["wo"]),
                             (bias_cols[:], a["bias_cols"]), (b_patch[:], row_bc(a["b_patch"])),
                             (resid[:, PTILES, :], a["cls_rows"]), (cls_mul[:], a["cls_mul"]),
                             (pos[0:PATCHES, :], a["pos"]), (pos[PATCHES:P, :], a["pos"])]:
                act.dma_start(dst, src).then_inc(s_w, 16)
            act.dma_start(b_out[:], row_bc(a["bo"])).then_inc(s_w2, 16)

            def norm_transposed(g):
                act.wait_ge(s_xnT_ps, g + 2)
                nc.scalar.copy(xnT[:, :, CLS:SEQ], ps_m0[:, 0:GT * P].rearrange("p (i s) -> p i s", i=GROUP))\
                    .then_inc(s_xnT, 1)

            def attention(g, more):
                act.wait_ge(s_q_ps, g + 1)
                nc.scalar.activation(qT[:], rows(ps_m1), ACT.Identity, bias=bias_cols[:, 0:1]).then_inc(s_q, 1)
                act.wait_ge(s_k_ps, g + 1)
                act.wait_ge(s_kbd, g * GROUP + 1)
                nc.scalar.activation(kT[:], rows(ps_m2), ACT.Identity, bias=bias_cols[:, 1:2]).then_inc(s_k, 1)
                for i in range(GROUP):
                    act.wait_ge(s_sub, g * GROUP + i + 2)
                    nc.scalar.activation(probs[i % 2][0:SEQ], probs[i % 2][0:SEQ], ACT.Exp,
                                         scale=1.0 / DH ** 0.5).then_inc(s_p, 1)
                    act.wait_ge(s_pT_ps, g * GROUP + i + 1)
                    nc.scalar.copy(probsT[i % 2][0:SEQ].rearrange("p (b h) k -> p b h k", b=2), probsT_ps)\
                        .then_inc(s_pT, 1)
                if more:
                    norm_transposed(g + 1)
                act.wait_ge(s_oT_ps, g + 1)
                nc.scalar.activation(oT_cls[:, ds(g * GROUP, GROUP), :], rows(ps_m0)[:, :, 0:CLS], ACT.Identity,
                                     bias=bias_cols[:, 2:3]).then_inc(s_cls, 1)
                nc.scalar.activation(oT[:].rearrange("p (i s) -> p i s", i=GROUP), rows(ps_m0)[:, :, CLS:SEQ],
                                     ACT.Identity, bias=bias_cols[:, 2:3]).then_inc(s_oT, 1)

            act.sem_inc(s_kbd, 1)
            act.wait_ge(s_xnT_ps, 1)
            nc.scalar.copy(xnT[:, :, 0:CLS], ps_m0[:, None, 0:CLS].to_broadcast([P, GROUP, CLS])).then_inc(s_xnT, 1)
            norm_transposed(0)
            act.wait_ge(s_w, 16 * 10)
            with act.Fori(0, LAST) as g:
                attention(g, True)
            attention(LAST, False)

        @block.tensor
        def _(pe):
            def patches(g, t, chunks):
                if chunks[0] == 0:
                    pe.wait_ge(s_x[t], 16 * (g + 1))
                    if t == 0 and not (isinstance(g, int) and g == 0):
                        pe.wait_ge(s_tok, g)
                for c in chunks:
                    mm = nc.tensor.matmul(ps_tok[:, t * D:(t + 1) * D], x_patch[t][0:PK, c, :], w_patch[0:PK, c, :],
                                          start=(c == 0), stop=(c == PC - 1))
                if chunks[-1] == PC - 1:
                    mm.then_inc(s_xfree[t], 1)

            def norm_transposes(g):
                pe.wait_ge(s_xn, g + 2)
                for t in range(GT):
                    mm = nc.tensor.transpose(ps_m0[:, t * P:(t + 1) * P], xn[:, t, :], ident[:])
                mm.then_inc(s_xnT_ps, 1)

            def qkv(g):
                pe.wait_ge(s_xnT, g + 2)
                pe.wait_ge(s_h, g + 1)
                nc.tensor.matmul(rows(ps_m1), wq[:], xnT[:], start=True, stop=True).then_inc(s_q_ps, 1)
                nc.tensor.matmul(rows(ps_m2), wk[:], xnT[:], start=True, stop=True).then_inc(s_k_ps, 1)
                for i in range(GROUP):
                    mm = nc.tensor.matmul(ps_m0[0:SEQ, i * D:(i + 1) * D], xnT[:, i, :], wv[:], start=True, stop=True)
                mm.then_inc(s_v_ps, 1)
                pe.wait_ge(s_q, g + 1)

            def score(g, i):
                pe.wait_ge(s_kbd, g * GROUP + i + 2)
                pe.wait_ge(s_sub, g * GROUP + i + 1)
                for b in range(2):
                    nc.tensor.matmul(scores[:, b], diag125[0:SEQ, :], causal[0:SEQ], start=True, stop=False)
                    mm = nc.tensor.matmul(scores[:, b], qT[:, i, :], kbd[:, i, 4 * b:4 * b + 4, :],
                                          start=False, stop=True)
                mm.then_inc(s_s, 1)

            def transposes(g, i):
                pe.wait_ge(s_p, g * GROUP + i + 1)
                pe.wait_ge(s_pT, g * GROUP + i + 1)
                for h in range(HEADS):
                    mm = nc.tensor.transpose(probsT_ps[:, h // 4, h % 4, :], probs[i % 2][0:SEQ, h, :],
                                             ident[0:SEQ, 0:SEQ])
                mm.then_inc(s_pT_ps, 1)

            def values(g, i):
                pe.wait_ge(s_pT, g * GROUP + i + 2)
                if i == 0:
                    pe.wait_ge(s_v, g + 1)
                if i >= 2:
                    pe.wait_ge(s_o, g * GROUP + i - 1)
                for h in range(HEADS):
                    mm = nc.tensor.matmul(o_ps(i)[:, h, :], probsT[i % 2][0:SEQ, h, :], v1[0:SEQ, i, h, :],
                                          start=True, stop=True)
                mm.then_inc(s_o_ps, 1)

            def turn_output(g, more):
                pe.wait_ge(s_o, (g + 1) * GROUP)
                pe.wait_ge(s_xnT, g + (3 if more else 2))
                for i in range(GROUP):
                    mm = nc.tensor.transpose(ps_m0[:, i * SEQ:(i + 1) * SEQ], o_rows[0:SEQ, i, :],
                                             ident[0:SEQ, 0:SEQ])
                mm.then_inc(s_oT_ps, 1)

            def project(g):
                pe.wait_ge(s_oT, g + 1)
                for t in range(GT):
                    mm = nc.tensor.matmul(ps_m1[:, t * D:(t + 1) * D], oT[:, t * P:(t + 1) * P], wo[:],
                                          start=True, stop=True)
                mm.then_inc(s_proj, 1)

            def attention(g, more, second):
                def ahead(start, stop):
                    if more:
                        patches(g + 1, 1, range(start, stop))

                def two_ahead(start, stop):
                    if second:
                        patches(g + 2, 0, range(start, stop))

                qkv(g)
                ahead(0, 4)
                score(g, 0)
                ahead(4, 14)
                transposes(g, 0)
                score(g, 1)
                ahead(14, 18)
                values(g, 0)
                transposes(g, 1)
                score(g, 2)
                ahead(18, PC)
                values(g, 1)
                transposes(g, 2)
                score(g, 3)
                two_ahead(0, 6)
                values(g, 2)
                transposes(g, 3)
                if more:
                    norm_transposes(g + 1)
                two_ahead(6, 9)
                values(g, 3)
                two_ahead(9, 13)
                turn_output(g, more)
                two_ahead(13, 17)
                project(g)
                two_ahead(17, PC)

            pe.sem_inc(s_sub, 1)
            pe.sem_inc(s_pT, 1)
            pe.sem_inc(s_h, 1)
            pe.sem_inc(s_s, GROUP)
            pe.wait_ge(s_wp, 16)
            patches(0, 0, range(PC))
            patches(0, 1, range(PC))
            pe.wait_ge(s_xn, 1)
            nc.tensor.transpose(ps_m0[:, 0:P], xn[:, 0, :], ident[:]).then_inc(s_xnT_ps, 1)
            patches(1, 0, range(PC))
            pe.wait_ge(s_xnT, 1)
            norm_transposes(0)
            pe.wait_ge(s_w, 16 * 10)
            pe.wait_ge(s_const, 5)
            with pe.Fori(0, LAST - 1) as g:
                attention(g, True, True)
            attention(LAST - 1, True, False)
            attention(LAST, False, False)
            pe.wait_ge(s_cls, GROUPS)
            nc.tensor.matmul(ps_m2[:, 0:D], oT_cls[:].rearrange("p i c -> p (i c)"), wo[:],
                             start=True, stop=True).then_inc(s_proj, 1)


def rstd_steps(dve, ch, var, veps, root, t, r, s_veps, s_root, n):
    dve.tensor_scalar(veps, var, EPS, None, ALU.add).then_inc(s_veps, 1)
    dve.wait_ge(s_root, n)
    ch.step(dve.reciprocal(r, root))
    ch.step(dve.tensor_tensor(t, r, r, ALU.mult))
    ch.step(dve.tensor_tensor(t, t, veps, ALU.mult))
    ch.step(dve.tensor_scalar(t, t, -0.5, 1.5, ALU.mult, ALU.add))
    return dve.tensor_tensor(r, r, t, ALU.mult)


EXPERTS, HIDDEN, HC = 8, 256, 2
TRIO = 3
TRIOS = TILES // TRIO


def norm_statistics(dve, ch, stats, mean, var, scratch):
    mean_e, mean_o, sq_e, sq_o = stats[:, :, 1], stats[:, :, 4], stats[:, :, 2], stats[:, :, 5]
    ch.mark(dve.tensor_tensor(mean, mean_e, mean_o, ALU.add))
    ch.mark(dve.tensor_tensor(scratch[0], mean_e, mean_o, ALU.subtract))
    ch.step(dve.tensor_tensor(scratch[1], sq_e, sq_o, ALU.add))
    ch.mark(dve.tensor_scalar(mean, mean, 0.5, None, ALU.mult))
    ch.mark(dve.tensor_scalar(scratch[1], scratch[1], 1.0 / D, None, ALU.mult))
    ch.step(dve.tensor_tensor(scratch[0], scratch[0], scratch[0], ALU.mult))
    return dve.scalar_tensor_tensor(out=var, in0=scratch[0], scalar=0.25, in1=scratch[1],
                                    op0=ALU.mult, op1=ALU.add)


def experts(nc, resid, ident, a, tables, s_turns, dve_marks, stats, scratch):
    with ExitStack() as ctx:
        def sb(name, shape, dt=F32):
            return ctx.enter_context(nc.sbuf_tensor(name, shape, dt))

        def sem(name):
            return ctx.enter_context(nc.semaphore(name))

        fc1 = sb("ex_fc1", [P, EXPERTS, 2 * HIDDEN])
        fc2 = sb("ex_fc2", [P, EXPERTS, HC, D])
        b1 = sb("ex_b1", [P, EXPERTS, 2 * HC])
        b2 = sb("ex_b2", [P, D])
        router = sb("ex_router", [P, EXPERTS])
        rb = sb("ex_router_bias", [P, EXPERTS])
        mean, var, veps, root, rstd, t0, t1 = (
            sb(f"ex_{n}", [P, TILES]) for n in ("mean", "var", "veps", "root", "rstd", "t0", "t1"))
        xs = [sb(f"ex_xs{j}", [P, D]) for j in range(TRIO)]
        xTs = [sb(f"ex_xTs{j}", [P, P]) for j in range(TRIO)]
        xT = sb("ex_xT", [P, TILES * P])
        logits, second, eq, pick1, pick2, cw = (
            sb(f"ex_{n}", [P, TILES, EXPERTS]) for n in ("logits", "second", "eq", "pick1", "pick2", "cw"))
        first_wins = sb("ex_first_wins", [P, EXPERTS])
        m1, m2, f1, f2, dl, den, w1, w2 = (
            sb(f"ex_{n}", [P, TILES]) for n in ("m1", "m2", "f1", "f2", "dl", "den", "w1", "w2"))
        cws = sb("ex_cws", [P, TRIO, EXPERTS])
        cwT = sb("ex_cwT", [P, TRIO * P])
        gate = [sb(f"ex_gate{j}", [P, TRIO * P]) for j in range(HC)]
        act_t = [[sb(f"ex_act{b}{j}", [P, TRIO * P]) for j in range(HC)] for b in range(2)]
        acc = sb("ex_acc", [P, TRIO, D])

        s_w = sem("ex_weights")
        s_router = sem("ex_router_loaded")
        s_const = sem("ex_constants")
        s_veps = sem("ex_variances_ready")
        s_root = sem("ex_roots_ready")
        s_rstd = sem("ex_rstd_ready")
        s_xs = sem("ex_xs_ready")
        s_xT_ps = sem("ex_xT_in_psum")
        s_xT = sem("ex_xT_ready")
        s_copy = sem("ex_xT_kept")
        s_logit = sem("ex_logits_in_psum")
        s_dl = sem("ex_top_difference")
        s_exp = sem("ex_top_exp")
        s_cws = sem("ex_cws_ready")
        s_cwT_ps = sem("ex_cwT_in_psum")
        s_cwT = sem("ex_cwT_ready")
        s_bias = sem("ex_bias_term_in_psum")
        s_init = sem("ex_acc_started")
        s_h1 = sem("ex_h1_in_psum")
        s_h2 = sem("ex_h2_in_psum")
        s_gate = sem("ex_gate_ready")
        s_a = sem("ex_act_ready")
        s_y = sem("ex_y_in_psum")
        s_acc = sem("ex_y_taken")
        STEPS = EXPERTS * HC

        with ExitStack() as prep:
            ps_x = [prep.enter_context(nc.psum_tensor(f"ex_ps_x{j}", [P, 512], F32)) for j in range(TRIO)]
            ps_l = prep.enter_context(nc.psum_tensor("ex_ps_logits", [P, 512], F32))
            block = prep.enter_context(nc.Block())

            @block.sync
            def _(sp):
                sp.dma_start(router[:], a["router"]).then_inc(s_router, 16)
                for dst, src in [(rb[:], row_bc(a["router_b"])), (fc1[:], a["fc1"]),
                                 (fc2[:], a["fc2"]), (b1[:], a["b1"]), (b2[0:EXPERTS, :], a["b2"])]:
                    sp.dma_start(dst, src).then_inc(s_w, 16)

            @block.gpsimd
            def _(pool):
                pool.iota(first_wins[:], pattern=[[-1, EXPERTS]], base=EXPERTS, channel_multiplier=0,
                          allow_small_or_imprecise_dtypes=True).then_inc(s_const, 1)
                with pool.Fori(0, TRIOS) as i:
                    for j in range(TRIO):
                        pool.wait_ge(s_xT, (i + 1) * TRIO + j + 1)
                        pool.tensor_copy(xT[:, ds((i * TRIO + j) * P, P)], xTs[j][:]).then_inc(s_copy, 1)

            @block.vector
            def _(dve):
                ch = Chain(dve, dve_marks, s_turns)
                ch.step(norm_statistics(dve, ch, stats, mean[:], var[:], (t0[:], t1[:])))
                rstd_steps(dve, ch, var[:], veps[:], root[:], t0[:], rstd[:], s_veps, s_root, 1).then_inc(s_rstd, 1)
                dve.wait_ge(s_rstd, 1)
                with dve.Fori(0, TRIOS) as i:
                    for j in range(TRIO):
                        t = i * TRIO + j
                        dve.wait_ge(s_xT_ps, t + 1)
                        dve.tensor_scalar(xs[j][:], resid[:, t, :], mean[:, ds(t, 1)], rstd[:, ds(t, 1)],
                                          ALU.subtract, ALU.mult).then_inc(s_xs, 1)
                dve.wait_ge(s_logit, TILES + TRIO)
                dve.wait_ge(s_const, 1)
                dve.wait_ge(s_w, 16 * 5)

                def wide(x):
                    return x[:, :, None].to_broadcast([P, TILES, EXPERTS])

                ch.step(dve.tensor_tensor(logits[:], ps_l[:, 0:TILES * EXPERTS].rearrange("p (t e) -> p t e", e=EXPERTS),
                                          rb[:, None, :].to_broadcast([P, TILES, EXPERTS]), ALU.add))
                for x, m, f, pick in ((logits, m1, f1, pick1), (second, m2, f2, pick2)):
                    ch.step(dve.tensor_reduce(m[:], x[:], AX_X, ALU.max))
                    ch.step(dve.tensor_tensor(eq[:], x[:], wide(m), ALU.is_equal))
                    ch.step(dve.tensor_tensor(eq[:], eq[:], first_wins[:, None, :].to_broadcast([P, TILES, EXPERTS]),
                                              ALU.mult))
                    ch.step(dve.tensor_reduce(f[:], eq[:], AX_X, ALU.max))
                    ch.step(dve.tensor_tensor(pick[:], eq[:], wide(f), ALU.is_equal))
                    if x is logits:
                        ch.step(dve.scalar_tensor_tensor(out=second[:], in0=pick1[:], scalar=-3e38, in1=logits[:],
                                                         op0=ALU.mult, op1=ALU.add))
                dve.tensor_tensor(dl[:], m2[:], m1[:], ALU.subtract).then_inc(s_dl, 1)
                dve.wait_ge(s_exp, 1)
                ch.step(dve.tensor_scalar(den[:], dl[:], 1.0, None, ALU.add))
                ch.step(dve.reciprocal(w1[:], den[:]))
                ch.mark(dve.tensor_tensor(w2[:], dl[:], w1[:], ALU.mult))
                ch.step(dve.tensor_tensor(cw[:], pick1[:], wide(w1), ALU.mult))
                ch.step(dve.tensor_tensor(pick2[:], pick2[:], wide(w2), ALU.mult))
                dve.tensor_tensor(cw[:], cw[:], pick2[:], ALU.add)

            @block.scalar
            def _(act):
                act.wait_ge(s_veps, 1)
                nc.scalar.activation(root[:], veps[:], ACT.Sqrt).then_inc(s_root, 1)
                act.sem_inc(s_xT, TRIO)
                with act.Fori(0, TRIOS) as i:
                    for j in range(TRIO):
                        t = i * TRIO + j
                        act.wait_ge(s_xT_ps, t + TRIO + 1)
                        act.wait_ge(s_logit, t + 1)
                        act.wait_ge(s_copy, t + 1)
                        nc.scalar.copy(xTs[j][:], ps_x[j][:, 0:P]).then_inc(s_xT, 1)
                act.wait_ge(s_dl, 1)
                nc.scalar.activation(dl[:], dl[:], ACT.Exp).then_inc(s_exp, 1)

            @block.tensor
            def _(pe):
                for s in (s_xT_ps, s_logit, s_copy):
                    pe.sem_inc(s, TRIO)
                pe.wait_ge(s_router, 16)
                with pe.Fori(0, TRIOS) as i:
                    for j in range(TRIO):
                        t = i * TRIO + j
                        pe.wait_ge(s_xs, t + 1)
                        pe.wait_ge(s_xT, t + 1)
                        nc.tensor.transpose(ps_x[j][:, 0:P], xs[j][:], ident[:]).then_inc(s_xT_ps, 1)
                    for j in range(TRIO):
                        t = i * TRIO + j
                        pe.wait_ge(s_xT, t + TRIO + 1)
                        nc.tensor.matmul(ps_l[:, ds(t * EXPERTS, EXPERTS)], xTs[j][:], router[:],
                                         start=True, stop=True).then_inc(s_logit, 1)

        with ExitStack() as main:
            ps_h1 = [main.enter_context(nc.psum_tensor(f"ex_ps_h1{j}", [P, 512], F32)) for j in range(HC)]
            ps_h2 = [main.enter_context(nc.psum_tensor(f"ex_ps_h2{j}", [P, 512], F32)) for j in range(HC)]
            ps_y = [main.enter_context(nc.psum_tensor(f"ex_ps_y{b}", [P, 512], F32)) for b in range(2)]
            ps_bias = main.enter_context(nc.psum_tensor("ex_ps_bias", [P, 512], F32))
            ps_cw = main.enter_context(nc.psum_tensor("ex_ps_cw", [P, 512], F32))
            W = TRIO * P
            compact = main.enter_context(nc.sbuf_tensor("ex_tables_compact", [P, SPLINES * 2 * QS], F32))
            rest = main.enter_context(nc.sbuf_tensor("ex_tables_rest", [P, SPLINES * 2 * QS], F32))
            parts = main.enter_context(nc.sbuf_tensor("ex_tables_parts", [P, PARTS, SPLINES * 2 * QS], BF16))
            unit_mask = main.enter_context(nc.sbuf_tensor("ex_unit_mask", [P, HG], F32))
            s_tables = main.enter_context(nc.semaphore("ex_tables_loaded"))
            s_spread = main.enter_context(nc.semaphore("ex_tables_spread"))
            s_tchain = main.enter_context(nc.semaphore("ex_tables_chain"))
            block = main.enter_context(nc.Block())

            x_rows, _, s_zeroed = scratch
            zeros = main.enter_context(nc.sbuf_tensor("ex_zeros", [P, D], F32))
            s_zero = main.enter_context(nc.semaphore("ex_zeros_set"))

            @block.sync
            def _(sp):
                sp.dma_start(compact[:], a["spline_tables"]).then_inc(s_tables, 16)
                sp.wait_ge(s_zero, 1)
                sp.dma_start(x_rows.rearrange("(n p) d -> p n d", p=P),
                             zeros[:, None, :].to_broadcast([P, ROWS // P, D])).then_inc(s_zeroed, 16)
                sp.wait_ge(s_zeroed, 16)

            @block.gpsimd
            def _(pool):
                ch = Chain(pool, s_tchain)
                pool.memset(zeros[:], 0.0).then_inc(s_zero, 1)
                ch.step(pool.memset(unit_mask[:], 1.0))
                ch.step(pool.affine_select(out=unit_mask[:], in_=unit_mask[:], compare_op=ALU.is_ge, fill=0.0,
                                           base=0, pattern=[[-GRID, HG]], channel_multiplier=1))
                ch.step(pool.affine_select(out=unit_mask[:], in_=unit_mask[:], compare_op=ALU.is_ge, fill=0.0,
                                           base=GRID - 1, pattern=[[GRID, HG]], channel_multiplier=-1))
                spread_tables(pool, ch, compact, parts, rest, unit_mask, tables, s_spread, s_tables)

            @block.vector
            def _(dve):
                ch = Chain(dve, dve_marks)
                dve.sem_inc(s_acc, 2)
                dve.sem_inc(s_a, HC)
                dve.sem_inc(s_init, 1)
                with dve.Fori(0, TRIOS) as i:
                    ch.enter(i, 2 * EXPERTS + 1 + TRIO)

                    def activated(e, j):
                        m = e * HC + j
                        dve.wait_ge(s_gate, i * STEPS + m + 1)
                        dve.wait_ge(s_h2, i * STEPS + m + 1)
                        dve.scalar_tensor_tensor(out=act_t[e % 2][j][:], in0=ps_h2[j][:, 0:W],
                                                 scalar=b1[:, e, HC + j:HC + j + 1], in1=gate[j][:],
                                                 op0=ALU.add, op1=ALU.mult).then_inc(s_a, 1)

                    def accumulate(e):
                        dve.wait_ge(s_y, i * EXPERTS + e + 1)
                        dve.wait_ge(s_acc, i * EXPERTS + e + 2)
                        ch.sync()
                        for s in range(TRIO):
                            out = acc[:, s, :] if e < EXPERTS - 1 else resid[:, i * TRIO + s, :]
                            ins = dve.scalar_tensor_tensor(out=out, in0=ps_y[e % 2][:, s * D:(s + 1) * D],
                                                           scalar=cws[:, s, e:e + 1], in1=acc[:, s, :],
                                                           op0=ALU.mult, op1=ALU.add)
                            if s < TRIO - 1:
                                ch.mark(ins)
                        ins.then_inc(s_acc, 1)

                    dve.wait_ge(s_acc, i * EXPERTS + 2)
                    dve.tensor_copy(cws[:], cw[:, ds(i * TRIO, TRIO), :]).then_inc(s_cws, 1)
                    activated(0, 0)
                    activated(0, 1)
                    activated(1, 0)
                    activated(1, 1)
                    dve.wait_ge(s_bias, i + 1)
                    dve.wait_ge(s_cws, i + 1)
                    ch.mark(dve.tensor_tensor(acc[:], ps_bias[:, 0:TRIO * D].rearrange("p (s d) -> p s d", s=TRIO),
                                              resid[:, ds(i * TRIO, TRIO), :], ALU.add))
                    ch.sync()
                    dve.sem_inc(s_init, 1)
                    for e in range(EXPERTS):
                        if e >= 1 and e + 1 < EXPERTS:
                            activated(e + 1, 0)
                            activated(e + 1, 1)
                        accumulate(e)
                    ch.sync()
                    dve.wait_ge(s_acc, (i + 1) * EXPERTS + 2)
                    dve.sem_inc(s_turns, 1)
                    tile_statistics(ch, stats, resid, [i * TRIO + s for s in range(TRIO)])
                    ch.leave(TRIOS)

            @block.scalar
            def _(act):
                act.sem_inc(s_cwT, 1)
                with act.Fori(0, TRIOS) as i:
                    for e in range(EXPERTS):
                        for j in range(HC):
                            m = e * HC + j
                            act.wait_ge(s_h1, i * STEPS + m + 1)
                            act.wait_ge(s_a, i * STEPS + m + 1)
                            nc.scalar.activation(gate[j][:], ps_h1[j][:, 0:W], ACT.Silu,
                                                 bias=b1[:, e, j:j + 1]).then_inc(s_gate, 1)
                        if e == 0:
                            act.wait_ge(s_cwT_ps, i + 1)
                            nc.scalar.copy(cwT[0:EXPERTS, :], ps_cw[0:EXPERTS, 0:W]).then_inc(s_cwT, 1)

            @block.tensor
            def _(pe):
                with pe.Fori(0, TRIOS) as i:
                    x = xT[:, ds(i * W, W)]

                    def hidden(e):
                        for j in range(HC):
                            pe.wait_ge(s_a, i * STEPS + e * HC + j + 1)
                            nc.tensor.matmul(ps_h1[j][:, 0:W], fc1[:, e, j * P:(j + 1) * P], x,
                                             start=True, stop=True).then_inc(s_h1, 1)
                            nc.tensor.matmul(ps_h2[j][:, 0:W], fc1[:, e, HIDDEN + j * P:HIDDEN + (j + 1) * P], x,
                                             start=True, stop=True).then_inc(s_h2, 1)

                    def outputs(e):
                        pe.wait_ge(s_a, i * STEPS + e * HC + HC + HC)
                        pe.wait_ge(s_acc, i * EXPERTS + e + 1)
                        for s in range(TRIO):
                            for j in range(HC):
                                mm = nc.tensor.matmul(ps_y[e % 2][:, s * D:(s + 1) * D],
                                                      act_t[e % 2][j][:, s * P:(s + 1) * P], fc2[:, e, j, :],
                                                      start=(j == 0), stop=(j == HC - 1))
                        mm.then_inc(s_y, 1)

                    hidden(0)
                    pe.wait_ge(s_cws, i + 1)
                    pe.wait_ge(s_cwT, i + 1)
                    for s in range(TRIO):
                        mm = nc.tensor.transpose(ps_cw[0:EXPERTS, s * P:(s + 1) * P], cws[:, s, :], ident[:])
                    mm.then_inc(s_cwT_ps, 1)
                    hidden(1)
                    pe.wait_ge(s_cwT, i + 2)
                    pe.wait_ge(s_init, i + 1)
                    for s in range(TRIO):
                        mm = nc.tensor.matmul(ps_bias[:, s * D:(s + 1) * D], cwT[0:EXPERTS, s * P:(s + 1) * P],
                                              b2[0:EXPERTS, :], start=True, stop=True)
                    mm.then_inc(s_bias, 1)
                    for e in range(EXPERTS):
                        if e >= 1 and e + 1 < EXPERTS:
                            hidden(e + 1)
                        outputs(e)


def attention(nc, resid, ident, a, s_turns, dve_marks, stats, wd_sum):
    with ExitStack() as ctx:
        def sb(name, shape, dt=F32):
            return ctx.enter_context(nc.sbuf_tensor(name, shape, dt))

        def sem(name):
            return ctx.enter_context(nc.semaphore(name))

        def psum(name):
            return ctx.enter_context(nc.psum_tensor(name, [P, 512], F32))

        ps_x, ps_q, ps_k, ps_v, ps_s, ps_pt, ps_o, ps_c = (
            psum(f"at_ps_{n}") for n in ("x", "q", "k", "v", "scores", "probsT", "o", "cls"))
        w_qkv = sb("at_w_qkv", [P, 3, D])
        wd = sb("at_wd", [P, SPLINES, P])
        EACH = SPLINES // GROUPS
        mean, var, veps, root, rstd, t0, t1 = (
            sb(f"at_{n}", [P, TILES]) for n in ("mean", "var", "veps", "root", "rstd", "t0", "t1"))
        xs = sb("at_xs", [P, GT, D])
        warm = sb("at_warm", [P, 1])
        xT_cls = sb("at_xT_cls", [P, IMAGES, CLS])
        xT = sb("at_xT", [P, GROUP, SEQ])
        qT = sb("at_qT", [P, GROUP, SEQ])
        kT = sb("at_kT", [P, GROUP, SEQ])
        v = sb("at_v", [P, GROUP, D])
        top, rsum = sb("at_top", [P, GROUP]), sb("at_rsum", [P, GROUP])
        probs = sb("at_probs", [P, GROUP, SEQ])
        probsT = sb("at_probsT", [P, GROUP, SEQ])
        o_cls = sb("at_o_cls", [P, IMAGES, D])
        o_cls_rows = sb("at_o_cls_rows", [P, D])

        s_w = sem("at_weights")
        s_wd = sem("at_wd_loaded")
        s_veps = sem("at_variances_ready")
        s_root = sem("at_roots_ready")
        s_rstd = sem("at_rstd_ready")
        s_xs = sem("at_xs_ready")
        s_xT_ps = sem("at_xT_in_psum")
        s_xT = sem("at_xT_ready")
        s_xc = sem("at_xT_cls_ready")
        s_q_ps = sem("at_q_in_psum")
        s_k_ps = sem("at_k_in_psum")
        s_v_ps = sem("at_v_in_psum")
        s_q = sem("at_q_ready")
        s_k = sem("at_k_ready")
        s_v = sem("at_v_ready")
        s_s = sem("at_scores_ready")
        s_sub = sem("at_scores_taken")
        s_e = sem("at_exp_ready")
        s_p = sem("at_probs_ready")
        s_pT_ps = sem("at_probsT_in_psum")
        s_pT = sem("at_probsT_ready")
        s_o = sem("at_o_in_psum")
        s_h = sem("at_o_taken")
        s_c = sem("at_o_cls_taken")
        s_rows = sem("at_o_cls_rows_moved")

        def images(ps, rows=P):
            return ps[0:rows, 0:GROUP * SEQ].rearrange("p (i s) -> p i s", i=GROUP)

        LAST = GROUPS - 1
        block = ctx.enter_context(nc.Block())

        @block.sync
        def _(sp):
            sp.dma_start(w_qkv[:], a["w_qkv"]).then_inc(s_w, 16)
            sp.dma_start(wd[:], a["wd_sums"]).then_inc(s_wd, 16)
            sp.wait_ge(s_c, GROUPS + 1)
            for c in range(CLS):
                sp.dma_start(o_cls_rows[c::CLS, :], o_cls[c:c + 1, :, :]).then_inc(s_rows, 16)

        @block.gpsimd
        def _(pool):
            pool.wait_ge(s_xT, 1)
            with pool.Fori(0, GROUPS) as g:
                pool.wait_ge(s_v_ps, g + 1)
                pool.tensor_copy(xT[:, :, 0:CLS], xT_cls[:, ds(g * GROUP, GROUP), :]).then_inc(s_xc, 1)

        @block.vector
        def _(dve):
            ch = Chain(dve, dve_marks, s_turns)
            ch.step(norm_statistics(dve, ch, stats, mean[:], var[:], (t0[:], t1[:])))
            rstd_steps(dve, ch, var[:], veps[:], root[:], t0[:], rstd[:], s_veps, s_root, 1).then_inc(s_rstd, 1)
            dve.wait_ge(s_rstd, 1)

            def normalise(slot, tile):
                return dve.tensor_scalar(xs[:, slot, :], resid[:, tile, :], mean[:, ds(tile, 1)], rstd[:, ds(tile, 1)],
                                         ALU.subtract, ALU.mult)

            def normalise_group(g):
                dve.wait_ge(s_xT_ps, g + 1)
                for t in range(GT - 1):
                    ch.mark(normalise(t, g * GT + t))
                ch.sync()
                normalise(GT - 1, g * GT + GT - 1).then_inc(s_xs, 1)

            def keep_values(g):
                dve.wait_ge(s_v_ps, g + 2)
                dve.tensor_copy(v[0:SEQ],
                                ps_v[0:SEQ, :].rearrange("p (i d) -> p i d", i=GROUP)).then_inc(s_v, 1)

            def wide(x):
                return x[0:SEQ, :, None].to_broadcast([SEQ, GROUP, SEQ])

            def softmax(g):
                dve.wait_ge(s_s, g + 1)
                ch.step(dve.tensor_reduce(top[0:SEQ, :], images(ps_s, SEQ), AX_X, ALU.max))
                dve.tensor_tensor(probs[0:SEQ], images(ps_s, SEQ), wide(top), ALU.subtract).then_inc(s_sub, 1)
                dve.wait_ge(s_e, g + 1)
                ch.step(dve.tensor_reduce(rsum[0:SEQ, :], probs[0:SEQ], AX_X, ALU.add))
                ch.step(dve.reciprocal(rsum[0:SEQ, :], rsum[0:SEQ, :]))
                dve.tensor_tensor(probs[0:SEQ], probs[0:SEQ], wide(rsum), ALU.mult).then_inc(s_p, 1)

            def group(g, more, second):
                if second:
                    normalise_group(g + 2)
                if more:
                    softmax(g + 1)
                now = ds(g * EACH, EACH)
                ch.mark(dve.tensor_reduce(wd_sum[:, now], wd[:, now, :], AX_X, ALU.add))
                dve.wait_ge(s_o, g + 1)
                if more:
                    keep_values(g + 1)
                tiles = resid[:, ds(g * GT, GT), :]
                dve.tensor_tensor(tiles, tiles, ps_o[:, 0:GT * D].rearrange("p (t d) -> p t d", t=GT),
                                  ALU.add).then_inc(s_h, 1)
                dve.wait_ge(s_h, g + 2)
                dve.sem_inc(s_turns, 1)
                tile_statistics(ch, stats, resid, [g * GT + t for t in range(GT)])

            normalise(0, PTILES).then_inc(s_xs, 1)
            normalise_group(0)
            keep_values(0)
            normalise_group(1)
            softmax(0)
            dve.wait_ge(s_wd, 16)
            with dve.Fori(0, LAST - 1) as g:
                ch.enter(g, 1 + GT + 3 + GT - 1)
                group(g, True, True)
                ch.leave(LAST - 1)
            group(LAST - 1, True, False)
            group(LAST, False, False)
            dve.wait_ge(s_rows, 16 * CLS)
            ch.step(dve.tensor_tensor(resid[:, PTILES, :], resid[:, PTILES, :], o_cls_rows[:], ALU.add))
            tile_statistics(ch, stats, resid, [PTILES])

        @block.scalar
        def _(act):
            def transposed(g):
                act.wait_ge(s_xT_ps, g + 2)
                nc.scalar.copy(xT[:, :, CLS:SEQ], ps_x[:, 0:GT * P].rearrange("p (i s) -> p i s", i=GROUP))\
                    .then_inc(s_xT, 1)

            def project(g):
                act.wait_ge(s_q_ps, g + 1)
                nc.scalar.copy(qT[:], images(ps_q)).then_inc(s_q, 1)
                act.wait_ge(s_k_ps, g + 1)
                nc.scalar.copy(kT[:], images(ps_k)).then_inc(s_k, 1)

            def exps(g):
                act.wait_ge(s_sub, g + 2)
                nc.scalar.activation(probs[0:SEQ], probs[0:SEQ], ACT.Exp, scale=1.0 / D ** 0.5).then_inc(s_e, 1)

            def group(g, more, second):
                if more:
                    project(g + 1)
                act.wait_ge(s_pT_ps, g + 1)
                nc.scalar.copy(probsT[0:SEQ], images(ps_pt, SEQ)).then_inc(s_pT, 1)
                if second:
                    transposed(g + 2)
                if more:
                    exps(g + 1)
                act.wait_ge(s_o, g + 1)
                nc.scalar.copy(o_cls[0:CLS, ds(g * GROUP, GROUP), :],
                               ps_c[0:CLS, :].rearrange("p (i d) -> p i d", i=GROUP)).then_inc(s_c, 1)

            act.wait_ge(s_veps, 1)
            nc.scalar.activation(root[:], veps[:], ACT.Sqrt).then_inc(s_root, 1)
            act.wait_ge(s_rstd, 1)
            nc.scalar.activation(warm[:, 0:1], rstd[:, 0:1], ACT.Exp)
            act.wait_ge(s_xT_ps, 1)
            nc.scalar.copy(xT_cls[:].rearrange("p i c -> p (i c)"), ps_x[:, 0:P]).then_inc(s_xT, 1)
            transposed(0)
            project(0)
            transposed(1)
            exps(0)
            with act.Fori(0, LAST - 1) as g:
                group(g, True, True)
            group(LAST - 1, True, False)
            group(LAST, False, False)

        @block.tensor
        def _(pe):
            def turn_x(g):
                pe.wait_ge(s_xs, g + 2)
                pe.wait_ge(s_xT, g + 1)
                for t in range(GT):
                    mm = nc.tensor.transpose(ps_x[:, t * P:(t + 1) * P], xs[:, t, :], ident[:])
                mm.then_inc(s_xT_ps, 1)

            def project(g):
                pe.wait_ge(s_xT, g + 2)
                pe.wait_ge(s_xc, g + 1)
                pe.wait_ge(s_q, g + 1)
                nc.tensor.matmul(images(ps_q), w_qkv[:, 0, :], xT[:], start=True, stop=True).then_inc(s_q_ps, 1)
                pe.wait_ge(s_k, g + 1)
                nc.tensor.matmul(images(ps_k), w_qkv[:, 1, :], xT[:], start=True, stop=True).then_inc(s_k_ps, 1)
                pe.wait_ge(s_v, g + 1)
                for i in range(GROUP):
                    mm = nc.tensor.matmul(ps_v[0:SEQ, i * D:(i + 1) * D], xT[:, i, :], w_qkv[:, 2, :],
                                          start=True, stop=True)
                mm.then_inc(s_v_ps, 1)

            def scores(g):
                pe.wait_ge(s_q, g + 2)
                pe.wait_ge(s_k, g + 2)
                pe.wait_ge(s_sub, g + 1)
                for i in range(GROUP):
                    mm = nc.tensor.matmul(images(ps_s, SEQ)[:, i, :], qT[:, i, :], kT[:, i, :], start=True, stop=True)
                mm.then_inc(s_s, 1)

            def group(g, more, second):
                if more:
                    project(g + 1)
                pe.wait_ge(s_p, g + 1)
                pe.wait_ge(s_pT, g + 1)
                for i in range(GROUP):
                    mm = nc.tensor.transpose(images(ps_pt, SEQ)[:, i, :], probs[0:SEQ, i, :], ident[0:SEQ, 0:SEQ])
                mm.then_inc(s_pT_ps, 1)
                if more:
                    scores(g + 1)
                if second:
                    turn_x(g + 2)
                pe.wait_ge(s_pT, g + 2)
                pe.wait_ge(s_v, g + 2)
                pe.wait_ge(s_h, g + 1)
                pe.wait_ge(s_c, g + 1)
                for i in range(GROUP):
                    values = v[0:SEQ, i, :]
                    rows = (i % 2) * PATCHES
                    nc.tensor.matmul(ps_o[rows:rows + PATCHES, (i // 2) * D:(i // 2 + 1) * D],
                                     probsT[0:SEQ, i, CLS:SEQ], values, start=True, stop=True)
                    mm = nc.tensor.matmul(ps_c[0:CLS, i * D:(i + 1) * D], probsT[0:SEQ, i, 0:CLS], values,
                                          start=True, stop=True)
                mm.then_inc(s_o, 1)

            for s in (s_v_ps, s_q, s_k, s_v, s_sub, s_pT, s_h, s_c):
                pe.sem_inc(s, 1)
            pe.wait_ge(s_w, 16)
            pe.wait_ge(s_xs, 1)
            nc.tensor.transpose(ps_x[:, 0:P], xs[:, 0, :], ident[:]).then_inc(s_xT_ps, 1)
            turn_x(0)
            project(0)
            turn_x(1)
            scores(0)
            with pe.Fori(0, LAST - 1) as g:
                group(g, True, True)
            group(LAST - 1, True, False)
            group(LAST, False, False)


SPLINES, CLUSTERS, PER_CLUSTER, GRID = 64, 8, 8, 16
BLOCK = 64
MAX_BLOCKS = (TILES * P + SPLINES * (BLOCK - 1)) // BLOCK
PAIR = 2
QUAD = 2 * PAIR
RING = 3
QUADS = -(-MAX_BLOCKS // (QUAD * RING)) * RING
ROWS = QUADS * QUAD * BLOCK
BANK_TILES = 7
BANKS = -(-TILES // BANK_TILES)
KEYS = BANKS * BANK_TILES
HG = P // GRID
QS = P // HG
PARTS = 3


def spread_tables(pool, ch, compact, hi_lo, rest, unit_mask, tables, s_tab, tables_loaded):
    pool.wait_ge(tables_loaded, 16)
    ch.step(pool.tensor_copy(hi_lo[:, 0, :], compact[:]))
    for n in range(1, PARTS):
        ch.step(pool.tensor_tensor(rest[:], compact[:] if n == 1 else rest[:], hi_lo[:, n - 1, :], ALU.subtract))
        ch.step(pool.tensor_copy(hi_lo[:, n, :], rest[:]))
    with pool.Fori(0, SPLINES) as t:
        for n in range(PARTS):
            pool.tensor_tensor(tables[:, t, :, n, :, :],
                               hi_lo[:, n, ds(t * 2 * QS, 2 * QS)].rearrange("p (q c) -> p q c", c=2)[:, :, :, None]
                               .to_broadcast([P, QS, 2, HG]),
                               unit_mask[:, None, None, :].to_broadcast([P, QS, 2, HG]), ALU.mult).then_inc(s_tab, 1)


def splines(nc, resid, ident, a, scratch, out, spread, s_turns, dve_marks, stats, wd_sum):
    x_rows, y_rows, s_zeroed = scratch
    with ExitStack() as ctx:
        def sb(name, shape, dt=F32):
            return ctx.enter_context(nc.sbuf_tensor(name, shape, dt))

        def sem(name):
            return ctx.enter_context(nc.semaphore(name))

        gb_cols = sb("sp_gamma_beta", [P, 2])
        dest_i = sb("sp_dest_int", [P, TILES], U32)
        tile_of = sb("sp_tile_of_block", [P, 2 * P], I32)
        expand = sb("sp_expand", [P, QS, P], BF16)
        s_w = sem("sp_weights")
        s_pool = sem("sp_pool_chain")
        s_scat = sem("sp_scattered")

        with ExitStack() as prep:
            def sb(name, shape, dt=F32):
                return prep.enter_context(nc.sbuf_tensor(name, shape, dt))

            ps_x = [prep.enter_context(nc.psum_tensor(f"sp_ps_x{j}", [P, 512], F32)) for j in range(TRIO)]
            ps_r = prep.enter_context(nc.psum_tensor("sp_ps_rank", [P, 5, 512], F32))
            pos_part, cl_sum = sb("sp_positive", [P, SPLINES]), sb("sp_cluster_sum", [P, CLUSTERS])
            sigs = sb("sp_signatures", [P, SPLINES + CLUSTERS], BF16)
            less_index = sb("sp_less_index", [P, SPLINES + CLUSTERS], BF16)
            sig_f = sb("sp_signatures_f", [P, SPLINES + CLUSTERS])
            mean, var, veps, root, rstd, t0, t1 = (
                sb(f"sp_{n}", [P, TILES]) for n in ("mean", "var", "veps", "root", "rstd", "t0", "t1"))
            xs = [sb(f"sp_xs{j}", [P, D]) for j in range(BANK_TILES)]
            xn = sb("sp_xn", [P, TILES, D])
            signs = [sb(f"sp_signs{j}", [P, P], BF16) for j in range(BANK_TILES)]
            c_key, t_key = sb("sp_cluster_key", [P, KEYS, CLUSTERS]), sb("sp_tile_key", [P, KEYS, SPLINES])
            c_max, t_max = sb("sp_cluster_max", [P, KEYS]), sb("sp_tile_max", [P, KEYS])
            chosen = sb("sp_chosen", [P, SPLINES, KEYS], BF16)
            so_far = sb("sp_so_far", [P, SPLINES, KEYS], BF16)
            after_first = sb("sp_after_first", [P, SPLINES, KEYS], BF16)
            start_blocks = sb("sp_start_blocks", [P, SPLINES], BF16)
            block_ones = sb("sp_block_ones", [P, P], BF16)
            minus_rest, ones = sb("sp_minus_rest", [P, P], BF16), sb("sp_ones", [P, P], BF16)
            count, whole, ends, starts = (sb(f"sp_{n}", [P, SPLINES]) for n in ("count", "whole", "ends", "starts"))
            count_i = sb("sp_count_int", [P, SPLINES], I32)
            zero64 = sb("sp_zero64", [P, SPLINES])
            rank = sb("sp_rank", [P, TILES, SPLINES])
            dest = sb("sp_dest", [P, TILES])
            first_row = sb("sp_first_row", [P, 2])
            past = sb("sp_past", [P, 2, SPLINES])
            block_tile = sb("sp_block_tile", [P, 2])

            def psem(name):
                return prep.enter_context(nc.semaphore(name))

            s_centred = psem("sp_stream_centred")
            s_const = psem("sp_constants")
            s_veps = psem("sp_variances_ready")
            s_root = psem("sp_roots_ready")
            s_rstd = psem("sp_rstd_ready")
            s_normed = psem("sp_stream_normed")
            s_sigs = psem("sp_signatures_ready")
            s_xs = psem("sp_xs_ready")
            s_xT_ps = psem("sp_xT_in_psum")
            s_sign = psem("sp_signs_ready")
            s_copy = psem("sp_xn_kept")
            s_score = psem("sp_scores_in_psum")
            s_taken = psem("sp_scores_taken")
            s_starts = psem("sp_starts_ready")
            s_chosen = psem("sp_chosen_ready")
            s_before = psem("sp_before_ready")
            s_rank = psem("sp_rank_in_psum")
            s_bt = psem("sp_block_tile_ready")
            s_bt_ps = psem("sp_block_tile_in_psum")
            s_dest = psem("sp_dest_ready")
            block = prep.enter_context(nc.Block())
            CH = 8
            WIDTH = SPLINES + CLUSTERS

            def bank_loop(eng, body):
                with eng.Fori(0, BANKS - 1) as i:
                    body(i, BANK_TILES)
                body(BANKS - 1, TILES - (BANKS - 1) * BANK_TILES)

            @block.sync
            def _(sp):
                sp.dma_start(gb_cols[:], a["gamma_beta"]).then_inc(s_w, 16)
            @block.gpsimd
            def _(pool):
                ch = Chain(pool, s_pool, s_turns)
                ch.mark(pool.memset(minus_rest[:], -1.0))
                ch.mark(pool.memset(after_first[:], 1.0))
                pool.memset(ones[:], 1.0).then_inc(s_const, 1)
                pool.memset(block_ones[:], float(BLOCK)).then_inc(s_const, 1)
                pool.memset(zero64[:], 0.0).then_inc(s_const, 1)
                ch.sync()
                pool.memset(after_first[:, :, 0], 0.0).then_inc(s_const, 1)
                pool.affine_select(out=minus_rest[:], in_=minus_rest[:], compare_op=ALU.is_ge, fill=0.0, base=0,
                                   pattern=[[-1, P]], channel_multiplier=1).then_inc(s_const, 1)
                pool.iota(less_index[:, 0:SPLINES].rearrange("p (c l) -> p c l", c=CLUSTERS),
                          pattern=[[0, CLUSTERS], [-1, PER_CLUSTER]], base=0, channel_multiplier=0,
                          allow_small_or_imprecise_dtypes=True).then_inc(s_const, 1)
                pool.iota(less_index[:, SPLINES:WIDTH], pattern=[[-1, CLUSTERS]], base=0, channel_multiplier=0,
                          allow_small_or_imprecise_dtypes=True).then_inc(s_const, 1)
                pool.iota(first_row[:], pattern=[[P * BLOCK, 2]], base=0, channel_multiplier=BLOCK,
                          allow_small_or_imprecise_dtypes=True).then_inc(s_const, 1)
                ch.step(pool.memset(expand[:], 1.0))
                ch.step(pool.affine_select(out=expand[:], in_=expand[:], compare_op=ALU.is_ge, fill=0.0, base=0,
                                           pattern=[[P, QS], [1, P]], channel_multiplier=-GRID))
                ch.step(pool.affine_select(out=expand[:], in_=expand[:], compare_op=ALU.is_ge, fill=0.0, base=GRID - 1,
                                           pattern=[[-P, QS], [-1, P]], channel_multiplier=GRID))
                for t in range(0, TILES, TILES // 3):
                    pool.wait_ge(s_normed, t + TILES // 3)
                    now = slice(t, t + TILES // 3)
                    ch.mark(pool.tensor_tensor(resid[:, now, :], resid[:, now, :], xn[:, now, :], ALU.add))
                ch.sync()

                def keep(i, n):
                    for j in range(n):
                        t = i * BANK_TILES + j
                        pool.wait_ge(s_xs, t + 1)
                        pool.tensor_copy(xn[:, t, :], xs[j][:]).then_inc(s_copy, 1)

                bank_loop(pool, keep)
                pool.wait_ge(s_dest, 1)
                pool.wait_ge(s_copy, TILES + BANK_TILES)
                pool.wait_ge(s_zeroed, 16)
                for t in range(TILES):
                    pool.indirect_dma_start(out=x_rows, out_offset=bass.IndirectOffsetOnAxis(ap=dest_i[:, t:t + 1], axis=0),
                                            in_=xn[:, t, :], in_offset=None).then_inc(s_scat, 16)
                pool.wait_ge(s_scat, 16 * TILES)

            @block.vector
            def _(dve):
                ch = Chain(dve, dve_marks, s_turns)
                ch.step(norm_statistics(dve, ch, stats, mean[:], var[:], (t0[:], t1[:])))
                rstd_steps(dve, ch, var[:], veps[:], root[:], t0[:], rstd[:], s_veps, s_root, 1).then_inc(s_rstd, 1)
                dve.wait_ge(s_rstd, 1)
                dve.tensor_tensor(xn[:], resid[:], mean[:, :, None].to_broadcast([P, TILES, D]), ALU.subtract)\
                    .then_inc(s_centred, 1)
                for src, n, at in ((wd_sum, SPLINES, 0), (cl_sum, CLUSTERS, SPLINES)):
                    ch.step(dve.tensor_scalar(pos_part[:, 0:n], src[:], 0.0, None, ALU.is_gt))
                    ch.step(dve.scalar_tensor_tensor(out=sig_f[:, at:at + n], in0=src[:], scalar=0.0,
                                                     in1=pos_part[:, 0:n], op0=ALU.is_lt, op1=ALU.subtract))
                    ch.step(dve.tensor_scalar(sig_f[:, at:at + n], sig_f[:, at:at + n], -1.0, None, ALU.mult))
                    if at == 0:
                        ch.step(dve.tensor_reduce(cl_sum[:], sig_f[:, 0:SPLINES].rearrange("p (c l) -> p c l", c=CLUSTERS),
                                                  AX_X, ALU.add))
                dve.tensor_scalar(sigs[:], sig_f[:], float(PER_CLUSTER), None, ALU.mult).then_inc(s_sigs, 1)
                for t in range(TILES):
                    dve.wait_ge(s_normed, t + 1)
                    tile_statistics(ch, stats, xn, [t])
                ch.sync()
                ch.step(norm_statistics(dve, ch, stats, mean[:], var[:], (t0[:], t1[:])))
                rstd_steps(dve, ch, var[:], veps[:], root[:], t0[:], rstd[:], s_veps, s_root, 2).then_inc(s_rstd, 1)
                dve.wait_ge(s_rstd, 2)

                def normalise(i, n):
                    for j in range(n):
                        t = i * BANK_TILES + j
                        dve.wait_ge(s_xT_ps, t + 1)
                        dve.wait_ge(s_copy, t + 1)
                        dve.tensor_scalar(xs[j][:], xn[:, t, :], mean[:, ds(t, 1)], rstd[:, ds(t, 1)],
                                          ALU.subtract, ALU.mult).then_inc(s_xs, 1)

                bank_loop(dve, normalise)
                dve.wait_ge(s_taken, 2 * BANKS)
                dve.wait_ge(s_const, 8)
                ch.step(dve.tensor_reduce(c_max[:], c_key[:], AX_X, ALU.max))
                ch.step(dve.tensor_tensor(c_key[:], c_key[:], c_max[:, :, None].to_broadcast([P, KEYS, CLUSTERS]),
                                          ALU.is_equal))
                keys = t_key[:].rearrange("p t (c l) -> p (t c) l", l=PER_CLUSTER)
                ch.step(dve.scalar_tensor_tensor(out=keys, in0=c_key[:].rearrange("p t c -> p (t c)")[:, :, None]
                                                 .to_broadcast([P, KEYS * CLUSTERS, PER_CLUSTER]), scalar=4096.0,
                                                 in1=keys, op0=ALU.mult, op1=ALU.add))
                ch.step(dve.tensor_reduce(t_max[:], t_key[:], AX_X, ALU.max))
                dve.tensor_tensor(chosen[:].rearrange("p s t -> p t s"), t_key[:],
                                  t_max[:, :, None].to_broadcast([P, KEYS, SPLINES]), ALU.is_equal).then_inc(s_chosen, 1)
                dve.wait_ge(s_chosen, 1)
                ch.step(dve.tensor_tensor_scan(so_far[:].rearrange("p s t -> p (s t)"),
                                               after_first[:].rearrange("p s t -> p (s t)"),
                                               chosen[:].rearrange("p s t -> p (s t)"), 0.0, ALU.mult, ALU.add))
                dve.sem_inc(s_before, 1)
                dve.wait_ge(s_rank, 1)
                ch.step(dve.tensor_scalar(count_i[:], ps_x[0][:, 0:SPLINES], float(BLOCK - 1), None, ALU.add))
                ch.step(dve.tensor_scalar(count_i[:], count_i[:], -BLOCK, None, ALU.bitwise_and))
                ch.step(dve.tensor_copy(whole[:], count_i[:]))
                ch.step(dve.tensor_tensor_scan(ends[:], whole[:], zero64[:], 0.0, ALU.add, ALU.add))
                ch.step(dve.tensor_tensor(starts[:], ends[:], whole[:], ALU.subtract))
                dve.tensor_scalar(start_blocks[:], starts[:], 1.0 / BLOCK, None, ALU.mult).then_inc(s_starts, 1)
                ch.step(dve.tensor_tensor(past[:], ends[:, None, :].to_broadcast([P, 2, SPLINES]),
                                          first_row[:, :, None].to_broadcast([P, 2, SPLINES]), ALU.is_le))
                ch.step(dve.tensor_reduce(block_tile[:], past[:], AX_X, ALU.add))
                dve.tensor_scalar(block_tile[:], block_tile[:], float(SPLINES - 1), None, ALU.min).then_inc(s_bt, 1)
                for c in range(5):
                    n = min(CH, TILES - c * CH)
                    dve.wait_ge(s_rank, c + 2)
                    ch.mark(dve.tensor_tensor(rank[:, c * CH:c * CH + n, :],
                                              ps_r[:, c, 0:n * SPLINES].rearrange("p (t s) -> p t s", t=n),
                                              chosen[:, :, c * CH:c * CH + n].rearrange("p s t -> p t s"), ALU.mult))
                ch.sync()
                ch.step(dve.tensor_reduce(dest[:], rank[:], AX_X, ALU.add))
                dve.tensor_copy(dest_i[:], dest[:]).then_inc(s_dest, 1)
                dve.wait_ge(s_bt_ps, 1)
                dve.tensor_copy(tile_of[0:1, :], ps_x[1][0:1, 0:2 * P])

            @block.scalar
            def _(act):
                act.sem_inc(s_sign, TRIO)
                act.wait_ge(s_w, 16)
                act.wait_ge(s_veps, 1)
                nc.scalar.activation(root[:], veps[:], ACT.Sqrt).then_inc(s_root, 1)
                act.wait_ge(s_centred, 1)
                for t in range(TILES):
                    nc.scalar.activation(xn[:, t, :], xn[:, t, :], ACT.Identity, scale=rstd[:, t:t + 1])\
                        .then_inc(s_normed, 1)

                act.wait_ge(s_veps, 2)
                nc.scalar.activation(root[:], veps[:], ACT.Sqrt).then_inc(s_root, 1)

                def take_signs(i, n):
                    for j in range(n):
                        t = i * BANK_TILES + j
                        act.wait_ge(s_xT_ps, t + BANK_TILES + 1)
                        act.wait_ge(s_score, t + 1)
                        nc.scalar.activation(signs[j][:], ps_x[j % TRIO][:, 0:P], ACT.Sign, bias=gb_cols[:, 1:2],
                                             scale=gb_cols[:, 0:1]).then_inc(s_sign, 1)
                    act.wait_ge(s_score, (i + 1) * BANK_TILES + BANK_TILES)
                    scores = ps_r[:, i, 0:BANK_TILES * WIDTH].rearrange("p (t s) -> p t s", t=BANK_TILES)
                    now = ds(i * BANK_TILES, BANK_TILES)
                    nc.scalar.copy(t_key[:, now, :], scores[:, :, 0:SPLINES]).then_inc(s_taken, 1)
                    nc.scalar.copy(c_key[:, now, :], scores[:, :, SPLINES:WIDTH]).then_inc(s_taken, 1)

                bank_loop(act, take_signs)

            @block.tensor
            def _(pe):
                for s in (s_xT_ps, s_copy, s_score):
                    pe.sem_inc(s, BANK_TILES)
                pe.wait_ge(s_sigs, 1)
                pe.wait_ge(s_const, 8)

                def turn_and_score(i, n):
                    def score(j):
                        if j < n:
                            pe.wait_ge(s_sign, i * BANK_TILES + j + TRIO + 1)
                        out = ps_r[:, i, j * WIDTH:(j + 1) * WIDTH]
                        nc.tensor.matmul(out, signs[min(j, n - 1)][:], sigs[:], start=True, stop=False)
                        nc.tensor.matmul(out, ones[0:1, :], less_index[0:1, :], start=False, stop=True)\
                            .then_inc(s_score, 1)

                    for j in range(n):
                        t = i * BANK_TILES + j
                        pe.wait_ge(s_xs, t + 1)
                        since = TRIO if j >= TRIO else 1 + j + (BANK_TILES - 1 - j) % TRIO
                        pe.wait_ge(s_sign, t - since + 1 + TRIO)
                        nc.tensor.transpose(ps_x[j % TRIO][:, 0:P], xs[j][:], ident[:]).then_inc(s_xT_ps, 1)
                        if j >= 2:
                            score(j - 2)
                    for j in range(n - 2, BANK_TILES):
                        score(j)

                bank_loop(pe, turn_and_score)
                pe.wait_ge(s_before, 1)
                pe.wait_ge(s_taken, 2 * BANKS)
                nc.tensor.matmul(ps_x[0][:, 0:SPLINES], ones[:], so_far[:, :, TILES - 1], start=True, stop=True)\
                    .then_inc(s_rank, 1)
                for c in range(5):
                    n = min(CH, TILES - c * CH)
                    nc.tensor.matmul(ps_r[:, c, 0:n * SPLINES], minus_rest[:],
                                     chosen[:, :, c * CH:c * CH + n].rearrange("p s t -> p t s"),
                                     start=True, stop=False)
                    nc.tensor.matmul(ps_r[:, c, 0:n * SPLINES], ones[:],
                                     so_far[:, :, c * CH:c * CH + n].rearrange("p s t -> p t s"),
                                     start=False, stop=False)
                pe.wait_ge(s_starts, 1)
                for c in range(5):
                    n = min(CH, TILES - c * CH)
                    nc.tensor.matmul(ps_r[:, c, 0:n * SPLINES], block_ones[0:1, :],
                                     start_blocks[0:1, None, :].to_broadcast([1, n, SPLINES]),
                                     start=False, stop=True).then_inc(s_rank, 1)
                pe.wait_ge(s_bt, 1)
                for c in range(2):
                    mm = nc.tensor.matmul(ps_x[1][0:1, c * P:(c + 1) * P], block_tile[:, c:c + 1], ident[:],
                                          start=True, stop=True)
                mm.then_inc(s_bt_ps, 1)

        spline_blocks(nc, resid, ident, a, scratch, spread, gb_cols, tile_of, expand, dve_marks)

        with ExitStack() as last:
            got = last.enter_context(nc.sbuf_tensor("sp_gathered", [P, TILES, D], F32))
            cuts = [0, 8, 16, 24, TILES]
            s_got = [last.enter_context(nc.semaphore(f"sp_rows_gathered{n}")) for n in range(len(cuts) - 1)]
            s_sum = last.enter_context(nc.semaphore("sp_rows_added"))
            s_out = last.enter_context(nc.semaphore("sp_stored"))
            block = last.enter_context(nc.Block())

            @block.gpsimd
            def _(pool):
                for t in range(TILES):
                    pool.indirect_dma_start(out=got[:, t, :], out_offset=None, in_=y_rows,
                                            in_offset=bass.IndirectOffsetOnAxis(ap=dest_i[:, t:t + 1], axis=0))\
                        .then_inc(s_got[sum(t >= c for c in cuts[1:])], 16)

            @block.vector
            def _(dve):
                for t0, t1 in zip(cuts, cuts[1:]):
                    dve.wait_ge(s_got[cuts.index(t0)], 16 * (t1 - t0))
                    dve.tensor_tensor(got[:, t0:t1, :], got[:, t0:t1, :], resid[:, t0:t1, :], ALU.add)\
                        .then_inc(s_sum, 1)

            @block.sync
            def _(sp):
                tiles = out.rearrange("(t i) s d -> i s t d", i=2)
                for n, (t0, t1) in enumerate(zip(cuts, cuts[1:])):
                    sp.wait_ge(s_sum, n + 1)
                    t1 = min(t1, PTILES)
                    for i in range(2):
                        sp.dma_start(tiles[i, CLS:SEQ, t0:t1, :], got[i * PATCHES:(i + 1) * PATCHES, t0:t1, :])\
                            .then_inc(s_out, 16)
                sp.dma_start(out[:, 0:CLS, :], got[:, PTILES, :]).then_inc(s_out, 16)
                sp.wait_ge(s_out, 16 * (2 * len(cuts) - 1))


def spline_blocks(nc, resid, ident, a, scratch, tables, gb_cols, tile_of, expand, dve_marks):
    x_rows, y_rows, _ = scratch
    with ExitStack() as ctx:
        def sb(name, shape, dt=F32):
            return ctx.enter_context(nc.sbuf_tensor(name, shape, dt))

        def ring(name, shape, dt=F32):
            return [sb(f"bl_{name}{z}", shape, dt) for z in range(RING)]

        def sem(name):
            return ctx.enter_context(nc.semaphore(name))

        def psum(name, shape):
            return ctx.enter_context(nc.psum_tensor(name, shape, F32))

        CHUNKS = 8
        QB = QS // CHUNKS
        N = PAIR * P
        ps_r = psum("bl_ps_spread", [P, 2, 512])
        ps_l = psum("bl_ps_looked_up", [P, PAIR, 2, 512])
        ps_x = psum("bl_ps_x", [P, 2, N])
        ps_t = psum("bl_ps_t", [P, 2, PAIR, P])
        grid = sb("bl_grid", [P, 1])
        grid_i = sb("bl_grid_i", [P, 1], I32)
        x = ring("x", [P, PAIR, D])
        w = [ring(f"w{b}_", [P, 2 * P + 2]) for b in range(QUAD)]
        table = [ring(f"table{b}_", [P, QS, PARTS, 2 * HG], BF16) for b in range(QUAD)]
        xT, sig, pos = (ring(n, [P, N]) for n in ("xT", "sig", "pos"))
        posT, hs, hsT, y = (ring(n, [P, PAIR, P]) for n in ("posT", "hs", "hsT", "y"))
        at = ring("at", [P, N], BF16)
        r, above = (sb(f"bl_{n}", [P, N]) for n in ("r", "above"))
        tmp = sb("bl_tmp", [P, PAIR, P])
        hot = sb("bl_hot", [P, QS, N], BF16)
        looked = sb("bl_looked", [P, PAIR, QS, 2, HG])

        s_const = sem("bl_constants")
        s_ldx = [sem(f"bl_x_loaded{z}") for z in range(RING)]
        s_ldw = [sem(f"bl_w_loaded{z}") for z in range(RING)]
        s_xfree = sem("bl_x_used")
        s_tab = sem("bl_table_ready")
        s_xT_ps = sem("bl_xT_in_psum")
        s_xT = sem("bl_xT_ready")
        s_h = sem("bl_h_in_psum")
        s_sig = sem("bl_sigmoid_ready")
        s_at = sem("bl_cell_ready")
        s_pos = sem("bl_position_ready")
        s_r = sem("bl_spread_in_psum")
        s_hot = sem("bl_hot_ready")
        s_posT_ps = sem("bl_posT_in_psum")
        s_posT = sem("bl_posT_ready")
        s_look = sem("bl_looked_up")
        s_taken = sem("bl_looked_up_taken")
        s_hs = sem("bl_hs_ready")
        s_hsT_ps = sem("bl_hsT_in_psum")
        s_hsT = sem("bl_hsT_ready")
        s_y = sem("bl_y_in_psum")
        s_yb = sem("bl_y_block_ready")
        s_yev = sem("bl_y_ready")
        s_st = [sem(f"bl_stored{z}") for z in range(RING)]
        TURNS = QUADS // RING
        MAGIC = 8388608.0
        LOAD = 16 * QUAD
        block = ctx.enter_context(nc.Block())

        def rows(b):
            return slice(b % 2 * BLOCK, (b % 2 + 1) * BLOCK)

        def in_turns(eng, step):
            step(0, lambda k: k % RING, lambda k: k // RING)
            with eng.Fori(0, TURNS - 1) as i:
                for j in range(1, RING + 1):
                    step(i * RING + j, lambda k, j=j: (j + k) % RING, lambda k, j=j: i + (j + k) // RING)
            for p in range(QUADS - RING + 1, QUADS):
                step(p, lambda k, p=p: (p + k) % RING, lambda k, p=p: (p + k) // RING)

        def is_last(p):
            return isinstance(p, int) and p == QUADS - 1

        def is_first(p):
            return isinstance(p, int) and p == 0

        @block.sync
        def _(sp):
            with sp.Fori(0, TURNS) as i:
                for z in range(RING):
                    p = i * RING + z
                    ts = [sp.value_load(tile_of[0:1, ds(p * QUAD + b, 1)], min_val=0, max_val=SPLINES - 1)
                          for b in range(QUAD)]
                    sp.wait_ge(s_xfree, p + 1)
                    sp.dma_start(x[z][:], x_rows[ds(p * N, N), :].rearrange("(a p) d -> p a d", p=P))\
                        .then_inc(s_ldx[z], 16)
                    sp.wait_ge(s_yev, p + 1)
                    for b in range(QUAD):
                        sp.dma_start(w[b][z][:], a["spline_w"][ts[b]]).then_inc(s_ldw[z], 16)

        @block.gpsimd
        def _(pool):
            pool.iota(grid_i[:], pattern=[[0, 1]], base=0, channel_multiplier=1).then_inc(s_const, 1)
            with pool.Fori(0, TURNS) as i:
                for z in range(RING):
                    p = i * RING + z
                    for b in range(QUAD):
                        t = pool.value_load(tile_of[0:1, ds(p * QUAD + b, 1)], min_val=0, max_val=SPLINES - 1)
                        if b == 0:
                            pool.wait_ge(s_look, p * 2 + 2)
                        pool.tensor_copy(table[b][z][:].rearrange("p q n c -> p (q n c)").bitcast(U32),
                                         tables[:, t].rearrange("p q n c u -> p (q n c u)").bitcast(U32))\
                            .then_inc(s_tab, 1)

        @block.vector
        def _(dve):
            ch = Chain(dve, dve_marks)
            dve.wait_ge(s_const, 1)
            ch.step(dve.tensor_scalar(grid_i[:], grid_i[:], GRID - 1, None, ALU.bitwise_and))
            ch.step(dve.tensor_copy(grid[:], grid_i[:]))

            def positions(p, z, part):
                if part == 0:
                    dve.wait_ge(s_sig, p + 1)
                    ch.mark(dve.tensor_scalar(r[:], sig[z][:], float(GRID), MAGIC, ALU.mult, ALU.add))
                elif part == 1:
                    ch.sync()
                    ch.mark(dve.tensor_scalar(r[:], r[:], MAGIC, float(GRID - 1), ALU.subtract, ALU.min))
                elif part == 2:
                    ch.sync()
                    ch.mark(dve.scalar_tensor_tensor(out=above[:], in0=sig[z][:], scalar=float(GRID), in1=r[:],
                                                     op0=ALU.mult, op1=ALU.is_lt))
                    ch.sync()
                    dve.tensor_tensor(at[z][:], r[:], above[:], ALU.subtract).then_inc(s_at, 1)
                else:
                    dve.wait_ge(s_at, p + 1)
                    dve.scalar_tensor_tensor(out=pos[z][:], in0=sig[z][:], scalar=float(GRID), in1=at[z][:],
                                             op0=ALU.mult, op1=ALU.subtract).then_inc(s_pos, 1)

            found = looked[:].rearrange("p a q c u -> p (a q) c u")

            def units(x):
                return x[:].rearrange("p a (q u) -> p (a q) u", u=HG)

            def sum_parts(p, half):
                dve.wait_ge(s_look, p * 2 + 2 * RING + half + 1)
                for pair in range(PAIR):
                    dve.tensor_reduce(
                        looked[:, pair, half * QS // 2:(half + 1) * QS // 2].rearrange("p q c u -> p q (c u)"),
                        ps_l[:, pair, half, 0:QS // 2 * PARTS * 2 * HG]
                        .rearrange("p (q n k) -> p q k n", q=QS // 2, n=PARTS), AX_X, ALU.add).then_inc(s_taken, 1)

            def sloped(p, z):
                dve.wait_ge(s_taken, (p + 2) * 2 * PAIR)
                dve.wait_ge(s_posT, p + 1)
                ch.mark(dve.tensor_tensor(units(tmp), found[:, :, 1, :], units(posT[z]), ALU.mult))

            def summed(p, z):
                ch.sync()
                dve.tensor_tensor(units(hs[z]), found[:, :, 0, :], units(tmp), ALU.add).then_inc(s_hs, 1)

            def step(p, z, turn):
                def one_hot(c):
                    dve.wait_ge(s_r, p * CHUNKS + c + 1)
                    dve.tensor_scalar(hot[:, c * QB:(c + 1) * QB, :], ps_r[:, c % 2, :].rearrange("p (q n) -> p q n", q=QB),
                                      grid[:], None, ALU.is_equal).then_inc(s_hot, 1)

                def ahead(part):
                    if not is_last(p):
                        positions(p + 1, z(1), part)

                one_hot(0)
                if not is_first(p):
                    sum_parts(p - 1, 1)
                one_hot(1)
                if not is_first(p):
                    sloped(p - 1, z(-1))
                one_hot(2)
                if not is_first(p):
                    summed(p - 1, z(-1))
                for c in range(3, CHUNKS):
                    one_hot(c)
                for part in range(3):
                    ahead(part)
                if not is_first(p):
                    dve.wait_ge(s_hs, p)
                sum_parts(p, 0)
                ahead(3)

            for part in range(4):
                positions(0, 0, part)
            step(0, lambda k: k % RING, None)
            with dve.Fori(0, TURNS - 1) as i:
                ch.enter(i, RING * 4)
                for j in range(1, RING + 1):
                    step(i * RING + j, lambda k, j=j: (j + k) % RING, None)
                ch.leave(TURNS - 1)
            for p in range(QUADS - RING + 1, QUADS):
                step(p, lambda k, p=p: (p + k) % RING, None)
            sum_parts(QUADS - 1, 1)
            sloped(QUADS - 1, (QUADS - 1) % RING)
            summed(QUADS - 1, (QUADS - 1) % RING)

        @block.scalar
        def _(act):
            for z in range(RING):
                act.sem_inc(s_st[z], 16)

            def normed(p, z):
                act.wait_ge(s_xT_ps, p + 1)
                act.sem_inc(s_xfree, 1)
                nc.scalar.activation(xT[z][:], ps_x[:, 0, :], ACT.Identity, bias=gb_cols[:, 1:2],
                                     scale=gb_cols[:, 0:1]).then_inc(s_xT, 1)

            def hidden(p, z):
                act.wait_ge(s_h, p + 1)
                nc.scalar.activation(sig[z][:], ps_x[:, 1, :], ACT.Sigmoid).then_inc(s_sig, 1)

            def turned(p, z):
                act.wait_ge(s_hsT_ps, p + 1)
                nc.scalar.copy(hsT[z][:], ps_t[:, 0]).then_inc(s_hsT, 1)

            def finish(p, z, turn):
                act.wait_ge(s_y, p + 1)
                act.wait_ge(s_st[z], turn * 16 + 16)
                for b in range(QUAD):
                    nc.scalar.activation(y[z][rows(b), b // 2, :], ps_t[rows(b), 1, b // 2, :], ACT.Identity,
                                         scale=w[b][z][rows(b), 2 * P:2 * P + 1]).then_inc(s_yb, 1)
                act.wait_ge(s_yb, (p + 1) * QUAD)
                act.sem_inc(s_yev, 1)
                act.dma_start(y_rows[ds(p * N, N), :].rearrange("(a p) d -> p a d", p=P), y[z][:]).then_inc(s_st[z], 16)

            def step(p, z, turn):
                if not is_last(p):
                    normed(p + 1, z(1))
                if not is_first(p):
                    turned(p - 1, z(-1))
                if not is_last(p):
                    hidden(p + 1, z(1))
                if not is_first(p):
                    finish(p - 1, z(-1), turn(-1))
                act.wait_ge(s_posT_ps, p + 1)
                nc.scalar.copy(posT[z(0)][:], ps_t[:, 0]).then_inc(s_posT, 1)

            normed(0, 0)
            hidden(0, 0)
            in_turns(act, step)
            turned(QUADS - 1, (QUADS - 1) % RING)
            finish(QUADS - 1, (QUADS - 1) % RING, (QUADS - 1) // RING)
            for z in range(RING):
                act.wait_ge(s_st[z], 16 * (TURNS + 1))

        @block.tensor
        def _(pe):
            def turn(out, src, done):
                for pair in range(PAIR):
                    mm = nc.tensor.transpose(out[:, pair * P:(pair + 1) * P], src(pair), ident[:])
                mm.then_inc(done, 1)

            def transpose_x(p, z, turns):
                pe.wait_ge(s_ldx[z], turns * 16 + 16)
                turn(ps_x[:, 0, :], lambda pair: x[z][:, pair, :], s_xT_ps)

            def hidden(p, z, turns, blocks=range(QUAD)):
                pe.wait_ge(s_xT, p + 1)
                pe.wait_ge(s_ldw[z], turns * LOAD + LOAD)
                for b in blocks:
                    now = slice(b * BLOCK, (b + 1) * BLOCK)
                    mm = nc.tensor.matmul(ps_x[:, 1, now], w[b][z][:, 0:P], xT[z][:, now], start=True, stop=True)
                if QUAD - 1 in blocks:
                    mm.then_inc(s_h, 1)

            def turn_hs(p, z):
                pe.wait_ge(s_hs, p + 1)
                turn(ps_t[:, 0].rearrange("p a n -> p (a n)"), lambda pair: hs[z][:, pair, :], s_hsT_ps)

            def finish(p, z, blocks=range(QUAD)):
                pe.wait_ge(s_hsT, p + 1)
                for b in blocks:
                    mm = nc.tensor.matmul(ps_t[rows(b), 1, b // 2, :], hsT[z][:, b // 2, rows(b)],
                                          w[b][z][:, P:2 * P], start=True, stop=True)
                if QUAD - 1 in blocks:
                    mm.then_inc(s_y, 1)

            def step(p, z, turns):
                def spread(c):
                    pe.wait_ge(s_hot, p * CHUNKS + c + 1)
                    for q in range(QB):
                        mm = nc.tensor.matmul(ps_r[:, c % 2, q * N:(q + 1) * N], expand[:, c * QB + q, :],
                                              at[z(0)][:], start=True, stop=True)
                    mm.then_inc(s_r, 1)

                def look_up(c):
                    pe.wait_ge(s_hot, p * CHUNKS + c + 3)
                    for q in range(c * QB, (c + 1) * QB):
                        half, at_q = q // (QS // 2), q % (QS // 2) * PARTS * 2 * HG
                        for b in range(QUAD):
                            mm = nc.tensor.matmul(ps_l[rows(b), b // 2, half, at_q:at_q + PARTS * 2 * HG],
                                                  hot[:, q, b * BLOCK:(b + 1) * BLOCK],
                                                  table[b][z(0)][:, q].rearrange("p n c -> p (n c)"),
                                                  start=True, stop=True)
                    if c % (CHUNKS // 2) == CHUNKS // 2 - 1:
                        mm.then_inc(s_look, 1)

                early, late = range(0, PAIR), range(PAIR, QUAD)
                pe.wait_ge(s_at, p + 1)
                spread(0)
                spread(1)
                if not is_last(p):
                    pe.wait_ge(s_sig, p + 1)
                    transpose_x(p + 1, z(1), turns(1))
                spread(2)
                spread(3)
                if not is_last(p):
                    hidden(p + 1, z(1), turns(1), early)
                spread(4)
                if not is_first(p):
                    turn_hs(p - 1, z(-1))
                spread(5)
                if not is_last(p):
                    hidden(p + 1, z(1), turns(1), late)
                spread(6)
                pe.wait_ge(s_tab, (p + 1) * QUAD)
                pe.wait_ge(s_taken, p * 2 * PAIR + PAIR)
                look_up(0)
                spread(7)
                if not is_first(p):
                    finish(p - 1, z(-1))
                for c in range(1, CHUNKS // 2):
                    look_up(c)
                pe.wait_ge(s_taken, (p + 1) * 2 * PAIR)
                look_up(4)
                look_up(5)
                if not is_first(p):
                    pe.wait_ge(s_yev, p + RING)
                pe.wait_ge(s_pos, p + 1)
                turn(ps_t[:, 0].rearrange("p a n -> p (a n)"),
                     lambda pair: pos[z(0)][:, pair * P:(pair + 1) * P], s_posT_ps)
                look_up(6)
                look_up(7)

            pe.sem_inc(s_yev, RING)
            pe.sem_inc(s_look, 2 * RING)
            pe.sem_inc(s_hot, 2)
            pe.sem_inc(s_taken, 2 * PAIR)
            pe.sem_inc(s_xfree, RING)
            transpose_x(0, 0, 0)
            hidden(0, 0, 0)
            in_turns(pe, step)
            turn_hs(QUADS - 1, (QUADS - 1) % RING)
            finish(QUADS - 1, (QUADS - 1) % RING)


def build(nc, a, out):
    with ExitStack() as ctx:
        resid = ctx.enter_context(nc.sbuf_tensor("resid", [P, TILES, D], F32))
        ident = ctx.enter_context(nc.sbuf_tensor("ident", [P, P], F32))
        tables = ctx.enter_context(nc.sbuf_tensor("tables", [P, SPLINES, QS, PARTS, 2, HG], BF16))
        stats = ctx.enter_context(nc.sbuf_tensor("token_stats", [P, TILES, 6], F32))
        wd_sum = ctx.enter_context(nc.sbuf_tensor("wd_sum", [P, SPLINES], F32))
        x_rows = nc.dram_tensor("x_rows", (ROWS, D), F32).ap()
        y_rows = nc.dram_tensor("y_rows", (ROWS, D), F32).ap()
        s_zeroed = ctx.enter_context(nc.semaphore("x_rows_zeroed"))
        s_turns = ctx.enter_context(nc.semaphore("turns"))
        dve_marks = Marks(ctx.enter_context(nc.semaphore("dve_chain")))
        scratch = (x_rows, y_rows, s_zeroed)
        with ExitStack() as setup:
            block = setup.enter_context(nc.Block())

            @block.gpsimd
            def _(pool):
                pool.memset(ident[:], 0.0).then_inc(s_turns, 1)
                pool.wait_ge(s_turns, 1)
                pool.affine_select(out=ident[:], in_=ident[:], compare_op=ALU.not_equal, fill=1.0,
                                   base=0, pattern=[[-1, P]], channel_multiplier=1)

        patch_attention(nc, resid, ident, a, s_turns, dve_marks, stats)
        experts(nc, resid, ident, a, tables, s_turns, dve_marks, stats, scratch)
        attention(nc, resid, ident, a, s_turns, dve_marks, stats, wd_sum)
        splines(nc, resid, ident, a, scratch, out, tables, s_turns, dve_marks, stats, wd_sum)


def kernel(**inputs):
    import numpy as np
    import concourse.bacc as bacc
    from concourse.bass_utils import run_bass_kernel_spmd as run

    v = {k: np.asarray(x) for k, x in inputs.items()}

    def flat(x, *shape):
        return np.ascontiguousarray(x.reshape(shape) if shape else x)

    x = v["x"].reshape(GROUPS, GT, 2, 3, 8, 28, 8, 28).transpose(0, 1, 3, 5, 7, 2, 4, 6)
    x = x.reshape(GROUPS, GT, PC, PK, P).transpose(0, 1, 3, 2, 4)
    arrays = {
        "x": flat(x),
        "w_patch": flat(v["L0_tok_W"].T.reshape(PC, PK, D).transpose(1, 0, 2)),
        "wq": flat(v["L0_attn_Wq"]), "wk": flat(v["L0_attn_Wk"]),
        "wv": flat(v["L0_attn_Wv"]), "wo": flat(v["L0_attn_Wo"]),
        "bias_cols": flat(np.stack([v["L0_attn_bq"], v["L0_attn_bk"], v["L0_attn_bv"]], 1)),
        "b_patch": flat(v["L0_tok_b"]),
        "bo": flat(v["L0_attn_bo"]),
        "cls_rows": flat(np.tile(np.stack([v["cls_tok"][0, 0], v["L0_tok_class_token"][0]]), (IMAGES, 1))),
        "cls_mul": flat(np.tile(np.stack([np.ones(D, np.float32), v["L0_tok_pos_embed"][0]]), (IMAGES, 1))),
        "pos": flat(v["L0_tok_pos_embed"][1:]),
        "gamma_beta": flat(np.stack([v["L1_ffn_gamma"], v["L1_ffn_beta"]], 1)),
        "wd_sums": flat(v["L1_ffn_Wd"].transpose(2, 0, 1)),
        "spline_w": flat(np.concatenate([v["L1_ffn_Wd"].transpose(0, 2, 1), v["L1_ffn_Wu"].transpose(0, 2, 1),
                                         np.tile(v["L1_ffn_scale"][:, None, None], (1, P, 2))], 2)),
        "spline_tables": flat(np.stack([v["L1_ffn_spline_bases"], v["L1_ffn_spline_slopes"]])
                              .reshape(2, SPLINES, QS, HG, GRID).transpose(3, 4, 1, 2, 0), P, SPLINES * 2 * QS),
        "w_qkv": flat(v["L1_attn_w_qkv"].reshape(D, 3, D)),
        "router": flat(v["L0_ffn_router_w"].T),
        "router_b": flat(v["L0_ffn_router_b"]),
        "fc1": flat(v["L0_ffn_fc1_w"].transpose(2, 0, 1)),
        "fc2": flat(v["L0_ffn_fc2_w"].reshape(EXPERTS, D, HC, P).transpose(3, 0, 2, 1)),
        "b1": flat(v["L0_ffn_fc1_b"].reshape(EXPERTS, 2 * HC, P).transpose(2, 0, 1)),
        "b2": flat(v["L0_ffn_fc2_b"]),
    }
    nc = bacc.Bacc("TRN2", target_bir_lowering=False, num_devices=1)
    aps = {n: nc.dram_tensor("in_" + n, x.shape, mybir.dt.from_np(x.dtype), kind="ExternalInput").ap()
           for n, x in arrays.items()}
    out = nc.dram_tensor("out", (IMAGES, SEQ, D), F32, kind="ExternalOutput").ap()
    build(nc, aps, out)
    r = run(nc, [{"in_" + n: x for n, x in arrays.items()}], core_ids=[0])
    return r.results[0]["out"]
```
